# Optimizing a Trainium2 kernel written in Bass

```python
import numpy as np
import jax
import jax.numpy as jnp

def _softmax(x, axis=-1):
    return jax.nn.softmax(x, axis=axis)

def _gelu(x):
    return jax.nn.gelu(x, approximate=True)

def _silu(x):
    return jax.nn.silu(x)

def _sigmoid(x):
    return jax.nn.sigmoid(x)

def _layernorm(x, axis=-1, eps=1e-05):
    m = jnp.mean(x, axis=axis, keepdims=True)
    v = jnp.var(x, axis=axis, keepdims=True)
    return (x - m) / jnp.sqrt(v + eps)

def _scatter_add(tgt, idx, src, axis=0):
    return tgt.at[idx].add(src)

def _segment_sum(src, seg, n):
    return jax.ops.segment_sum(src, seg, n)
kernel_name = 'mk_seq_preln_d2_jaxref_r8_7903f6'

def setup_inputs(seed: int=0):
    np.random.seed(seed)
    _w = jnp.asarray

    def _L0_attn_setup():
        import jax, jax.numpy as jnp
        import numpy as np
        import math
        B, S, E = (2, 256, 128)
        H, DC, DR = (16, 32, 128)
        HD = E // H

        def _linear_params(key, din, dout):
            k1, k2 = jax.random.split(key)
            bound = 1.0 / math.sqrt(din)
            w = jax.random.uniform(k1, (din, dout), minval=-bound, maxval=bound, dtype=jnp.float32)
            b = jax.random.uniform(k2, (dout,), minval=-bound, maxval=bound, dtype=jnp.float32)
            return (w, b)

        def _gelu(x):
            return jax.nn.gelu(x, approximate=False)

        def _rope_cos_sin(seq_len, d_rope):
            inv_freq = 1.0 / 10000.0 ** (jnp.arange(0, d_rope, 2, dtype=jnp.float32) / d_rope)
            t = jnp.arange(seq_len, dtype=jnp.float32)
            freqs = t[:, None] * inv_freq[None, :]
            emb = jnp.concatenate([freqs, freqs], axis=-1)
            return (jnp.cos(emb), jnp.sin(emb))

        def _apply_rope(x, cos, sin):
            d = x.shape[-1]
            x1, x2 = (x[..., :d // 2], x[..., d // 2:])
            rot = jnp.concatenate([-x2, x1], axis=-1)
            return x * cos + rot * sin
        key = jax.random.key(seed)
        ks = jax.random.split(key, 10)
        x = jax.random.normal(ks[0], (B, S, E), dtype=jnp.float32)
        wq, bq = _linear_params(ks[1], E, DC)
        wqc, bqc = _linear_params(ks[2], DC, E - DR)
        wqr, bqr = _linear_params(ks[3], E, DR)
        wkv, bkv = _linear_params(ks[4], E, DC)
        wkr, bkr = _linear_params(ks[5], E, DR)
        wkc, bkc = _linear_params(ks[6], DC, E - DR)
        wv, bv = _linear_params(ks[7], DC, E)
        wo, bo = _linear_params(ks[8], E, E)
        return dict(x=x, wq=wq, bq=bq, wqc=wqc, bqc=bqc, wqr=wqr, bqr=bqr, wkv=wkv, bkv=bkv, wkr=wkr, bkr=bkr, wkc=wkc, bkc=bkc, wv=wv, bv=bv, wo=wo, bo=bo)
    _L0_attn_in = _L0_attn_setup()

    def _L0_ffn_setup():
        import jax, jax.numpy as jnp
        import numpy as np
        HIDDEN = 128
        N_ROUTED = 16
        N_SHARED = 2
        TOP_K = 2
        MID_R = HIDDEN // 4
        MID_S = HIDDEN // 2
        key = jax.random.key(seed)
        ks = jax.random.split(key, 8)
        s = 0.02
        return {'x': jax.random.normal(ks[0], (2, 128, HIDDEN), dtype=jnp.float32), 'router_w': jax.random.normal(ks[1], (HIDDEN, N_ROUTED), dtype=jnp.float32) * s, 'wg_r': jax.random.normal(ks[2], (N_ROUTED, HIDDEN, MID_R), dtype=jnp.float32) * s, 'wu_r': jax.random.normal(ks[3], (N_ROUTED, HIDDEN, MID_R), dtype=jnp.float32) * s, 'wd_r': jax.random.normal(ks[4], (N_ROUTED, MID_R, HIDDEN), dtype=jnp.float32) * s, 'wg_s': jax.random.normal(ks[5], (N_SHARED, HIDDEN, MID_S), dtype=jnp.float32) * s, 'wu_s': jax.random.normal(ks[6], (N_SHARED, HIDDEN, MID_S), dtype=jnp.float32) * s, 'wd_s': jax.random.normal(ks[7], (N_SHARED, MID_S, HIDDEN), dtype=jnp.float32) * s}
    _L0_ffn_in = _L0_ffn_setup()

    def _L1_attn_setup():
        import jax, jax.numpy as jnp
        import numpy as np
        B, S, H = (8, 256, 128)
        CHUNK = 64
        INTER = 256
        BASE_LR = 0.01
        MAX_GRAD_NORM = 1.0
        EPS = 1e-06

        def rmsnorm(x, w):
            return x * jax.lax.rsqrt(jnp.mean(x * x, axis=-1, keepdims=True) + EPS) * w

        def mem_fwd(params, x):
            w0, w1, ln = params
            h = jax.nn.silu(x @ w0.T)
            y = h @ w1.T
            return x + rmsnorm(y, ln)

        def forward(x, wq_w, wk_w, wv_w, q_norm_w, k_norm_w, alpha_w, theta_w, eta_w, mem_w0, mem_w1, mem_ln_w):
            Bx, Sx, Hx = x.shape
            NC = Sx // CHUNK
            xc = x.reshape(Bx, NC, CHUNK, Hx)
            xf = xc.reshape(Bx, NC, CHUNK * Hx)
            alpha = jax.nn.sigmoid(jnp.mean(xf @ alpha_w.T, axis=0))
            theta = jax.nn.sigmoid(xf @ theta_w.T) * BASE_LR
            eta = jax.nn.sigmoid(jnp.mean(xf @ eta_w.T, axis=0))
            beta = 1.0 - alpha
            k = rmsnorm(jax.nn.silu(xc @ wk_w.T), k_norm_w)
            v = jax.nn.silu(xc @ wv_w.T)
            mem0 = (mem_w0, mem_w1, mem_ln_w)
            surp0 = jax.tree_util.tree_map(jnp.zeros_like, mem0)

            def step(carry, inp):
                mem, surp = carry
                k_c, v_c, th_c, eta_c, beta_c = inp

                def loss_fn(p):
                    pred = mem_fwd(p, k_c)
                    return jnp.mean((v_c - pred) ** 2 * th_c[:, :, None])
                grads = jax.grad(loss_fn)(mem)
                total = jnp.sqrt(sum((jnp.sum(g * g) for g in grads)))
                clip = jax.lax.stop_gradient(jnp.minimum(MAX_GRAD_NORM / (total + 1e-06), 1.0))
                new_surp = tuple((eta_c * s_ - g * clip for s_, g in zip(surp, grads)))
                new_mem = tuple((beta_c * m + ns for m, ns in zip(mem, new_surp)))
                return ((new_mem, new_surp), None)
            xs = (jnp.swapaxes(k, 0, 1), jnp.swapaxes(v, 0, 1), jnp.swapaxes(theta, 0, 1), eta, beta)
            (mem_f, _), _ = jax.lax.scan(step, (mem0, surp0), xs)
            q = rmsnorm(jax.nn.silu(x @ wq_w.T), q_norm_w)
            return mem_fwd(mem_f, q)
        key = jax.random.key(seed)
        ks = jax.random.split(key, 9)
        s = 0.02
        return {'x': jax.random.normal(ks[0], (B, S, H), jnp.float32), 'wq_w': jax.random.normal(ks[1], (H, H), jnp.float32) * s, 'wk_w': jax.random.normal(ks[2], (H, H), jnp.float32) * s, 'wv_w': jax.random.normal(ks[3], (H, H), jnp.float32) * s, 'q_norm_w': jnp.ones((H,), jnp.float32), 'k_norm_w': jnp.ones((H,), jnp.float32), 'alpha_w': jax.random.normal(ks[4], (1, CHUNK * H), jnp.float32) * s, 'theta_w': jax.random.normal(ks[5], (1, CHUNK * H), jnp.float32) * s, 'eta_w': jax.random.normal(ks[6], (1, CHUNK * H), jnp.float32) * s, 'mem_w0': jax.random.normal(ks[7], (INTER, H), jnp.float32) * s, 'mem_w1': jax.random.normal(ks[8], (H, INTER), jnp.float32) * s, 'mem_ln_w': jnp.ones((H,), jnp.float32)}
    _L1_attn_in = _L1_attn_setup()

    def _L1_ffn_setup():
        import jax, jax.numpy as jnp
        import numpy as np
        from jax import lax
        DIM = 128
        INTER = 64
        N_EXPERTS = 16
        TOPK = 4
        ROUTE_SCALE = 2.5
        VOCAB = 4000

        def _silu_and_mul(gu):
            gate, up = jnp.split(gu, 2, axis=-1)
            return jax.nn.silu(gate) * up
        key = jax.random.key(seed)
        ks = jax.random.split(key, 8)
        x = jax.random.normal(ks[0], (2, 64, DIM), dtype=jnp.float32)
        input_ids = jax.random.randint(ks[1], (2, 64), 0, VOCAB)
        s = 0.02
        gate_w = jax.random.normal(ks[2], (N_EXPERTS, DIM), dtype=jnp.float32) * s
        gate_b = jax.random.normal(ks[3], (N_EXPERTS,), dtype=jnp.float32) * s
        w13 = jax.random.normal(ks[4], (N_EXPERTS, 2 * INTER, DIM), dtype=jnp.float32) * s
        w2 = jax.random.normal(ks[5], (N_EXPERTS, DIM, INTER), dtype=jnp.float32) * s
        w13_s = jax.random.normal(ks[6], (2 * INTER, DIM), dtype=jnp.float32) * s
        w2_s = jax.random.normal(ks[7], (DIM, INTER), dtype=jnp.float32) * s
        return {'x': x, 'input_ids': input_ids, 'gate_w': gate_w, 'gate_b': gate_b, 'w13': w13, 'w2': w2, 'w13_s': w13_s, 'w2_s': w2_s}
    _L1_ffn_in = _L1_ffn_setup()
    _d = {'L0_attn_x': _L0_attn_in['x'], 'L0_attn_wq': _L0_attn_in['wq'], 'L0_attn_bq': _L0_attn_in['bq'], 'L0_attn_wqc': _L0_attn_in['wqc'], 'L0_attn_bqc': _L0_attn_in['bqc'], 'L0_attn_wqr': _L0_attn_in['wqr'], 'L0_attn_bqr': _L0_attn_in['bqr'], 'L0_attn_wkv': _L0_attn_in['wkv'], 'L0_attn_bkv': _L0_attn_in['bkv'], 'L0_attn_wkr': _L0_attn_in['wkr'], 'L0_attn_bkr': _L0_attn_in['bkr'], 'L0_attn_wkc': _L0_attn_in['wkc'], 'L0_attn_bkc': _L0_attn_in['bkc'], 'L0_attn_wv': _L0_attn_in['wv'], 'L0_attn_bv': _L0_attn_in['bv'], 'L0_attn_wo': _L0_attn_in['wo'], 'L0_attn_bo': _L0_attn_in['bo'], 'L0_ffn_router_w': _L0_ffn_in['router_w'], 'L0_ffn_wg_r': _L0_ffn_in['wg_r'], 'L0_ffn_wu_r': _L0_ffn_in['wu_r'], 'L0_ffn_wd_r': _L0_ffn_in['wd_r'], 'L0_ffn_wg_s': _L0_ffn_in['wg_s'], 'L0_ffn_wu_s': _L0_ffn_in['wu_s'], 'L0_ffn_wd_s': _L0_ffn_in['wd_s'], 'L1_attn_wq_w': _L1_attn_in['wq_w'], 'L1_attn_wk_w': _L1_attn_in['wk_w'], 'L1_attn_wv_w': _L1_attn_in['wv_w'], 'L1_attn_q_norm_w': _L1_attn_in['q_norm_w'], 'L1_attn_k_norm_w': _L1_attn_in['k_norm_w'], 'L1_attn_alpha_w': _L1_attn_in['alpha_w'], 'L1_attn_theta_w': _L1_attn_in['theta_w'], 'L1_attn_eta_w': _L1_attn_in['eta_w'], 'L1_attn_mem_w0': _L1_attn_in['mem_w0'], 'L1_attn_mem_w1': _L1_attn_in['mem_w1'], 'L1_attn_mem_ln_w': _L1_attn_in['mem_ln_w'], 'L1_ffn_input_ids': _L1_ffn_in['input_ids'], 'L1_ffn_gate_w': _L1_ffn_in['gate_w'], 'L1_ffn_gate_b': _L1_ffn_in['gate_b'], 'L1_ffn_w13': _L1_ffn_in['w13'], 'L1_ffn_w2': _L1_ffn_in['w2'], 'L1_ffn_w13_s': _L1_ffn_in['w13_s'], 'L1_ffn_w2_s': _L1_ffn_in['w2_s']}
    _x0 = _d['L0_attn_x']
    _d['L0_attn_x'] = jax.random.normal(jax.random.fold_in(jax.random.key(seed), 1), (4, 1024, 128), dtype=_x0.dtype)
    del _x0
    return _d

def reference(L0_attn_x, L0_attn_wq, L0_attn_bq, L0_attn_wqc, L0_attn_bqc, L0_attn_wqr, L0_attn_bqr, L0_attn_wkv, L0_attn_bkv, L0_attn_wkr, L0_attn_bkr, L0_attn_wkc, L0_attn_bkc, L0_attn_wv, L0_attn_bv, L0_attn_wo, L0_attn_bo, L0_ffn_router_w, L0_ffn_wg_r, L0_ffn_wu_r, L0_ffn_wd_r, L0_ffn_wg_s, L0_ffn_wu_s, L0_ffn_wd_s, L1_attn_wq_w, L1_attn_wk_w, L1_attn_wv_w, L1_attn_q_norm_w, L1_attn_k_norm_w, L1_attn_alpha_w, L1_attn_theta_w, L1_attn_eta_w, L1_attn_mem_w0, L1_attn_mem_w1, L1_attn_mem_ln_w, L1_ffn_input_ids, L1_ffn_gate_w, L1_ffn_gate_b, L1_ffn_w13, L1_ffn_w2, L1_ffn_w13_s, L1_ffn_w2_s):

    def _L0_attn_ref(x, wq, bq, wqc, bqc, wqr, bqr, wkv, bkv, wkr, bkr, wkc, bkc, wv, bv, wo, bo):
        import jax, jax.numpy as jnp
        import numpy as np
        import math
        B, S, E = (2, 256, 128)
        H, DC, DR = (16, 32, 128)
        HD = E // H

        def _linear_params(key, din, dout):
            k1, k2 = jax.random.split(key)
            bound = 1.0 / math.sqrt(din)
            w = jax.random.uniform(k1, (din, dout), minval=-bound, maxval=bound, dtype=jnp.float32)
            b = jax.random.uniform(k2, (dout,), minval=-bound, maxval=bound, dtype=jnp.float32)
            return (w, b)

        def _gelu(x):
            return jax.nn.gelu(x, approximate=False)

        def _rope_cos_sin(seq_len, d_rope):
            inv_freq = 1.0 / 10000.0 ** (jnp.arange(0, d_rope, 2, dtype=jnp.float32) / d_rope)
            t = jnp.arange(seq_len, dtype=jnp.float32)
            freqs = t[:, None] * inv_freq[None, :]
            emb = jnp.concatenate([freqs, freqs], axis=-1)
            return (jnp.cos(emb), jnp.sin(emb))

        def _apply_rope(x, cos, sin):
            d = x.shape[-1]
            x1, x2 = (x[..., :d // 2], x[..., d // 2:])
            rot = jnp.concatenate([-x2, x1], axis=-1)
            return x * cos + rot * sin
        b, s, _ = x.shape
        cq = _gelu(x @ wq + bq)
        q_c = cq @ wqc + bqc
        q_r = x @ wqr + bqr
        ckv = _gelu(x @ wkv + bkv)
        k_r = x @ wkr + bkr
        k_c = ckv @ wkc + bkc
        v = (ckv @ wv + bv).reshape(b, s, H, HD).transpose(0, 2, 1, 3)
        cos, sin = _rope_cos_sin(s, DR)
        q_r = _apply_rope(q_r, cos, sin)
        k_r = _apply_rope(k_r, cos, sin)
        q = _gelu(jnp.concatenate([q_c, q_r], axis=-1)).reshape(b, s, H, HD).transpose(0, 2, 1, 3)
        k = _gelu(jnp.concatenate([k_c, k_r], axis=-1)).reshape(b, s, H, HD).transpose(0, 2, 1, 3)
        scale = 1.0 / math.sqrt(HD)
        scores = jnp.einsum('bhqd,bhkd->bhqk', q, k) * scale
        causal = jnp.triu(jnp.ones((s, s), dtype=bool), k=1)
        scores = jnp.where(causal[None, None], -jnp.inf, scores)
        attn = jax.nn.softmax(scores, axis=-1)
        out = jnp.einsum('bhqk,bhkd->bhqd', attn, v)
        out = out.transpose(0, 2, 1, 3).reshape(b, s, E)
        return out @ wo + bo

    def _L0_ffn_ref(x, router_w, wg_r, wu_r, wd_r, wg_s, wu_s, wd_s):
        import jax, jax.numpy as jnp
        import numpy as np
        HIDDEN = 128
        N_ROUTED = 16
        N_SHARED = 2
        TOP_K = 2
        MID_R = HIDDEN // 4
        MID_S = HIDDEN // 2
        orig_shape = x.shape
        flat = x.reshape(-1, orig_shape[-1])
        gs = jnp.einsum('td,ndm->tnm', flat, wg_s)
        us = jnp.einsum('td,ndm->tnm', flat, wu_s)
        out = jnp.einsum('tnm,nmd->td', jax.nn.silu(gs) * us, wd_s)
        logits = (flat @ router_w).astype(jnp.float32)
        probs = jax.nn.softmax(logits, axis=-1)
        weights, indices = jax.lax.top_k(probs, TOP_K)
        weights = weights / (weights.sum(axis=-1, keepdims=True) + 1e-09)
        weights = weights.astype(x.dtype)
        comb = jnp.sum(jax.nn.one_hot(indices, N_ROUTED, dtype=x.dtype) * weights[..., None], axis=1)
        g = jnp.einsum('td,edm->tem', flat, wg_r)
        u = jnp.einsum('td,edm->tem', flat, wu_r)
        h = jax.nn.silu(g) * u
        h = h * comb[:, :, None]
        out = out + jnp.einsum('tem,emd->td', h, wd_r)
        return out.reshape(orig_shape)

    def _L1_attn_ref(x, wq_w, wk_w, wv_w, q_norm_w, k_norm_w, alpha_w, theta_w, eta_w, mem_w0, mem_w1, mem_ln_w):
        import jax, jax.numpy as jnp
        import numpy as np
        B, S, H = (8, 256, 128)
        CHUNK = 64
        INTER = 256
        BASE_LR = 0.01
        MAX_GRAD_NORM = 1.0
        EPS = 1e-06

        def rmsnorm(x, w):
            return x * jax.lax.rsqrt(jnp.mean(x * x, axis=-1, keepdims=True) + EPS) * w

        def mem_fwd(params, x):
            w0, w1, ln = params
            h = jax.nn.silu(x @ w0.T)
            y = h @ w1.T
            return x + rmsnorm(y, ln)

        def forward(x, wq_w, wk_w, wv_w, q_norm_w, k_norm_w, alpha_w, theta_w, eta_w, mem_w0, mem_w1, mem_ln_w):
            Bx, Sx, Hx = x.shape
            NC = Sx // CHUNK
            xc = x.reshape(Bx, NC, CHUNK, Hx)
            xf = xc.reshape(Bx, NC, CHUNK * Hx)
            alpha = jax.nn.sigmoid(jnp.mean(xf @ alpha_w.T, axis=0))
            theta = jax.nn.sigmoid(xf @ theta_w.T) * BASE_LR
            eta = jax.nn.sigmoid(jnp.mean(xf @ eta_w.T, axis=0))
            beta = 1.0 - alpha
            k = rmsnorm(jax.nn.silu(xc @ wk_w.T), k_norm_w)
            v = jax.nn.silu(xc @ wv_w.T)
            mem0 = (mem_w0, mem_w1, mem_ln_w)
            surp0 = jax.tree_util.tree_map(jnp.zeros_like, mem0)

            def step(carry, inp):
                mem, surp = carry
                k_c, v_c, th_c, eta_c, beta_c = inp

                def loss_fn(p):
                    pred = mem_fwd(p, k_c)
                    return jnp.mean((v_c - pred) ** 2 * th_c[:, :, None])
                grads = jax.grad(loss_fn)(mem)
                total = jnp.sqrt(sum((jnp.sum(g * g) for g in grads)))
                clip = jax.lax.stop_gradient(jnp.minimum(MAX_GRAD_NORM / (total + 1e-06), 1.0))
                new_surp = tuple((eta_c * s_ - g * clip for s_, g in zip(surp, grads)))
                new_mem = tuple((beta_c * m + ns for m, ns in zip(mem, new_surp)))
                return ((new_mem, new_surp), None)
            xs = (jnp.swapaxes(k, 0, 1), jnp.swapaxes(v, 0, 1), jnp.swapaxes(theta, 0, 1), eta, beta)
            (mem_f, _), _ = jax.lax.scan(step, (mem0, surp0), xs)
            q = rmsnorm(jax.nn.silu(x @ wq_w.T), q_norm_w)
            return mem_fwd(mem_f, q)
        return forward(x, wq_w, wk_w, wv_w, q_norm_w, k_norm_w, alpha_w, theta_w, eta_w, mem_w0, mem_w1, mem_ln_w)

    def _L1_ffn_ref(x, input_ids, gate_w, gate_b, w13, w2, w13_s, w2_s):
        import jax, jax.numpy as jnp
        import numpy as np
        from jax import lax
        DIM = 128
        INTER = 64
        N_EXPERTS = 16
        TOPK = 4
        ROUTE_SCALE = 2.5
        VOCAB = 4000

        def _silu_and_mul(gu):
            gate, up = jnp.split(gu, 2, axis=-1)
            return jax.nn.silu(gate) * up
        B, S, D = x.shape
        xt = x.reshape(-1, D)
        T = xt.shape[0]
        scores = jax.nn.sigmoid(xt.astype(jnp.float32) @ gate_w.T)
        biased = scores + gate_b
        _, idx = lax.top_k(biased, TOPK)
        w = jnp.take_along_axis(scores, idx, axis=-1)
        w = w / jnp.sum(w, axis=-1, keepdims=True)
        w = w * ROUTE_SCALE
        comb = jnp.zeros((T, N_EXPERTS), jnp.float32)
        comb = comb.at[jnp.arange(T)[:, None], idx].add(w)
        comb = comb.astype(x.dtype)

        def expert_body(y, args):
            w13_e, w2_e, c_e = args
            h = _silu_and_mul(xt @ w13_e.T)
            return (y + c_e[:, None] * (h @ w2_e.T), None)
        y, _ = lax.scan(expert_body, jnp.zeros_like(xt), (w13, w2, comb.T))
        y = y + _silu_and_mul(xt @ w13_s.T) @ w2_s.T
        return y.astype(x.dtype).reshape(B, S, D)
    x = L0_attn_x
    x = x + _L0_attn_ref(_layernorm(x, axis=-1), L0_attn_wq, L0_attn_bq, L0_attn_wqc, L0_attn_bqc, L0_attn_wqr, L0_attn_bqr, L0_attn_wkv, L0_attn_bkv, L0_attn_wkr, L0_attn_bkr, L0_attn_wkc, L0_attn_bkc, L0_attn_wv, L0_attn_bv, L0_attn_wo, L0_attn_bo)
    x = x + _L0_ffn_ref(_layernorm(x, axis=-1), L0_ffn_router_w, L0_ffn_wg_r, L0_ffn_wu_r, L0_ffn_wd_r, L0_ffn_wg_s, L0_ffn_wu_s, L0_ffn_wd_s)
    x = x + _L1_attn_ref(_layernorm(x, axis=-1), L1_attn_wq_w, L1_attn_wk_w, L1_attn_wv_w, L1_attn_q_norm_w, L1_attn_k_norm_w, L1_attn_alpha_w, L1_attn_theta_w, L1_attn_eta_w, L1_attn_mem_w0, L1_attn_mem_w1, L1_attn_mem_ln_w)
    x = x + _L1_ffn_ref(_layernorm(x, axis=-1), L1_ffn_input_ids, L1_ffn_gate_w, L1_ffn_gate_b, L1_ffn_w13, L1_ffn_w2, L1_ffn_w13_s, L1_ffn_w2_s)
    return x

_drawn_inputs = setup_inputs


def setup_inputs(seed=0):
    import zlib

    import numpy as np

    out = dict(_drawn_inputs(seed))
    spreads = {'L1_attn_q_norm_w': (1.0, 0.2),
     'L1_attn_k_norm_w': (1.0, 0.2),
     'L1_attn_mem_ln_w': (1.0, 0.2)}
    factors = {'L0_attn_wqr': 8.0,
     'L0_attn_bqr': 8.0,
     'L0_attn_wkv': 6.056,
     'L0_attn_bkv': 5.961,
     'L0_attn_wkr': 8.0,
     'L0_attn_bkr': 8.0,
     'L0_ffn_router_w': 8.0,
     'L0_ffn_wg_r': 8.0,
     'L0_ffn_wu_r': 8.0,
     'L0_ffn_wd_r': 8.0,
     'L0_ffn_wg_s': 8.0,
     'L0_ffn_wu_s': 8.0,
     'L0_ffn_wd_s': 8.0,
     'L1_ffn_gate_w': 8.0,
     'L1_ffn_gate_b': 8.0,
     'L1_ffn_w13': 8.0,
     'L1_ffn_w2': 8.0,
     'L1_ffn_w13_s': 8.0,
     'L1_ffn_w2_s': 8.0,
     'L1_attn_alpha_w': 8.0}
    for name, (base, spread) in spreads.items():
        noise = np.random.default_rng([zlib.crc32(name.encode()), seed]).standard_normal(out[name].shape)
        drawn = base * np.exp(spread * noise) if base else spread * noise
        out[name] = jnp.asarray(drawn.astype(out[name].dtype))
    for name, factor in factors.items():
        out[name] = (out[name] * factor).astype(out[name].dtype)
    return out
```

```python
from contextlib import ExitStack

import concourse.bass as bass
from concourse import mybir

FP32 = mybir.dt.float32
BF16 = mybir.dt.bfloat16
ACT = mybir.ActivationFunctionType
ALU = mybir.AluOpType

P = 128
BATCH, SEQ = 4, 1024
HEADS, HEAD_DIM = 16, 8
HEAD_GROUP = 4
HEAD_GROUPS = HEADS // HEAD_GROUP
LATENT = 32
GROUP = 512
TILES = GROUP // P
GROUPS = BATCH * SEQ // GROUP
KEY_TILES = SEQ // P
HALVES = SEQ // GROUP
V_COLS = HEAD_GROUP * (HEAD_DIM + 1)
V_SLOT = V_COLS + 32
LN_EPS = 1e-5
NEG = -1.0e30


def wait(engine, semaphore, value):
    if isinstance(value, int) and value <= 0:
        return
    engine.wait_ge(semaphore, value)


def settle(engine, idle):
    engine.sem_inc(idle, 1)


class Chain:

    def __init__(self, engine, semaphore):
        self.engine, self.semaphore, self.base, self.n = engine, semaphore, 0, 0

    def at(self, base):
        self.base, self.n = base, 0

    def add(self, instruction):
        instruction.then_inc(self.semaphore, 1)
        self.n += 1
        return self.base + self.n

    def wait(self, value=None):
        self.engine.wait_ge(self.semaphore, self.base + self.n if value is None else value)


class Memory:

    def __init__(self, nc, stack, prefix=""):
        self.nc, self.stack, self.prefix = nc, stack, prefix
        self.semaphores = []

    def sb(self, name, shape, dtype=FP32):
        return self.stack.enter_context(self.nc.sbuf_tensor(self.prefix + name, shape, dtype))

    def ps(self, name, shape, dtype=FP32):
        return self.stack.enter_context(self.nc.psum_tensor(self.prefix + name, shape, dtype))

    def sem(self, name):
        if not self.semaphores:
            self.stack.callback(self.release)
        self.semaphores.append(self.nc.alloc_semaphore(self.prefix + name))
        return self.semaphores[-1]

    def release(self):
        self.nc.clear_and_free_semaphores(self.semaphores)
        self.nc.all_engine_barrier()


def project_stage(nc, keep, w, io):
    with ExitStack() as stack:
        m = Memory(nc, stack, "in_")
        x_in = m.sb("x_in", [P, 2, TILES, P])
        stats = m.sb("ln_stats", [P, 2, TILES, 6])
        moments = m.sb("ln_moments", [P, 2, TILES, 2])
        var_eps = m.sb("var_eps", [P, 2, TILES])
        rstd = m.sb("rstd", [P, 2, TILES])
        xn = m.sb("xn", [P, 2, TILES, P])
        xnT = m.sb("xnT", [P, 2, GROUP])
        straight = m.sb("rope_straight", [P, 2, 2, GROUP])
        crossed = m.sb("rope_crossed", [P, 2, 2, GROUP])
        roped = m.sb("roped", [P, 2, GROUP])
        qk = m.sb("qk_gelu", [P, 2, GROUP])
        rest = m.sb("qk_rest", [P, 2, GROUP])
        parts = m.sb("qk_parts_sb", [P, 2, 2, 3, GROUP], BF16)
        latent = m.sb("latent", [LATENT + 1, 2, GROUP])
        xT_ps = m.ps("xT_ps", [P, GROUP])
        proj_ps = [m.ps(f"proj_ps{n}", [P, GROUP]) for n in range(4)]
        lat_ps = m.ps("lat_ps", [P, GROUP])
        v_ps = m.ps("v_ps", [P, GROUP])

        x_loaded = [m.sem("x_loaded0"), m.sem("x_loaded1")]
        var_ready, rstd_ready, xn_ready = m.sem("var_ready"), m.sem("rstd_ready"), m.sem("xn_ready")
        turned, xT_ready, projected = m.sem("turned"), m.sem("xT_ready"), m.sem("projected")
        lat_done, lat_ready, v_done, v_kept = m.sem("lat_done"), m.sem("lat_ready"), m.sem("v_done"), m.sem("v_kept")
        rotated, summed, gelu_done = m.sem("rotated"), m.sem("summed"), m.sem("gelu_done")
        hi_done, rest_done, mid_done, lo_done = m.sem("hi_done"), m.sem("rest_done"), m.sem("mid_done"), m.sem("lo_done")
        dve_own, latent_ones, v_ones = m.sem("dve_own"), m.sem("latent_ones"), m.sem("v_ones")
        idle = m.sem("idle_in")
        stored = keep.parts_stored

        x_v = io["x"].rearrange("b (h t p) e -> (b h) p t e", h=HALVES, p=P)
        parts_v = io["parts"].rearrange("k b a r s -> k b r a s")
        V_v = keep.V[:].rearrange("p b h j (g c) -> p b h j g c", c=HEAD_DIM + 1)

        block = stack.enter_context(nc.Block())

        def batches(engine, body):
            body(0, False)
            with engine.Fori(1, BATCH - 1) as b:
                body(b, False)
            body(BATCH - 1, True)

        @block.sync
        def _(sp):
            def load(g, half):
                wait(sp, xn_ready, g - 1)
                sp.dma_start(x_in[:, half], x_v[g]).then_inc(x_loaded[half], 16)

            load(0, 0)
            load(1, 1)

            for dst, src in w["loads"]:
                sp.dma_start(dst, src).then_inc(keep.weights, 16)

            def body(b, last):
                for half in range(HALVES):
                    g = 2 * b + half
                    if not last:
                        load(g + 2, half)
                    sp.wait_ge(lo_done, g + 1)
                    sp.wait_ge(mid_done, g + 1)
                    sp.wait_ge(hi_done, g + 1)
                    for k in range(2):
                        sp.dma_start(parts_v[k, b][:, :, half * GROUP:(half + 1) * GROUP],
                                     parts[:, half, k]).then_inc(stored[half], 16)

            batches(sp, body)
            for half in range(HALVES):
                sp.wait_ge(stored[half], 32 * BATCH)

        @block.vector
        def _(dve):
            own = Chain(dve, dve_own)
            nc.vector.memset(keep.V[:], 1.0).then_inc(v_ones, 1)
            nc.vector.memset(latent[LATENT:LATENT + 1], 1.0).then_inc(latent_ones, 1)
            LINKS = 2

            def norm(g, b, half):
                own.at(LINKS * g)
                dve.wait_ge(x_loaded[half], 16 * (b + 1))
                wait(dve, turned, g - 1)
                for t in range(TILES):
                    last = nc.vector.bn_stats(stats[:, half, t], x_in[:, half, t])
                own.add(last)
                own.wait()
                settle(dve, idle)
                for t in range(TILES):
                    last = nc.vector.bn_aggr(moments[:, half, t], stats[:, half, t])
                own.add(last)
                own.wait()
                nc.vector.tensor_scalar_add(var_eps[:, half], moments[:, half, :, 1], LN_EPS).then_inc(var_ready, 1)
                dve.wait_ge(rstd_ready, g + 1)
                for t in range(TILES):
                    last = nc.vector.tensor_scalar(xn[:, half, t], x_in[:, half, t], moments[:, half, t, 0:1],
                                                   rstd[:, half, t:t + 1], ALU.subtract, ALU.mult)
                last.then_inc(xn_ready, 1)

            def rotate(g, half):
                dve.wait_ge(projected, g + 1)
                wait(dve, summed, g - 1)
                cols = slice(half * GROUP, (half + 1) * GROUP)
                for k in range(2):
                    nc.vector.scalar_tensor_tensor(straight[:, half, k], proj_ps[2 * k][:], w["qk_bias"][:, 2 * k:2 * k + 1],
                                                   w["cos"][:, cols], ALU.add, ALU.mult)
                    last = nc.vector.scalar_tensor_tensor(crossed[:, half, k], proj_ps[2 * k + 1][:],
                                                          w["qk_bias"][:, 2 * k + 1:2 * k + 2],
                                                          w["sin"][:, cols], ALU.add, ALU.mult)
                last.then_inc(rotated, 1)

            def low_part(g, b, half):
                dve.wait_ge(mid_done, g + 1)
                wait(dve, stored[half], 32 * b)
                nc.vector.tensor_tensor(parts[:, half, :, 2], rest[:], parts[:, half, :, 1],
                                        ALU.subtract).then_inc(lo_done, 1)

            norm(0, 0, 0)

            def body(b, last):
                for half in range(HALVES):
                    g = 2 * b + half
                    if half == 0:
                        norm(g + 1, b, 1)
                    elif not last:
                        norm(g + 1, b + 1, 0)
                    rotate(g, half)
                    low_part(g, b, half)

            dve.wait_ge(keep.weights, 16 * len(w["loads"]))
            batches(dve, body)

        @block.gpsimd
        def _(pool):
            nc.gpsimd.memset(keep.minus_half[:], -0.5).then_inc(keep.started, 1)
            pool.wait_ge(keep.started, 1)

            def root(g, half):
                pool.wait_ge(var_ready, g + 1)
                nc.gpsimd.tensor_tensor(rstd[:, half], var_eps[:, half], keep.minus_half[:, 0:TILES],
                                        ALU.pow).then_inc(rstd_ready, 1)

            root(0, 0)

            def body(b, last):
                for half in range(HALVES):
                    g = 2 * b + half
                    if not (last and half == 1):
                        root(g + 1, 1 - half)
                    pool.wait_ge(rotated, g + 1)
                    wait(pool, gelu_done, g)
                    nc.gpsimd.tensor_tensor(roped[:], straight[:, half], crossed[:, half],
                                            ALU.add).then_inc(summed, 1)
                    pool.wait_ge(hi_done, g + 1)
                    wait(pool, lo_done, g)
                    nc.gpsimd.tensor_tensor(rest[:], qk[:], parts[:, half, :, 0],
                                            ALU.subtract).then_inc(rest_done, 1)

            batches(pool, body)

        @block.scalar
        def _(act):
            act.wait_ge(v_ones, 1)
            act.wait_ge(latent_ones, 1)

            def body(b, last):
                for half in range(HALVES):
                    g = 2 * b + half
                    act.wait_ge(turned, g + 1)
                    wait(act, projected, g - 1)
                    nc.scalar.copy(xnT[:, half], xT_ps[:]).then_inc(xT_ready, 1)
                    act.wait_ge(lat_done, g + 1)
                    wait(act, v_done, g - 1)
                    nc.scalar.activation(latent[0:LATENT, half], lat_ps[0:LATENT, :], ACT.Gelu,
                                         bias=w["bkv"][:, 0:1]).then_inc(lat_ready, 1)
                    act.wait_ge(summed, g + 1)
                    wait(act, rest_done, g)
                    nc.scalar.activation(qk[:], roped[:], ACT.Gelu).then_inc(gelu_done, 1)
                    act.wait_ge(gelu_done, g + 1)
                    wait(act, stored[half], 32 * b)
                    nc.scalar.copy(parts[:, half, :, 0], qk[:]).then_inc(hi_done, 1)
                    act.wait_ge(v_done, g + 1)
                    src = v_ps[:].rearrange("p (t h g d) -> p t h g d", t=TILES, h=HEAD_GROUPS, g=HEAD_GROUP)
                    for h in range(HEAD_GROUPS):
                        last_copy = nc.scalar.copy(V_v[:, b, h, half * TILES:(half + 1) * TILES, :, 0:HEAD_DIM], src[:, :, h])
                    last_copy.then_inc(v_kept, 1)
                    act.wait_ge(rest_done, g + 1)
                    nc.scalar.copy(parts[:, half, :, 1], rest[:]).then_inc(mid_done, 1)

            batches(act, body)

        @block.tensor
        def _(pe):
            pe.wait_ge(keep.weights, 16 * len(w["loads"]))

            def body(b, last):
                for half in range(HALVES):
                    g = 2 * b + half
                    pe.wait_ge(xn_ready, g + 1)
                    wait(pe, xT_ready, g)
                    for t in range(TILES):
                        mm = nc.tensor.transpose(xT_ps[:, t * P:(t + 1) * P], xn[:, half, t], w["ident"][:])
                    mm.then_inc(turned, 1)
                    pe.wait_ge(xT_ready, g + 1)
                    wait(pe, lat_ready, g)
                    nc.tensor.matmul(lat_ps[0:LATENT, :], w["wkv"][:], xnT[:, half], start=True,
                                     stop=True).then_inc(lat_done, 1)
                    wait(pe, rotated, g)
                    for n in range(4):
                        mm = nc.tensor.matmul(proj_ps[n][:], w["wqk"][:, n], xnT[:, half], start=True, stop=True)
                    mm.then_inc(projected, 1)
                    pe.wait_ge(lat_ready, g + 1)
                    wait(pe, v_kept, g)
                    for t in range(TILES):
                        mm = nc.tensor.matmul(v_ps[:, t * P:(t + 1) * P], latent[:, half, t * P:(t + 1) * P],
                                              w["wv"][:], start=True, stop=True)
                    mm.then_inc(v_done, 1)

            batches(pe, body)


def attention_schedule():
    tasks = [("out", 1)]
    halves = [[("max", g, i) for i in range(KEY_TILES // 2) for g in range(HEAD_GROUP)],
              [("max", g, i) for i in range(KEY_TILES // 2, KEY_TILES) for g in range(HEAD_GROUP)]]
    tasks += halves[0] + halves[1][:2] + [("rows", 0)] + halves[1][2:8] + [("out", 0)] + halves[1][8:] + [("rows", 1)]
    cost = {"max": 0, "out": 600, "rows": 200}
    spent, places = 0, []
    total = sum(cost[t[0]] + (100 + (t[2] + 1) * P if t[0] == "max" else 0) for t in tasks)
    for t in tasks:
        places.append(min(46, int(spent / total * 46)))
        spent += cost[t[0]] + (100 + (t[2] + 1) * P if t[0] == "max" else 0)
    places[-1] = 47
    places[0] = 1
    at = tasks.index(("out", 0))
    places = [max(p, 24) if n >= at else p for n, p in enumerate(places)]
    return tasks, places


ENTRIES = 36
CHUNKS = 48
ROUNDS = CHUNKS // HEAD_GROUP
ROUND_LIST = [(half, j) for half in range(HALVES) for j in range((half + 1) * TILES)]
MAX_ROWS = 72
STACK = MAX_ROWS + 2
LOADS = 13


def attention_stage(nc, keep, w, io):
    tasks, places = attention_schedule()
    assert len(tasks) == ENTRIES
    with ExitStack() as stack:
        m = Memory(nc, stack, "attn_")
        q_stack = m.sb("q_stack", [P, HEAD_GROUPS, HALVES, HEAD_GROUP, GROUP], BF16)
        k_stack = m.sb("k_stack", [P, HEAD_GROUPS, HEAD_GROUP, SEQ], BF16)
        V_slot = m.sb("V_slot", [P, 2, KEY_TILES, V_SLOT])
        probs = m.sb("probs", [P, 2, HEAD_GROUP, GROUP])
        ones = m.sb("ones", [2 * HEAD_GROUPS * HEAD_GROUP * SEQ // GROUP, GROUP], BF16)
        outT = m.sb("outT", [P, 2, GROUP])
        junk = m.sb("junk", [P, 2, SEQ], BF16)
        maxima = m.sb("maxima", [P, 2, HALVES, HEAD_GROUP, TILES])
        max_rows = m.sb("max_rows", [HEAD_GROUP * TILES, HALVES, 2, P], BF16)
        recip = m.sb("recip", [P, 2, TILES, HEAD_GROUP])
        ring = [m.ps(f"ring{n}", [P, 2 * GROUP]) for n in range(2)]
        score_ps = [m.ps(f"score_ps{n}", [P, GROUP]) for n in range(2)]
        out_ps = [m.ps(f"out_ps{n}", [P, GROUP]) for n in range(2)]

        ones_set, ones_loaded = m.sem("ones_set"), m.sem("ones_loaded")
        stack_loaded = [m.sem(f"stack_loaded{n}") for n in range(HEAD_GROUPS)]
        ring_filled, ring_read = m.sem("ring_filled"), m.sem("ring_read")
        rows_loaded = [m.sem("rows_loaded0"), m.sem("rows_loaded1")]
        scored, exp_done, round_done = m.sem("scored"), m.sem("exp_done"), m.sem("round_done")
        out_copied = [m.sem("out_copied0"), m.sem("out_copied1")]
        V_ready, recip_ready, rows_hi = m.sem("V_ready"), m.sem("recip_ready"), m.sem("rows_hi")
        V_pad, idle = m.sem("V_pad"), m.sem("idle_attn")
        attn_v = keep.attn[:].rearrange("p b i (h g d) -> p b i h g d", h=HEAD_GROUPS, g=HEAD_GROUP)

        parts_v = io["parts"].rearrange("k b a (d h) s -> k b (a d) h s", h=HEADS)

        def entry(u, n):
            return ENTRIES * u + 33 + n

        first_maxima = [t for t in tasks if t[0] != "out"]

        def batches(engine, body):
            body(0)
            with engine.Fori(1, BATCH - 1) as b:
                body(b)
            body(BATCH - 1)

        block = stack.enter_context(nc.Block())

        @block.sync
        def _(sp):
            def load(b, h):
                wait(sp, scored, CHUNKS * (4 * b + h - 3))
                q_src, k_src = (parts_v[k, b][:, HEAD_GROUP * h:HEAD_GROUP * (h + 1), :] for k in range(2))
                for turn in range(3):
                    row = 24 * turn
                    sp.dma_start(k_stack[row:row + 24, h], k_src).then_inc(stack_loaded[h], 16)
                    cut = 8 * turn
                    for half in range(HALVES):
                        cols = slice(half * GROUP, (half + 1) * GROUP)
                        sp.dma_start(q_stack[row:row + 24 - cut, h, half], q_src[cut:24, :, cols]).then_inc(stack_loaded[h], 16)
                        if turn:
                            sp.dma_start(q_stack[row + 24 - cut:row + 24, h, half],
                                         q_src[0:cut, :, cols]).then_inc(stack_loaded[h], 16)

            load(0, 0)
            sp.wait_ge(ones_set, 1)
            sp.dma_start(k_stack[MAX_ROWS:STACK].rearrange("p h g s -> p (h g s)"), ones[:]).then_inc(ones_loaded, 16)
            load(0, 1)

            def put_rows(u, h, half):
                made = entry(u - 1, tasks.index(("rows", half))) + 1
                if isinstance(u, int) and u == 0:
                    made = first_maxima.index(("rows", half)) + 1
                sp.wait_ge(ring_read, made)
                for n in range(2):
                    sp.dma_start(q_stack[MAX_ROWS + n:MAX_ROWS + n + 1, h, half],
                                 max_rows[:, half, n]).then_inc(rows_loaded[half], 16)

            put_rows(0, 0, 0)
            put_rows(0, 0, 1)

            def body(b):
                for h in range(HEAD_GROUPS):
                    u = HEAD_GROUPS * b + h
                    final = isinstance(b, int) and b == BATCH - 1
                    if h < 2:
                        load(b, h + 2)
                    elif not final:
                        load(b + 1, h - 2)
                    if not (final and h == 3):
                        put_rows(u + 1, (h + 1) % 4, 0)
                        put_rows(u + 1, (h + 1) % 4, 1)

            batches(sp, body)

        @block.gpsimd
        def _(pool):
            nc.gpsimd.memset(ones[:], 1.0).then_inc(ones_set, 1)
            nc.gpsimd.memset(V_slot[:], 0.0).then_inc(V_pad, 1)
            pool.wait_ge(V_pad, 1)

            def body(b):
                for h in range(HEAD_GROUPS):
                    u = HEAD_GROUPS * b + h
                    wait(pool, round_done, ROUNDS * (u - 1))
                    nc.gpsimd.tensor_copy(V_slot[:, h % 2, :, 0:V_COLS], keep.V[:, b, h]).then_inc(V_ready, 1)

            batches(pool, body)

        @block.scalar
        def _(act):
            def body(b):
                for h in range(HEAD_GROUPS):
                    u = HEAD_GROUPS * b + h
                    for r, (half, j) in enumerate(ROUND_LIST):
                        lo = max(0, j * P - half * GROUP)
                        for g in range(HEAD_GROUP):
                            n = r * HEAD_GROUP + g
                            act.wait_ge(scored, CHUNKS * u + n + 1)
                            if g == 0:
                                wait(act, round_done, ROUNDS * u + r - 1)
                            nc.scalar.activation(probs[:, r % 2, g, lo:], score_ps[n % 2][:, lo:], ACT.Exp,
                                                 scale=HEAD_DIM ** -0.5).then_inc(exp_done, 1)
                        if half == 1 and j in (0, KEY_TILES - 1):
                            done = 0 if j == 0 else 1
                            act.wait_ge(round_done, ROUNDS * u + (TILES if done == 0 else ROUNDS))
                            if not (isinstance(u, int) and u == 0):
                                act.wait_ge(ring_filled, (entry(u, 0) if done
                                                          else entry(u - 1, tasks.index(("out", 0)))) + 1)
                            nc.scalar.copy(outT[:, done], out_ps[done][:]).then_inc(out_copied[done], 1)

            batches(act, body)

        @block.vector
        def _(dve):
            def maximum(G, p, g, i):
                width = (i + 1) * P
                wait(dve, ring_read, G - 1)
                dve.wait_ge(ring_filled, G + 1)
                settle(dve, idle)
                nc.vector.tensor_tensor_reduce(out=junk[:, G0(G) % 2, 0:width], in0=ring[G0(G) % 2][:, 0:width],
                                               in1=w["causal"][:, SEQ - width:SEQ], scale=1.0, scalar=-3.0e38,
                                               op0=ALU.add, op1=ALU.max,
                                               accum_out=maxima[:, p, i // TILES, g, i % TILES:i % TILES + 1]
                                               ).then_inc(ring_read, 1)

            parity = [0]

            def G0(_):
                return parity[0]

            def rows(G, u, half):
                dve.wait_ge(ring_filled, G + 1)
                wait(dve, rows_loaded[half], 32 * u)
                src = ring[G0(G) % 2][0:HEAD_GROUP * TILES, 0:P]
                nc.vector.tensor_scalar_mul(max_rows[:, half, 0], src, -1.0).then_inc(rows_hi, 1)
                dve.wait_ge(rows_hi, 2 * u + half + 1)
                nc.vector.scalar_tensor_tensor(max_rows[:, half, 1], src, -1.0, max_rows[:, half, 0],
                                               ALU.mult, ALU.subtract).then_inc(ring_read, 1)

            def out(G, u, b, h, half):
                dve.wait_ge(ring_filled, G + 1)
                src = ring[G0(G) % 2][:, 0:GROUP].rearrange("p (i g c) -> p i g c", i=TILES, g=HEAD_GROUP)
                nc.vector.reciprocal(recip[:, half], src[:, :, :, HEAD_DIM]).then_inc(recip_ready, 1)
                dve.wait_ge(recip_ready, 2 * u + half + 1)
                nc.vector.tensor_tensor(attn_v[:, b, half * TILES:(half + 1) * TILES, h],
                                        src[:, :, :, 0:HEAD_DIM],
                                        recip[:, half].unsqueeze(3).to_broadcast([P, TILES, HEAD_GROUP, HEAD_DIM]),
                                        ALU.mult).then_inc(ring_read, 1)

            for G, t in enumerate(first_maxima):
                parity[0] = G % 2
                if t[0] == "max":
                    maximum(G, 0, t[1], t[2])
                else:
                    rows(G, 0, t[1])

            def body(b):
                for h in range(HEAD_GROUPS):
                    u = HEAD_GROUPS * b + h
                    final = isinstance(b, int) and b == BATCH - 1 and h == 3
                    for n, t in enumerate(tasks):
                        G = entry(u, n)
                        parity[0] = (33 + n) % 2
                        if t[0] == "out" and t[1] == 1:
                            if not (isinstance(u, int) and u == 0):
                                out(G, u - 1, b if h else b - 1, (h - 1) % 4, 1)
                        elif final and t[0] != "out":
                            continue
                        elif t[0] == "max":
                            maximum(G, (h + 1) % 2, t[1], t[2])
                        elif t[0] == "rows":
                            rows(G, u + 1, t[1])
                        else:
                            G = entry(u, 1) if final else G
                            parity[0] = 34 % 2 if final else parity[0]
                            out(G, u, b, h, 0)
                    if final:
                        parity[0] = 35 % 2
                        out(entry(u, 2), u, b, h, 1)

            batches(dve, body)

        @block.tensor
        def _(pe):
            def maximum(G, p, slot, g, i):
                wait(pe, ring_read, G - 1)
                for c in range(0, (i + 1) * P, GROUP):
                    width = min(GROUP, (i + 1) * P - c)
                    mm = nc.tensor.matmul(ring[p][:, c:c + width], q_stack[0:72, slot, i // TILES, g, i % TILES * P:(i % TILES + 1) * P],
                                          k_stack[0:72, slot, g, c:c + width], start=True, stop=True)
                mm.then_inc(ring_filled, 1)

            def rows(G, p, half, par):
                pe.wait_ge(ring_read, G if half else G - 1)
                nc.tensor.matmul(ring[p][0:HEAD_GROUP * TILES, 0:P],
                                 maxima[:, par, half].rearrange("p g i -> p (g i)"), w["ident"][:],
                                 start=True, stop=True).then_inc(ring_filled, 1)

            def out(G, p, u, half):
                pe.wait_ge(out_copied[half], u + 1)
                wait(pe, ring_read, G - 1)
                for t in range(TILES):
                    mm = nc.tensor.transpose(ring[p][:, t * P:(t + 1) * P], outT[:, half, t * P:(t + 1) * P], w["ident"][:])
                mm.then_inc(ring_filled, 1)

            pe.wait_ge(stack_loaded[0], LOADS * 16)
            for G, t in enumerate(first_maxima):
                if t[0] == "max":
                    maximum(G, G % 2, 0, t[1], t[2])
                else:
                    rows(G, G % 2, t[1], 0)

            pe.wait_ge(ones_loaded, 16)

            def body(b):
                for h in range(HEAD_GROUPS):
                    u = HEAD_GROUPS * b + h
                    final = isinstance(b, int) and b == BATCH - 1 and h == 3

                    def values(r):
                        half, j = ROUND_LIST[r]
                        lo = max(0, j * P - half * GROUP)
                        if r == 0:
                            pe.wait_ge(V_ready, u + 1)
                        if j == 0:
                            wait(pe, out_copied[half], u)
                        pe.wait_ge(exp_done, CHUNKS * u + HEAD_GROUP * (r + 1))
                        for g in range(HEAD_GROUP):
                            mm = nc.tensor.matmul(out_ps[half][32 * g:32 * g + 32, lo:],
                                                  V_slot[:, h % 2, j, g * (HEAD_DIM + 1):g * (HEAD_DIM + 1) + 32],
                                                  probs[:, r % 2, g, lo:], start=(j == 0),
                                                  stop=(j == (half + 1) * TILES - 1))
                        mm.then_inc(round_done, 1)

                    for n in range(CHUNKS):
                        r, g = divmod(n, HEAD_GROUP)
                        half, j = ROUND_LIST[r]
                        lo = max(0, j * P - half * GROUP)
                        diagonal = j >= half * TILES
                        if n == 0:
                            pe.wait_ge(rows_loaded[0], 32 * (u + 1))
                            if not final:
                                if h < 3:
                                    pe.wait_ge(stack_loaded[h + 1], LOADS * 16 * (b + 1))
                                else:
                                    pe.wait_ge(stack_loaded[0], LOADS * 16 * (b + 2))
                        if n == HEAD_GROUP * TILES:
                            pe.wait_ge(rows_loaded[1], 32 * (u + 1))
                        wait(pe, exp_done, CHUNKS * u + n - 1)
                        mm = nc.tensor.matmul(score_ps[n % 2][:, lo:], k_stack[0:STACK, h, g, j * P:(j + 1) * P],
                                              q_stack[0:STACK, h, half, g, lo:],
                                              start=True, stop=not diagonal)
                        if diagonal:
                            mm = nc.tensor.matmul(score_ps[n % 2][:, lo:lo + P], w["ident_bf"][:], w["future_bf"][:],
                                                  start=False, stop=True)
                        mm.then_inc(scored, 1)
                        if g == 1 and r:
                            values(r - 1)
                        for k, t in enumerate(tasks):
                            if places[k] != n:
                                continue
                            G, p = entry(u, k), (33 + k) % 2
                            if t == ("out", 1):
                                if not (isinstance(u, int) and u == 0):
                                    out(G, p, u - 1, 1)
                            elif final and t[0] != "out":
                                continue
                            elif t[0] == "max":
                                maximum(G, p, (h + 1) % 4, t[1], t[2])
                            elif t[0] == "rows":
                                rows(G, p, t[1], (h + 1) % 2)
                            else:
                                out(entry(u, 1) if final else G, 34 % 2 if final else p, u, 0)
                    values(ROUNDS - 1)
                    if final:
                        out(entry(u, 2), 35 % 2, u, 1)

            batches(pe, body)



CHUNK_LEN = 64
ALL_TILES = BATCH * SEQ // P
EXPERTS = 16
COMB_ROWS = 96


def pairs(engine, body):
    body(0)
    with engine.Fori(1, GROUPS // 2) as g2:
        body(g2)


class Norm:

    def __init__(self, nc, keep, m, name, ident):
        self.nc, self.keep, self.ident = nc, keep, ident
        self.stats = m.sb(name + "_stats", [P, ALL_TILES, 6])
        self.work = m.sb(name + "_work", [P, 5, ALL_TILES])
        self.mean, self.rstd = m.sb(name + "_mean", [P, ALL_TILES]), m.sb(name + "_rstd", [P, ALL_TILES])
        self.xn = m.sb(name + "_xn", [P, 2, TILES, P])
        self.turn_ps = [m.ps(f"{name}_turn{n}", [P, GROUP]) for n in range(2)]
        self.var_ready, self.rstd_ready = m.sem(name + "_var"), m.sem(name + "_rstd")
        self.xn_ready, self.turned, self.copied = m.sem(name + "_xn"), m.sem(name + "_turned"), m.sem(name + "_copied")
        self.own_sem = m.sem(name + "_own")
        self.x_v = keep.x[:].rearrange("p (g t) e -> p g t e", t=TILES)
        self.stats_v = self.stats[:].rearrange("p (g t) s -> p g t s", t=TILES)
        self.xT_v = keep.xT and keep.xT[:].rearrange("p (g n) -> p g n", n=GROUP)

    def take_stats(self, g):
        for t in range(TILES):
            last = self.nc.vector.bn_stats(self.stats_v[:, g, t], self.x_v[:, g, t])
        return last

    def finish(self, dve):
        nc, s, work = self.nc, self.stats, self.work
        own = Chain(dve, self.own_sem)
        total, diff, m2, square, var = (work[:, n] for n in range(5))
        nc.vector.tensor_tensor(total, s[:, :, 1], s[:, :, 4], ALU.add)
        nc.vector.tensor_tensor(diff, s[:, :, 1], s[:, :, 4], ALU.subtract)
        own.add(nc.vector.tensor_tensor(m2, s[:, :, 2], s[:, :, 5], ALU.add))
        own.wait()
        nc.vector.tensor_scalar_mul(self.mean[:], total, 0.5)
        own.add(nc.vector.scalar_tensor_tensor(square, diff, 0.25, diff, ALU.mult, ALU.mult))
        own.wait()
        own.add(nc.vector.scalar_tensor_tensor(var, m2, 1.0 / P, square, ALU.mult, ALU.add))
        own.wait()
        nc.vector.tensor_scalar_add(total, var, LN_EPS).then_inc(self.var_ready, 1)

    def root(self, pool):
        pool.wait_ge(self.var_ready, 1)
        self.nc.gpsimd.tensor_tensor(self.rstd[:], self.work[:, 0], self.keep.minus_half[:], ALU.pow).then_inc(self.rstd_ready, 1)

    def scale(self, dve, g, q):
        wait(dve, self.turned, g - 1)
        for t in range(TILES):
            last = self.nc.vector.tensor_scalar(self.xn[:, q, t], self.x_v[:, g, t],
                                                self.mean[:].rearrange("p (g t) -> p g t", t=TILES)[:, g, t:t + 1],
                                                self.rstd[:].rearrange("p (g t) -> p g t", t=TILES)[:, g, t:t + 1],
                                                ALU.subtract, ALU.mult)
        last.then_inc(self.xn_ready, 1)

    def turn(self, pe, g, q):
        pe.wait_ge(self.xn_ready, g + 1)
        wait(pe, self.copied, g - 1)
        for t in range(TILES):
            mm = self.nc.tensor.transpose(self.turn_ps[q][:, t * P:(t + 1) * P], self.xn[:, q, t], self.ident)
        mm.then_inc(self.turned, 1)

    def copy(self, act, g, q):
        act.wait_ge(self.turned, g + 1)
        self.nc.scalar.copy(self.xT_v[:, g], self.turn_ps[q][:]).then_inc(self.copied, 1)


def output_projection_stage(nc, keep, w, io):
    with ExitStack() as stack:
        m = Memory(nc, stack, "out_")
        norm = Norm(nc, keep, m, "n0", w["ident"][:])
        a_in = m.sb("a_in", [P, 2, BATCH, P])
        aT = m.sb("aT", [P, 2, GROUP])
        x_in = m.sb("x_in2", [P, 2, TILES, P])
        a_ps = [m.ps(f"a_ps{n}", [P, GROUP]) for n in range(2)]
        y_ps = [m.ps(f"y_ps{n}", [P, GROUP]) for n in range(2)]
        x_loaded = [m.sem("x2_loaded0"), m.sem("x2_loaded1")]
        a_ready, biased, a_turned, aT_ready = m.sem("a_ready"), m.sem("biased"), m.sem("a_turned"), m.sem("aT_ready")
        y_done, x_ready, stats_done = m.sem("y_done"), m.sem("x_ready"), m.sem("stats_done")
        x_v = io["x"].rearrange("b (c s) e -> c b s e", s=CHUNK_LEN)
        block = stack.enter_context(nc.Block())

        @block.sync
        def _(sp):
            def body(g2):
                for q in range(2):
                    g = 2 * g2 + q
                    wait(sp, x_ready, g - 1)
                    for t in range(TILES):
                        for half in range(2):
                            sp.dma_start(x_in[64 * half:64 * half + 64, q, t],
                                         x_v[2 * g + t // 2, 2 * (t % 2) + half]).then_inc(x_loaded[q], 16)

            pairs(sp, body)

        @block.gpsimd
        def _(pool):
            def body(g2):
                for q in range(2):
                    g = 2 * g2 + q
                    wait(pool, a_turned, g - 1)
                    nc.gpsimd.tensor_copy(a_in[:, q], keep.attn[:, :, g]).then_inc(a_ready, 1)
                    pool.wait_ge(x_loaded[q], 128 * (g2 + 1))
                    nc.gpsimd.tensor_tensor(x_in[:, q], x_in[:, q], w["bo"][:].unsqueeze(1).to_broadcast([P, TILES, P]),
                                            ALU.add).then_inc(biased, 1)

            pairs(pool, body)
            norm.root(pool)

        @block.tensor
        def _(pe):
            def body(g2):
                for q in range(2):
                    g = 2 * g2 + q
                    pe.wait_ge(a_ready, g + 1)
                    wait(pe, aT_ready, g - 1)
                    for b in range(BATCH):
                        mm = nc.tensor.transpose(a_ps[q][:, b * P:(b + 1) * P], a_in[:, q, b], w["ident"][:])
                    mm.then_inc(a_turned, 1)
                    pe.wait_ge(aT_ready, g + 1)
                    wait(pe, x_ready, g - 1)
                    for t in range(TILES):
                        mm = nc.tensor.matmul(y_ps[q][:, t * P:(t + 1) * P], aT[:, q, t * P:(t + 1) * P], w["wo"][:],
                                              start=True, stop=True)
                    mm.then_inc(y_done, 1)

            pairs(pe, body)

            def turns(g2):
                for q in range(2):
                    norm.turn(pe, 2 * g2 + q, q)

            pairs(pe, turns)

        @block.scalar
        def _(act):
            def body(g2):
                for q in range(2):
                    g = 2 * g2 + q
                    act.wait_ge(a_turned, g + 1)
                    wait(act, y_done, g - 1)
                    nc.scalar.copy(aT[:, q].rearrange("p (c b s) -> p c b s", c=2, b=BATCH),
                                   a_ps[q][:].rearrange("p (b c s) -> p c b s", b=BATCH, c=2)).then_inc(aT_ready, 1)

            pairs(act, body)

            def copies(g2):
                for q in range(2):
                    norm.copy(act, 2 * g2 + q, q)

            pairs(act, copies)

        @block.vector
        def _(dve):
            def body(g2):
                for q in range(2):
                    g = 2 * g2 + q
                    dve.wait_ge(y_done, g + 1)
                    dve.wait_ge(biased, g + 1)
                    nc.vector.tensor_tensor(norm.x_v[:, g], y_ps[q][:].rearrange("p (t e) -> p t e", t=TILES), x_in[:, q],
                                            ALU.add).then_inc(x_ready, 1)
                    dve.wait_ge(x_ready, g + 1)
                    norm.take_stats(g).then_inc(stats_done, 1)

            pairs(dve, body)
            dve.wait_ge(stats_done, GROUPS)
            norm.finish(dve)
            dve.wait_ge(norm.rstd_ready, 1)

            def scales(g2):
                for q in range(2):
                    norm.scale(dve, 2 * g2 + q, q)

            pairs(dve, scales)


def route_stage(nc, keep, w, router, top_k, sigmoid_bias=None, route_scale=None):
    with ExitStack() as stack:
        m = Memory(nc, stack, "rt%d_" % top_k)
        scores = m.sb("scores", [P, ALL_TILES, EXPERTS])
        ranked = m.sb("ranked", [P, ALL_TILES, 8])
        ranks = m.sb("ranks", [P, ALL_TILES, 8], mybir.dt.uint32)
        best = m.sb("best", [P, ALL_TILES, top_k])
        raised = m.sb("raised", [P, ALL_TILES, EXPERTS])
        chosen = m.sb("chosen", [P, ALL_TILES, EXPERTS])
        hit = m.sb("hit", [P, ALL_TILES, EXPERTS])
        gates = m.sb("gates", [P, ALL_TILES, EXPERTS])
        comb = m.sb("comb", [P, ALL_TILES, EXPERTS])
        sums = m.sb("sums", [P, 3, ALL_TILES])
        rest = m.sb("comb_rest", [EXPERTS, 2, GROUP])
        mid = m.sb("comb_mid", [EXPERTS, 2, GROUP], BF16)
        high = m.sb("comb_high", [EXPERTS, 2, GROUP])
        logit_ps = m.ps("logit_ps", [P, ALL_TILES * EXPERTS])
        comb_ps = [m.ps(f"combT_ps{n}", [P, GROUP]) for n in range(2)]
        clear, logits_done, raised_ready = m.sem("comb_clear"), m.sem("logits_done"), m.sem("raised_ready")
        gates_ready, comb_ready, turned = m.sem("gates_ready"), m.sem("comb_ready"), m.sem("comb_turned")
        hi_done, rest_done, mid_done, parts_done = m.sem("chi"), m.sem("crest"), m.sem("cmid"), m.sem("cparts")
        own_sem = m.sem("route_own")
        comb3_v = keep.comb3[:].rearrange("p (g n) -> p g n", n=GROUP)
        wide = [P, ALL_TILES, EXPERTS]
        block = stack.enter_context(nc.Block())

        @block.tensor
        def _(pe):
            for t in range(ALL_TILES):
                mm = nc.tensor.matmul(logit_ps[:, t * EXPERTS:(t + 1) * EXPERTS], keep.xT[:, t * P:(t + 1) * P], router[:],
                                      start=True, stop=True)
            mm.then_inc(logits_done, 1)
            pe.wait_ge(comb_ready, 1)
            for g in range(GROUPS):
                wait(pe, rest_done, g - 1)
                for t in range(TILES):
                    mm = nc.tensor.matmul(comb_ps[g % 2][0:EXPERTS, t * P:(t + 1) * P], comb[:, TILES * g + t], w["ident"][:],
                                          start=True, stop=True)
                mm.then_inc(turned, 1)

        @block.scalar
        def _(act):
            act.wait_ge(raised_ready, 1)
            nc.scalar.activation(gates[:], raised[:], ACT.Sigmoid if sigmoid_bias is not None else ACT.Exp).then_inc(gates_ready, 1)
            act.wait_ge(clear, 1)
            for g in range(GROUPS):
                q = g % 2
                act.wait_ge(turned, g + 1)
                nc.scalar.copy(comb3_v[0:EXPERTS, g], comb_ps[q][0:EXPERTS, :]).then_inc(hi_done, 1)
                act.wait_ge(rest_done, g + 1)
                wait(act, parts_done, g - 1)
                nc.scalar.copy(mid[:, q], rest[:, q]).then_inc(mid_done, 1)

        @block.gpsimd
        def _(pool):
            nc.gpsimd.memset(keep.comb3[:], 0.0).then_inc(clear, 1)
            pool.wait_ge(clear, 1)
            for g in range(GROUPS):
                q = g % 2
                pool.wait_ge(mid_done, g + 1)
                nc.gpsimd.tensor_copy(comb3_v[32:32 + EXPERTS, g], mid[:, q])
                nc.gpsimd.tensor_tensor(comb3_v[64:64 + EXPERTS, g], rest[:, q], mid[:, q],
                                        ALU.subtract).then_inc(parts_done, 1)

        @block.vector
        def _(dve):
            own = Chain(dve, own_sem)
            flat = logit_ps[:].rearrange("p (t e) -> p t e", t=ALL_TILES)
            dve.wait_ge(logits_done, 1)
            if sigmoid_bias is not None:
                own.add(nc.vector.tensor_copy(raised[:], flat))
                own.wait()
                dve.sem_inc(raised_ready, 1)
                dve.wait_ge(gates_ready, 1)
                own.add(nc.vector.tensor_tensor(scores[:], gates[:], sigmoid_bias[:].unsqueeze(1).to_broadcast(wide), ALU.add))
            else:
                own.add(nc.vector.tensor_copy(scores[:], flat))
            own.wait()
            for t in range(ALL_TILES):
                last = nc.vector.max(ranked[:, t], scores[:, t])
            own.add(last)
            own.wait()
            if sigmoid_bias is None:
                nc.vector.tensor_tensor(raised[:], scores[:], ranked[:, :, 0:1].to_broadcast(wide),
                                        ALU.subtract).then_inc(raised_ready, 1)
            for t in range(ALL_TILES):
                last = nc.vector.max_index(ranks[:, t], ranked[:, t], scores[:, t])
            own.add(last)
            own.wait()
            own.add(nc.vector.tensor_copy(best[:], ranks[:, :, 0:top_k]))
            own.wait()
            for k in range(top_k):
                dst = chosen if k == 0 else hit
                own.add(nc.vector.tensor_tensor(dst[:], w["indices"][:].unsqueeze(1).to_broadcast(wide),
                                                best[:, :, k:k + 1].to_broadcast(wide), ALU.is_equal))
                own.wait()
                if k:
                    own.add(nc.vector.tensor_tensor(chosen[:], chosen[:], hit[:], ALU.add))
                    own.wait()
            dve.wait_ge(gates_ready, 1)
            nc.vector.reduce_sum(sums[:, 0], gates[:], mybir.AxisListType.X)
            own.add(nc.vector.tensor_tensor(chosen[:], chosen[:], gates[:], ALU.mult))
            own.wait()
            own.add(nc.vector.reduce_sum(sums[:, 1], chosen[:], mybir.AxisListType.X))
            own.wait()
            if sigmoid_bias is None:
                own.add(nc.vector.scalar_tensor_tensor(sums[:, 2], sums[:, 0], 1e-9, sums[:, 1], ALU.mult, ALU.add))
            else:
                own.add(nc.vector.tensor_scalar_mul(sums[:, 2], sums[:, 1], 1.0 / route_scale))
            own.wait()
            own.add(nc.vector.reciprocal(sums[:, 0], sums[:, 2]))
            own.wait()
            nc.vector.tensor_tensor(comb[:], chosen[:], sums[:, 0].unsqueeze(2).to_broadcast(wide),
                                    ALU.mult).then_inc(comb_ready, 1)
            for g in range(GROUPS):
                q = g % 2
                dve.wait_ge(hi_done, g + 1)
                wait(dve, parts_done, g - 1)
                nc.vector.tensor_tensor(rest[:, q], comb_ps[q][0:EXPERTS, :], comb3_v[0:EXPERTS, g],
                                        ALU.subtract).then_inc(rest_done, 1)


def expert_stage(nc, keep, w, name, routed, shared_rows, store=None):
    chunks = routed + 1
    rows = lambda c: shared_rows if c == routed else P
    gate_w, up_w, down_w, spread = w[name + "_gate"], w[name + "_up"], w[name + "_down"], w[name + "_spread"]
    with ExitStack() as stack:
        m = Memory(nc, stack, name + "_")
        gated = m.sb("gated", [P, 2, GROUP])
        product = m.sb("product", [P, 2, GROUP])
        hid = m.sb("hid", [P, 2, chunks, GROUP])
        result = m.sb("result", [P, 2, TILES, P]) if store is not None else None
        gate_ps = [m.ps(f"gate_ps{n}", [P, GROUP]) for n in range(2)]
        up_ps = [m.ps(f"up_ps{n}", [P, GROUP]) for n in range(2)]
        comb_ps = m.ps("comb_ps", [P, GROUP])
        y_ps = [m.ps(f"yy_ps{n}", [P, GROUP]) for n in range(2)]
        gate_done, up_done, silu_done = m.sem("gate_done"), m.sem("up_done"), m.sem("silu_done")
        comb_shown, product_done, hid_done = m.sem("comb_shown"), m.sem("product_done"), m.sem("hid_done")
        y_done, x_ready = m.sem("yy_done"), m.sem("xx_ready")
        stored = [m.sem("stored0"), m.sem("stored1")]
        x_v = keep.x[:].rearrange("p (g t) e -> p g t e", t=TILES)
        xT_v = keep.xT[:].rearrange("p (g n) -> p g n", n=GROUP)
        comb3_v = keep.comb3[:].rearrange("p (g n) -> p g n", n=GROUP)
        block = stack.enter_context(nc.Block())

        @block.tensor
        def _(pe):
            def down(g, q):
                pe.wait_ge(hid_done, chunks * (g + 1))
                wait(pe, x_ready, g - 1)
                for t in range(TILES):
                    for c in range(chunks):
                        mm = nc.tensor.matmul(y_ps[q][:, t * P:(t + 1) * P], hid[0:rows(c), q, c, t * P:(t + 1) * P],
                                              down_w[0:rows(c), c], start=(c == 0), stop=(c == chunks - 1))
                mm.then_inc(y_done, 1)

            def body(g2):
                for q in range(2):
                    g = 2 * g2 + q
                    for c in range(chunks):
                        n = chunks * g + c
                        par = (chunks * q + c) % 2
                        wait(pe, silu_done, n - 1)
                        nc.tensor.matmul(gate_ps[par][0:rows(c), :], gate_w[:, c, 0:rows(c)], xT_v[:, g],
                                         start=True, stop=True).then_inc(gate_done, 1)
                        wait(pe, product_done, n - 1)
                        nc.tensor.matmul(up_ps[par][0:rows(c), :], up_w[:, c, 0:rows(c)], xT_v[:, g],
                                         start=True, stop=True).then_inc(up_done, 1)
                        if c < routed:
                            wait(pe, hid_done, n if c else n - 1)
                            nc.tensor.matmul(comb_ps[:], spread[:, c], comb3_v[:, g], start=True,
                                             stop=True).then_inc(comb_shown, 1)
                        if c == 1 and not (isinstance(g, int) and g == 0):
                            down(g - 1, 1 - q)

            pairs(pe, body)
            down(GROUPS - 1, 1)

        @block.scalar
        def _(act):
            def body(g2):
                for q in range(2):
                    g = 2 * g2 + q
                    for c in range(chunks):
                        n, par = chunks * g + c, (chunks * q + c) % 2
                        act.wait_ge(gate_done, n + 1)
                        wait(act, product_done, n - 1)
                        nc.scalar.activation(gated[0:rows(c), par], gate_ps[par][0:rows(c), :],
                                             ACT.Silu).then_inc(silu_done, 1)

            pairs(act, body)

        @block.vector
        def _(dve):
            def residual(g, q, g2):
                dve.wait_ge(y_done, g + 1)
                y = y_ps[q][:].rearrange("p (t e) -> p t e", t=TILES)
                if store is not None:
                    wait(dve, stored[q], 128 * g2)
                    nc.vector.tensor_tensor(result[:, q], y, x_v[:, g], ALU.add).then_inc(x_ready, 1)
                else:
                    nc.vector.tensor_tensor(x_v[:, g], y, x_v[:, g], ALU.add).then_inc(x_ready, 1)

            def body(g2):
                for q in range(2):
                    g = 2 * g2 + q
                    for c in range(chunks):
                        n, par = chunks * g + c, (chunks * q + c) % 2
                        dve.wait_ge(up_done, n + 1)
                        dve.wait_ge(silu_done, n + 1)
                        R = rows(c)
                        if c == 0:
                            wait(dve, y_done, g - 1)
                        if c < routed:
                            wait(dve, hid_done, n - 1)
                            nc.vector.tensor_tensor(product[:, par], up_ps[par][:], gated[:, par],
                                                    ALU.mult).then_inc(product_done, 1)
                            dve.wait_ge(comb_shown, routed * g + c + 1)
                            dve.wait_ge(product_done, n + 1)
                            nc.vector.tensor_tensor(hid[:, q, c], comb_ps[:], product[:, par], ALU.mult).then_inc(hid_done, 1)
                        else:
                            nc.vector.tensor_tensor(hid[0:R, q, c], up_ps[par][0:R, :], gated[0:R, par],
                                                    ALU.mult).then_inc(product_done, 1)
                            dve.wait_ge(product_done, n + 1)
                            dve.sem_inc(hid_done, 1)
                        if c == 2 and not (isinstance(g, int) and g == 0):
                            residual(g - 1, 1 - q, g2 if q else g2 - 1)

            pairs(dve, body)
            residual(GROUPS - 1, 1, GROUPS // 2 - 1)

        if store is not None:
            out_v = store.rearrange("b (c s) e -> c b s e", s=CHUNK_LEN)

            @block.sync
            def _(sp):
                def body(g2):
                    for q in range(2):
                        g = 2 * g2 + q
                        sp.wait_ge(x_ready, g + 1)
                        for t in range(TILES):
                            for half in range(2):
                                sp.dma_start(out_v[2 * g + t // 2, 2 * (t % 2) + half],
                                             result[64 * half:64 * half + 64, q, t]).then_inc(stored[q], 16)

                pairs(sp, body)
                for q in range(2):
                    sp.wait_ge(stored[q], 128 * GROUPS // 2)



INNER = 256
RMS_EPS = 1e-6
STEPS = SEQ // CHUNK_LEN
BASE_RATE = 0.01
CHUNK_TOKENS = BATCH * CHUNK_LEN
HALVES_IN = INNER // P


def memory_inputs_stage(nc, keep, w):
    with ExitStack() as stack:
        m = Memory(nc, stack, "mi_")
        norm = Norm(nc, keep, m, "n1", w["ident"][:])
        xT_s = m.sb("xT_s", [P, 2, GROUP])
        dot_terms = m.sb("dot_terms", [P, 3, TILES, P])
        raw = m.sb("raw", [P, 2, TILES, P])
        squares = m.sb("squares", [P, 2, TILES, P])
        mean_sq = m.sb("mean_sq", [P, 2, 2, TILES])
        inv = m.sb("inv", [P, 2, TILES])
        normed = m.sb("normed", [P, 2, TILES, P])
        proj_ps = [m.ps(f"proj{n}", [P, GROUP]) for n in range(3)]
        back_ps = [m.ps(f"back{n}", [P, GROUP]) for n in range(2)]
        stats_done, x_read, xT_ready = m.sem("st_done"), m.sem("xread"), m.sem("xT_s_ready")
        dots_ready, dots_taken = m.sem("dots_ready"), m.sem("dots_taken")
        projected, activated, v_active = m.sem("projected3"), m.sem("activated"), m.sem("v_active")
        squared, summed, inv_ready = m.sem("squared"), m.sem("summed_sq"), m.sem("inv_ready")
        normed_ready, kept, back_done, back_kept = m.sem("normed_r"), m.sem("nkept"), m.sem("back_d"), m.sem("back_k")
        scaled, own_sem, pool_sem = m.sem("scaled"), m.sem("mi_own"), m.sem("mi_pool")
        tok_v = [a[:].rearrange("p (g t) e -> p g t e", t=TILES) for a in (keep.q, keep.k, keep.v)]
        T_v = [a[:].rearrange("p (g n) -> p g n", n=GROUP) for a in (keep.qT, keep.kT)]
        dots_v = keep.dots[:].rearrange("p d (g t) -> p g d t", t=TILES)
        block = stack.enter_context(nc.Block())

        @block.vector
        def _(dve):
            own = Chain(dve, own_sem)

            def statistics(g2):
                for q in range(2):
                    norm.take_stats(2 * g2 + q).then_inc(stats_done, 1)

            pairs(dve, statistics)
            dve.wait_ge(stats_done, GROUPS)
            norm.finish(dve)
            dve.wait_ge(norm.rstd_ready, 1)

            def body(g2):
                for q in range(2):
                    g = 2 * g2 + q
                    wait(dve, dots_ready, g - 1)
                    norm.scale(dve, g, q)
                    dve.wait_ge(dots_ready, g + 1)
                    nc.vector.reduce_sum(dots_v[:, g], dot_terms[:], mybir.AxisListType.X).then_inc(dots_taken, 1)
                    own.at(g)
                    dve.wait_ge(squared, g + 1)
                    wait(dve, inv_ready, g)
                    own.add(nc.vector.reduce_sum(mean_sq[:, 0], squares[:], mybir.AxisListType.X))
                    own.wait()
                    nc.vector.tensor_scalar(mean_sq[:, 1], mean_sq[:, 0], 1.0 / P, RMS_EPS, ALU.mult, ALU.add).then_inc(summed, 1)

            pairs(dve, body)

        @block.gpsimd
        def _(pool):
            norm.root(pool)
            own = Chain(pool, pool_sem)

            def body(g2):
                for q in range(2):
                    g = 2 * g2 + q
                    own.at(g)
                    pool.wait_ge(norm.xn_ready, g + 1)
                    wait(pool, dots_taken, g)
                    for d in range(3):
                        last = nc.gpsimd.tensor_tensor(dot_terms[:, d], norm.xn[:, q],
                                                       w["gate_rows"][:, d:d + 1].to_broadcast([P, TILES, P]), ALU.mult)
                    last.then_inc(dots_ready, 1)
                    pool.wait_ge(activated, g + 1)
                    wait(pool, summed, g)
                    nc.gpsimd.tensor_tensor(squares[:], raw[:], raw[:], ALU.mult).then_inc(squared, 1)
                    pool.wait_ge(summed, g + 1)
                    nc.gpsimd.tensor_tensor(inv[:], mean_sq[:, 1], keep.minus_half[:, 0:2 * TILES].rearrange("p (n t) -> p n t", n=2),
                                            ALU.pow).then_inc(inv_ready, 1)
                    pool.wait_ge(inv_ready, g + 1)
                    wait(pool, back_done, g)
                    for n in range(2):
                        last = nc.gpsimd.tensor_tensor(normed[:, n], raw[:, n], inv[:, n].unsqueeze(2).to_broadcast([P, TILES, P]), ALU.mult)
                    last.then_inc(scaled, 1)
                    pool.wait_ge(scaled, g + 1)
                    for n in range(2):
                        last = nc.gpsimd.tensor_tensor(normed[:, n], normed[:, n], w["qk_norm"][:, n:n + 1].to_broadcast([P, TILES, P]), ALU.mult)
                    last.then_inc(normed_ready, 1)
                    pool.wait_ge(normed_ready, g + 1)
                    for n in range(2):
                        last = nc.gpsimd.tensor_copy(tok_v[n][:, g], normed[:, n])
                    last.then_inc(kept, 1)
                    pool.wait_ge(kept, g + 1)

            pairs(pool, body)

        @block.scalar
        def _(act):
            def back(g):
                act.wait_ge(back_done, g + 1)
                for n in range(2):
                    last = nc.scalar.copy(T_v[n][:, g], back_ps[n][:])
                last.then_inc(back_kept, 1)

            def body(g2):
                for q in range(2):
                    g = 2 * g2 + q
                    act.wait_ge(norm.turned, g + 1)
                    wait(act, projected, g - 1)
                    nc.scalar.copy(xT_s[:, q], norm.turn_ps[q][:]).then_inc(norm.copied, 1)
                    act.wait_ge(projected, g + 1)
                    wait(act, scaled, g)
                    for n in range(2):
                        last = nc.scalar.activation(raw[:, n], proj_ps[n][:].rearrange("p (t e) -> p t e", t=TILES), ACT.Silu)
                    last.then_inc(activated, 1)
                    nc.scalar.activation(tok_v[2][:, g], proj_ps[2][:].rearrange("p (t e) -> p t e", t=TILES), ACT.Silu).then_inc(v_active, 1)
                    if not (isinstance(g, int) and g == 0):
                        back(g - 1)

            pairs(act, body)
            back(GROUPS - 1)

        @block.tensor
        def _(pe):
            def back(g):
                pe.wait_ge(normed_ready, g + 1)
                wait(pe, back_kept, g)
                for n in range(2):
                    for t in range(TILES):
                        mm = nc.tensor.transpose(back_ps[n][:, t * P:(t + 1) * P], normed[:, n, t], w["ident"][:])
                mm.then_inc(back_done, 1)

            def body(g2):
                for q in range(2):
                    g = 2 * g2 + q
                    norm.turn(pe, g, q)
                    pe.wait_ge(norm.copied, g + 1)
                    wait(pe, v_active, g)
                    for t in range(TILES):
                        for n in range(3):
                            mm = nc.tensor.matmul(proj_ps[n][:, t * P:(t + 1) * P], xT_s[:, q, t * P:(t + 1) * P], w["qkv1"][:, n],
                                                  start=True, stop=True)
                    mm.then_inc(projected, 1)
                    if not (isinstance(g, int) and g == 0):
                        back(g - 1)

            pairs(pe, body)
            back(GROUPS - 1)


def recurrence_stage(nc, keep, w):
    W0, W1, W1T, GAIN, END = 0, INNER, 2 * INNER, 3 * INNER, 3 * INNER + P
    with ExitStack() as stack:
        m = Memory(nc, stack, "rc_")
        mem, moment = keep.mem, m.sb("moment", [P, END])
        faded, moment_faded = m.sb("faded", [P, END]), m.sb("moment_faded", [P, END])
        k_s = m.sb("k_s", [P, 2, 2, P])
        kT_s = m.sb("kT_s", [P, 2, CHUNK_TOKENS])
        kv = m.sb("kv", [P, 2, 2, P])
        gates = m.sb("gates_s", [P, 3, ALL_TILES])
        term_sums = m.sb("term_sums", [P, 3, ALL_TILES])
        pair_sum = m.sb("pair_sum", [P, 2, STEPS])
        rate_s = m.sb("rate_s", [P, 2, 2])
        sigT, sig = m.sb("sigT", [P, 2, CHUNK_TOKENS]), m.sb("sig", [P, 2, INNER])
        hT, h = m.sb("hT", [P, 2, CHUNK_TOKENS]), m.sb("h", [P, 2, INNER])
        slope = m.sb("slope", [P, 2, 2, INNER])
        sq_junk = m.sb("sq_junk", [P, 3, 2 * INNER])
        ss = m.sb("ss", [P, 2, 2])
        r = m.sb("r", [P, 2])
        yr = m.sb("yr", [P, 2, P])
        yg = m.sb("yg", [P, 2, P])
        G = m.sb("G", [P, 2, P])
        D = m.sb("D", [P, 2, P])
        Gy = m.sb("Gy", [P, 2, P])
        Dy_junk = m.sb("Dy_junk", [P, 2, P])
        Dy = m.sb("Dy", [P, 3, 2])
        inner = m.sb("inner", [P, 2, P])
        dy = m.sb("dy", [P, 2, P])
        dyT = m.sb("dyT", [P, 2 * P])
        da = m.sb("da", [P, 2, INNER])
        norms = m.sb("norms", [P, 3])
        size = m.sb("size", [P, 4])
        aT_ps = m.ps("aT_ps", [P, 2, CHUNK_TOKENS])
        a_ps = m.ps("aa_ps", [P, 2, INNER])
        y_ps = m.ps("y3_ps", [P, 4, P])
        dyT_ps = m.ps("dyT_ps", [P, 4 * P])
        dh_ps = m.ps("dh_ps", [P, 2, INNER])
        g01_ps = m.ps("g01_ps", [P, 2 * INNER])
        g1T_ps = m.ps("g1T_ps", [P, 2 * INNER])
        total_ps = m.ps("total_ps", [P, 2 * INNER])

        names = ("state_set dots_summed gates_ready k_ready kv_ready faded_ready sigT_done sig_done hT_ready h_ready "
                 "slope_ready aT_done a_done y_done y_squared ms_ready r_ready yr_ready yg_ready G_ready D_ready Gy_ready "
                 "Dy_ready dy_ready dyT_done dyT_ready dh_done da_ready g1_done g0_done gain_done w1_squared w0_squared "
                 "gain_squared totalled rooted clip_ready mem_ready moment_ready sums_copied pairs_summed gates_final inner_ready Dy_scaled c1_ready size_ready size_eps size_inv own_p idle").split()
        S = {n: m.sem("rc_" + n) for n in names}
        k_v = keep.k[:].rearrange("p (c t) e -> p c t e", t=2)
        v_v = keep.v[:].rearrange("p (c t) e -> p c t e", t=2)
        kT_v = keep.kT[:].rearrange("p (c n) -> p c n", n=CHUNK_TOKENS)
        gate_v = gates[:].rearrange("p d (c t) -> p d c t", t=2)
        step_v = gates[:].rearrange("p d (c o) -> p d c o", o=1)
        clip = m.sb("clip", [P, 1])
        gain_b = lambda: mem[:, GAIN:END].unsqueeze(1).to_broadcast([P, 2, P])
        block = stack.enter_context(nc.Block())

        def steps(engine, body):
            body(0)
            with engine.Fori(1, STEPS // 2 - 1) as c2:
                body(c2)
            body(STEPS // 2 - 1)

        @block.tensor
        def _(pe):
            nc.tensor.matmul(total_ps[:, 0:ALL_TILES], w["block_ones"][:], keep.dots[:, 0], start=True, stop=True)
            nc.tensor.matmul(total_ps[:, ALL_TILES:3 * ALL_TILES], w["ones"][:], keep.dots[:, 1:3].rearrange("p d t -> p (d t)"),
                             start=True, stop=True).then_inc(S["dots_summed"], 1)

            def body(c2):
                for q in range(2):
                    c = 2 * c2 + q
                    pe.wait_ge(S["k_ready"], c + 1)
                    wait(pe, S["mem_ready"], c)
                    wait(pe, S["hT_ready"], c)
                    for i in range(2):
                        mm = nc.tensor.matmul(aT_ps[:, i], mem[:, W0 + i * P:W0 + (i + 1) * P], kT_s[:, q], start=True, stop=True)
                    mm.then_inc(S["aT_done"], 1)
                    wait(pe, S["h_ready"], c)
                    for t in range(2):
                        mm = nc.tensor.matmul(a_ps[:, t], kT_s[:, q, t * P:(t + 1) * P], mem[:, W0:W0 + INNER], start=True, stop=True)
                    mm.then_inc(S["a_done"], 1)
                    pe.wait_ge(S["hT_ready"], c + 1)
                    wait(pe, S["yr_ready"], c)
                    for t in range(2):
                        for i in range(2):
                            mm = nc.tensor.matmul(y_ps[:, t], hT[:, i, t * P:(t + 1) * P], mem[:, W1T + i * P:W1T + (i + 1) * P],
                                                  start=(i == 0), stop=(i == 1))
                    mm.then_inc(S["y_done"], 1)
                    pe.wait_ge(S["dy_ready"], c + 1)
                    wait(pe, S["dyT_ready"], c)
                    for t in range(2):
                        mm = nc.tensor.transpose(dyT_ps[:, t * P:(t + 1) * P], dy[:, t], w["ident"][:])
                    mm.then_inc(S["dyT_done"], 1)
                    pe.wait_ge(S["h_ready"], c + 1)
                    wait(pe, S["moment_ready"], c)
                    for t in range(2):
                        nc.tensor.matmul(g01_ps[:, W1:W1 + INNER], dy[:, t], h[:, t], start=(t == 0), stop=(t == 1))
                    for i in range(2):
                        for t in range(2):
                            nc.tensor.matmul(g1T_ps[:, i * P:(i + 1) * P], h[:, t, i * P:(i + 1) * P], dy[:, t],
                                             start=(t == 0), stop=(t == 1))
                    pe.wait_ge(S["Gy_ready"], c + 1)
                    for t in range(2):
                        mm = nc.tensor.matmul(g1T_ps[:, INNER:INNER + P], w["ones"][:], Gy[:, t], start=(t == 0), stop=(t == 1))
                    mm.then_inc(S["g1_done"], 1)
                    pe.wait_ge(S["dyT_ready"], c + 1)
                    wait(pe, S["da_ready"], c)
                    for t in range(2):
                        mm = nc.tensor.matmul(dh_ps[:, t], dyT[:, t * P:(t + 1) * P], mem[:, W1:W1 + INNER], start=True, stop=True)
                    mm.then_inc(S["dh_done"], 1)
                    pe.wait_ge(S["da_ready"], c + 1)
                    pe.wait_ge(S["w1_squared"], c + 1)
                    for t in range(2):
                        mm = nc.tensor.matmul(g01_ps[:, W0:W0 + INNER], k_s[:, q, t], da[:, t], start=(t == 0), stop=(t == 1))
                    mm.then_inc(S["g0_done"], 1)
                    pe.wait_ge(S["w0_squared"], c + 1)
                    for n in range(3):
                        mm = nc.tensor.matmul(total_ps[:, 0:1], w["ones"][:] if n < 2 else w["mean_ones"][:], norms[:, n:n + 1],
                                              start=(n == 0), stop=(n == 2))
                    mm.then_inc(S["totalled"], 1)

            steps(pe, body)

        @block.scalar
        def _(act):
            act.wait_ge(S["pairs_summed"], 1)
            nc.scalar.activation(gates[:, 0], term_sums[:, 0], ACT.Sigmoid)
            nc.scalar.activation(gates[:, 1:3, 0:STEPS], pair_sum[:], ACT.Sigmoid, scale=1.0 / BATCH).then_inc(S["gates_ready"], 1)

            def body(c2):
                for q in range(2):
                    c = 2 * c2 + q
                    act.wait_ge(S["aT_done"], c + 1)
                    nc.scalar.activation(sigT[:], aT_ps[:], ACT.Sigmoid).then_inc(S["sigT_done"], 1)
                    act.wait_ge(S["a_done"], c + 1)
                    wait(act, S["slope_ready"], c)
                    nc.scalar.activation(sig[:], a_ps[:], ACT.Sigmoid).then_inc(S["sig_done"], 1)
                    act.wait_ge(S["y_done"], c + 1)
                    wait(act, S["ms_ready"], c)
                    for t in range(2):
                        last = nc.scalar.activation(sq_junk[:, 0, t * P:(t + 1) * P], y_ps[:, t], ACT.Square, accum_out=ss[:, 0, t:t + 1])
                    last.then_inc(S["y_squared"], 1)
                    act.wait_ge(S["dyT_done"], c + 1)
                    wait(act, S["dh_done"], c)
                    nc.scalar.copy(dyT[:], dyT_ps[:, 0:2 * P]).then_inc(S["dyT_ready"], 1)
                    act.wait_ge(S["g1_done"], c + 1)
                    wait(act, S["totalled"], c)
                    nc.scalar.activation(sq_junk[:, 1, 0:INNER], g01_ps[:, W1:W1 + INNER], ACT.Square, accum_out=norms[:, 0:1])
                    nc.scalar.activation(sq_junk[:, 1, INNER:INNER + P], g1T_ps[:, INNER:INNER + P], ACT.Square,
                                         accum_out=norms[:, 2:3]).then_inc(S["w1_squared"], 1)
                    act.wait_ge(S["g0_done"], c + 1)
                    nc.scalar.activation(sq_junk[:, 2, 0:INNER], g01_ps[:, W0:W0 + INNER], ACT.Square,
                                         accum_out=norms[:, 1:2]).then_inc(S["w0_squared"], 1)
                    act.wait_ge(S["w0_squared"], c + 1)

            steps(act, body)

        @block.gpsimd
        def _(pool):
            nc.gpsimd.memset(moment[:], 0.0).then_inc(S["state_set"], 1)
            pool.wait_ge(S["state_set"], 1)
            pool.wait_ge(S["gates_final"], 1)
            own = Chain(pool, S["own_p"])
            LINKS = 5

            def feed(c, q):
                nc.gpsimd.tensor_copy(k_s[:, q], k_v[:, c])
                nc.gpsimd.tensor_copy(rate_s[:, q], gate_v[:, 0, c])
                nc.gpsimd.tensor_copy(kT_s[:, q], kT_v[:, c]).then_inc(S["k_ready"], 1)
                own.add(nc.gpsimd.tensor_tensor(kv[:, q], k_v[:, c], v_v[:, c], ALU.subtract))
                own.wait()
                settle(pool, S["idle"])
                nc.gpsimd.tensor_tensor(kv[:, q], kv[:, q], gate_v[:, 0, c].unsqueeze(2).to_broadcast([P, 2, P]),
                                        ALU.mult).then_inc(S["kv_ready"], 1)

            own.at(0)
            feed(0, 0)

            def body(c2):
                for q in range(2):
                    c = 2 * c2 + q
                    last = isinstance(c, int) and c == STEPS - 1
                    own.at(LINKS * c + 1)
                    wait(pool, S["mem_ready"], c)
                    wait(pool, S["moment_ready"], c)
                    settle(pool, S["idle"])
                    own.add(nc.gpsimd.tensor_tensor(moment_faded[:], moment[:], step_v[:, 2, c].to_broadcast([P, END]), ALU.mult))
                    own.add(nc.gpsimd.tensor_tensor(faded[:], mem[:], step_v[:, 1, c].to_broadcast([P, END]), ALU.mult))
                    own.wait()
                    nc.gpsimd.tensor_tensor(faded[:], faded[:], moment_faded[:], ALU.add).then_inc(S["faded_ready"], 1)
                    pool.wait_ge(S["h_ready"], c + 1)
                    own.add(nc.gpsimd.tensor_tensor(slope[:, 1], h[:], sig[:], ALU.mult))
                    own.add(nc.gpsimd.tensor_tensor(slope[:, 0], h[:], sig[:], ALU.add))
                    own.wait()
                    nc.gpsimd.tensor_tensor(slope[:, 0], slope[:, 0], slope[:, 1], ALU.subtract).then_inc(S["slope_ready"], 1)
                    pool.wait_ge(S["ms_ready"], c + 1)
                    nc.gpsimd.tensor_tensor(r[:], ss[:, 1], keep.minus_half[:, 0:2], ALU.pow).then_inc(S["r_ready"], 1)
                    if not last:
                        feed(c + 1, 1 - q)
                        assert own.n == LINKS
                    pool.wait_ge(S["size_ready"], c + 1)
                    nc.gpsimd.tensor_tensor(size[:, 1:2], size[:, 0:1], w["half"][:, 0:1], ALU.pow).then_inc(S["rooted"], 1)

            steps(pool, body)

        @block.vector
        def _(dve):
            dve.wait_ge(S["dots_summed"], 1)
            nc.vector.tensor_copy(term_sums[:], total_ps[:, 0:3 * ALL_TILES].rearrange("p (d t) -> p d t", d=3)).then_inc(S["sums_copied"], 1)
            dve.wait_ge(S["sums_copied"], 1)
            both = term_sums[:, 1:3].rearrange("p d (c t) -> p d c t", t=2)
            nc.vector.tensor_tensor(pair_sum[:], both[:, :, :, 0], both[:, :, :, 1], ALU.add).then_inc(S["pairs_summed"], 1)
            dve.wait_ge(S["gates_ready"], 1)
            nc.vector.tensor_scalar_mul(gates[:, 0], gates[:, 0], 2.0 * BASE_RATE / (CHUNK_TOKENS * P))
            nc.vector.tensor_scalar(gates[:, 1, 0:STEPS], gates[:, 1, 0:STEPS], -1.0, 1.0, ALU.mult,
                                    ALU.add).then_inc(S["gates_final"], 1)

            def body(c2):
                for q in range(2):
                    c = 2 * c2 + q
                    dve.wait_ge(S["sigT_done"], c + 1)
                    nc.vector.tensor_tensor(hT[:], aT_ps[:], sigT[:], ALU.mult).then_inc(S["hT_ready"], 1)
                    dve.wait_ge(S["sig_done"], c + 1)
                    nc.vector.tensor_tensor(h[:], a_ps[:], sig[:], ALU.mult).then_inc(S["h_ready"], 1)
                    dve.wait_ge(S["y_squared"], c + 1)
                    nc.vector.tensor_scalar(ss[:, 1], ss[:, 0], 1.0 / P, RMS_EPS, ALU.mult, ALU.add).then_inc(S["ms_ready"], 1)
                    dve.wait_ge(S["r_ready"], c + 1)
                    nc.vector.tensor_tensor(yr[:], y_ps[:, 0:2], r[:].unsqueeze(2).to_broadcast([P, 2, P]), ALU.mult).then_inc(S["yr_ready"], 1)
                    dve.wait_ge(S["yr_ready"], c + 1)
                    nc.vector.tensor_tensor(yg[:], yr[:], gain_b(), ALU.mult).then_inc(S["yg_ready"], 1)
                    dve.wait_ge(S["yg_ready"], c + 1)
                    dve.wait_ge(S["kv_ready"], c + 1)
                    for t in range(2):
                        last = nc.vector.scalar_tensor_tensor(G[:, t], yg[:, t], rate_s[:, q, t:t + 1], kv[:, q, t], ALU.mult, ALU.add)
                    last.then_inc(S["G_ready"], 1)
                    dve.wait_ge(S["G_ready"], c + 1)
                    nc.vector.tensor_tensor(D[:], G[:], gain_b(), ALU.mult).then_inc(S["D_ready"], 1)
                    dve.wait_ge(S["D_ready"], c + 1)
                    for t in range(2):
                        last = nc.vector.tensor_tensor_reduce(out=Dy_junk[:, t], in0=D[:, t], in1=yr[:, t], scale=1.0, scalar=0.0,
                                                              op0=ALU.mult, op1=ALU.add, accum_out=Dy[:, 0, t:t + 1])
                    last.then_inc(S["Dy_ready"], 1)
                    dve.wait_ge(S["Dy_ready"], c + 1)
                    nc.vector.tensor_scalar_mul(Dy[:, 1], Dy[:, 0], -1.0 / P).then_inc(S["c1_ready"], 1)
                    dve.wait_ge(S["c1_ready"], c + 1)
                    for t in range(2):
                        last = nc.vector.scalar_tensor_tensor(inner[:, t], yr[:, t], Dy[:, 1, t:t + 1], D[:, t], ALU.mult, ALU.add)
                    last.then_inc(S["inner_ready"], 1)
                    dve.wait_ge(S["inner_ready"], c + 1)
                    nc.vector.tensor_tensor(dy[:], inner[:], r[:].unsqueeze(2).to_broadcast([P, 2, P]), ALU.mult).then_inc(S["dy_ready"], 1)
                    nc.vector.tensor_tensor(Gy[:], G[:], yr[:], ALU.mult).then_inc(S["Gy_ready"], 1)
                    dve.wait_ge(S["dh_done"], c + 1)
                    dve.wait_ge(S["slope_ready"], c + 1)
                    nc.vector.tensor_tensor(da[:], dh_ps[:], slope[:, 0], ALU.mult).then_inc(S["da_ready"], 1)
                    dve.wait_ge(S["totalled"], c + 1)
                    nc.vector.tensor_copy(size[:, 0:1], total_ps[:, 0:1]).then_inc(S["size_ready"], 1)
                    dve.wait_ge(S["rooted"], c + 1)
                    nc.vector.tensor_scalar_add(size[:, 2:3], size[:, 1:2], 1e-6).then_inc(S["size_eps"], 1)
                    dve.wait_ge(S["size_eps"], c + 1)
                    nc.vector.reciprocal(size[:, 3:4], size[:, 2:3]).then_inc(S["size_inv"], 1)
                    dve.wait_ge(S["size_inv"], c + 1)
                    nc.vector.tensor_scalar(clip[:], size[:, 3:4], 1.0, -1.0, ALU.min, ALU.mult).then_inc(S["clip_ready"], 1)
                    dve.wait_ge(S["clip_ready"], c + 1)
                    dve.wait_ge(S["faded_ready"], c + 1)
                    for dst, base, sig_ in ((mem, faded, "mem_ready"), (moment, moment_faded, "moment_ready")):
                        nc.vector.scalar_tensor_tensor(dst[:, 0:W1T], g01_ps[:], clip[:], base[:, 0:W1T], ALU.mult, ALU.add)
                        nc.vector.scalar_tensor_tensor(dst[:, W1T:END], g1T_ps[:, 0:INNER + P], clip[:], base[:, W1T:END],
                                                       ALU.mult, ALU.add).then_inc(S[sig_], 1)

            steps(dve, body)


def memory_read_stage(nc, keep, w):
    W0, W1T, GAIN, END = 0, 2 * INNER, 3 * INNER, 3 * INNER + P
    mem = keep.mem
    with ExitStack() as stack:
        m = Memory(nc, stack, "mr_")
        norm = Norm(nc, keep, m, "n2", w["ident"][:])
        hT = m.sb("hT2", [P, 2, HALVES_IN, GROUP])
        xq = m.sb("xq", [P, 2, TILES, P])
        yr = m.sb("yr2", [P, 2, TILES, P])
        yg = m.sb("yg2", [P, TILES, P])
        junk = m.sb("sq_junk2", [P, GROUP])
        ss = m.sb("ss2", [P, 2, TILES])
        r = m.sb("r2", [P, TILES])
        a_ps = [m.ps(f"a2_ps{n}", [P, GROUP]) for n in range(4)]
        y_ps = [m.ps(f"y2_ps{n}", [P, GROUP]) for n in range(2)]
        a_done, h_ready, y_done, squared = m.sem("a2_done"), m.sem("h2_ready"), m.sem("y2_done"), m.sem("y2_sq")
        ms_ready, r_ready, yr_ready, xq_ready = m.sem("ms2"), m.sem("r2_ready"), m.sem("yr2_ready"), m.sem("xq_ready")
        yg_ready, x_ready, stats_done = m.sem("yg2_ready"), m.sem("x3_ready"), m.sem("st3_done")
        idle = m.sem("idle_read")
        qT_v = keep.qT[:].rearrange("p (g n) -> p g n", n=GROUP)
        q_v = keep.q[:].rearrange("p (g t) e -> p g t e", t=TILES)
        block = stack.enter_context(nc.Block())

        @block.tensor
        def _(pe):
            def read_out(g, q):
                pe.wait_ge(h_ready, g + 1)
                wait(pe, yr_ready, g - 1)
                for t in range(TILES):
                    for i in range(2):
                        mm = nc.tensor.matmul(y_ps[q][:, t * P:(t + 1) * P], hT[:, q, i, t * P:(t + 1) * P],
                                              mem[:, W1T + i * P:W1T + (i + 1) * P], start=(i == 0), stop=(i == 1))
                mm.then_inc(y_done, 1)

            def body(g2):
                for q in range(2):
                    g = 2 * g2 + q
                    wait(pe, h_ready, g - 1)
                    for i in range(2):
                        mm = nc.tensor.matmul(a_ps[2 * q + i][:], mem[:, W0 + i * P:W0 + (i + 1) * P], qT_v[:, g], start=True, stop=True)
                    mm.then_inc(a_done, 1)
                    if not (isinstance(g, int) and g == 0):
                        read_out(g - 1, 1 - q)

            pairs(pe, body)
            read_out(GROUPS - 1, 1)

            def turns(g2):
                for q in range(2):
                    norm.turn(pe, 2 * g2 + q, q)

            pairs(pe, turns)

        @block.scalar
        def _(act):
            def square(g, q):
                act.wait_ge(y_done, g + 1)
                wait(act, ms_ready, g)
                for t in range(TILES):
                    last = nc.scalar.activation(junk[:, t * P:(t + 1) * P], y_ps[q][:, t * P:(t + 1) * P], ACT.Square,
                                                accum_out=ss[:, 0, t:t + 1])
                last.then_inc(squared, 1)

            def body(g2):
                for q in range(2):
                    g = 2 * g2 + q
                    act.wait_ge(a_done, g + 1)
                    wait(act, y_done, g - 1)
                    for i in range(2):
                        last = nc.scalar.activation(hT[:, q, i], a_ps[2 * q + i][:], ACT.Silu)
                    last.then_inc(h_ready, 1)
                    if not (isinstance(g, int) and g == 0):
                        square(g - 1, 1 - q)

            pairs(act, body)
            square(GROUPS - 1, 1)

            def copies(g2):
                for q in range(2):
                    norm.copy(act, 2 * g2 + q, q)

            pairs(act, copies)

        @block.gpsimd
        def _(pool):
            def body(g2):
                for q in range(2):
                    g = 2 * g2 + q
                    nc.gpsimd.tensor_tensor(xq[:, q], norm.x_v[:, g], q_v[:, g], ALU.add).then_inc(xq_ready, 1)
                    pool.wait_ge(ms_ready, g + 1)
                    nc.gpsimd.tensor_tensor(r[:], ss[:, 1], keep.minus_half[:, 0:TILES], ALU.pow).then_inc(r_ready, 1)
                    pool.wait_ge(yr_ready, g + 1)
                    nc.gpsimd.tensor_tensor(yg[:], yr[:, q], mem[:, GAIN:END].unsqueeze(1).to_broadcast([P, TILES, P]),
                                            ALU.mult).then_inc(yg_ready, 1)
                    pool.wait_ge(yg_ready, g + 1)
                    settle(pool, idle)
                    nc.gpsimd.tensor_tensor(norm.x_v[:, g], yg[:], xq[:, q], ALU.add).then_inc(x_ready, 1)
                    pool.wait_ge(x_ready, g + 1)
                    settle(pool, idle)

            pairs(pool, body)
            norm.root(pool)

        @block.vector
        def _(dve):
            def statistics(g):
                dve.wait_ge(x_ready, g + 1)
                norm.take_stats(g).then_inc(stats_done, 1)

            def body(g2):
                for q in range(2):
                    g = 2 * g2 + q
                    dve.wait_ge(squared, g + 1)
                    nc.vector.tensor_scalar(ss[:, 1], ss[:, 0], 1.0 / P, RMS_EPS, ALU.mult, ALU.add).then_inc(ms_ready, 1)
                    dve.wait_ge(r_ready, g + 1)
                    nc.vector.tensor_tensor(yr[:, q], y_ps[q][:].rearrange("p (t e) -> p t e", t=TILES),
                                            r[:].unsqueeze(2).to_broadcast([P, TILES, P]), ALU.mult).then_inc(yr_ready, 1)
                    if not (isinstance(g, int) and g == 0):
                        statistics(g - 1)

            pairs(dve, body)
            statistics(GROUPS - 1)
            dve.wait_ge(stats_done, GROUPS)
            norm.finish(dve)
            dve.wait_ge(norm.rstd_ready, 1)

            def scales(g2):
                for q in range(2):
                    norm.scale(dve, 2 * g2 + q, q)

            pairs(dve, scales)


class Keep:
    pass


def build(nc, io, out, debug=None):
    with ExitStack() as stack:
        m = Memory(nc, stack)
        keep = Keep()
        keep.started, keep.weights = m.sem("started"), m.sem("weights")
        keep.parts_stored = [m.sem("parts_stored0"), m.sem("parts_stored1")]
        keep.minus_half = m.sb("minus_half", [P, ALL_TILES])
        io["parts"] = nc.dram_tensor("qk_parts", [2, BATCH, 3, P, SEQ], BF16, kind="Internal").ap()
        w = {"loads": []}

        def load(memory, *names):
            for name in names:
                src = io[name]
                tile = memory.sb("w_" + name, list(src.shape), src.dtype)
                w["loads"].append((tile[:], src))
                w[name] = tile

        load(m, "ident", "wo", "bo", "router0", "indices", "ffn0_gate", "ffn0_up", "ffn0_down", "ffn0_spread",
             "gate_rows", "qk_norm", "qkv1", "ones", "block_ones", "mean_ones", "half", "memory",
             "router1", "router1_bias", "ffn1_gate", "ffn1_up", "ffn1_down", "ffn1_spread")
        keep.mem = w["memory"]

        keep.x = m.sb("x", [P, ALL_TILES, P])
        keep.xT = keep.comb3 = None

        def routed_input(memory, n):
            keep.xT = memory.sb(f"xT_{n}", [P, ALL_TILES * P])
            keep.comb3 = memory.sb(f"comb3_{n}", [COMB_ROWS, ALL_TILES * P], BF16)

        with ExitStack() as attention:
            keep.attn = Memory(nc, attention).sb("attn", [P, BATCH, KEY_TILES, P])
            with ExitStack() as first:
                f = Memory(nc, first)
                load(f, "ident_bf", "future_bf", "causal", "cos", "sin", "wqk", "qk_bias", "wkv", "bkv", "wv")
                keep.V = f.sb("V", [P, BATCH, HEAD_GROUPS, KEY_TILES, V_COLS])
                project_stage(nc, keep, w, io)
                attention_stage(nc, keep, w, io)
            routed_input(Memory(nc, attention), 0)
            output_projection_stage(nc, keep, w, io)
            route_stage(nc, keep, w, w["router0"], 2)
            expert_stage(nc, keep, w, "ffn0", 4, P)
        keep.xT = None
        with ExitStack() as memory:
            f = Memory(nc, memory)
            keep.q = f.sb("q1", [P, ALL_TILES, P])
            keep.qT = f.sb("qT1", [P, ALL_TILES * P])
            with ExitStack() as scan:
                f = Memory(nc, scan)
                keep.k = f.sb("k1", [P, ALL_TILES, P])
                keep.kT = f.sb("kT1", [P, ALL_TILES * P])
                keep.v = f.sb("v1", [P, ALL_TILES, P])
                keep.dots = f.sb("dots", [P, 3, ALL_TILES])
                memory_inputs_stage(nc, keep, w)
                recurrence_stage(nc, keep, w)
            routed_input(Memory(nc, memory), 1)
            memory_read_stage(nc, keep, w)
            route_stage(nc, keep, w, w["router1"], 4, w["router1_bias"], 2.5)
            expert_stage(nc, keep, w, "ffn1", 8, P, store=out)



_L0 = "L0_attn_"
_L1 = "L1_attn_"


def laid_out(inputs):
    import numpy as np

    a = {n: np.asarray(v) for n, v in inputs.items()}
    f32, bf = np.float32, mybir.dt.np(BF16)
    half = P // 2
    by_element = np.arange(P).reshape(HEADS, HEAD_DIM).T.ravel()
    swapped = np.roll(np.arange(P), -half)[by_element]
    inverse = 1.0 / 10000.0 ** (np.arange(0, P, 2, dtype=f32) / P)
    angle = (np.arange(SEQ, dtype=f32)[:, None] * inverse.astype(f32)[None, :]).T
    cos, sin = np.cos(angle).astype(f32), np.sin(angle).astype(f32)
    tile_rows = lambda v, n: np.broadcast_to(v, (n, *v.shape))
    q, k = np.arange(P)[:, None], np.arange(P)[None, :]
    pair = lambda e, rows, cols: e.reshape(-1, rows, *e.shape[1:])

    def spread(chunks, per):
        s = np.zeros((COMB_ROWS, chunks, P), bf)
        for c in range(chunks):
            for row in range(P):
                for part in range(3):
                    s[32 * part + c * per + row // (P // per), c, row] = 1
        return s

    def by_chunk(e, per):
        n, d, mid = e.shape
        return e.reshape(n // per, per, d, mid).transpose(2, 0, 1, 3).reshape(d, n // per, per * mid)

    def down(e, per):
        n, mid, d = e.shape
        return e.reshape(n // per, per * mid, d).transpose(1, 0, 2)

    def with_shared(routed, shared):
        out = np.zeros((P, routed.shape[1] + 1, P), f32)
        out[:, :-1] = routed
        out[:shared.shape[0], -1, :shared.shape[1]] = shared
        return out

    w13, w2 = a["L1_ffn_w13"], a["L1_ffn_w2"]
    mid1 = w13.shape[1] // 2
    gate1, up1 = w13[:, :mid1].transpose(0, 2, 1), w13[:, mid1:].transpose(0, 2, 1)
    gates = np.concatenate([a[_L1 + n + "_w"].reshape(1, CHUNK_LEN, P) for n in ("theta", "alpha", "eta")])
    return {
        "x": a[_L0 + "x"],
        "ident": np.eye(P, dtype=f32), "ident_bf": np.eye(P).astype(bf),
        "future_bf": np.where(k < q, NEG, 0).astype(bf),
        "causal": np.concatenate([np.zeros((P, SEQ - P)), np.where(k > q, NEG, 0)], 1).astype(f32),
        "cos": np.concatenate([cos, cos])[by_element],
        "sin": np.concatenate([-sin, sin])[by_element],
        "wqk": np.stack([a[_L0 + n][:, cols] for n in ("wqr", "wkr") for cols in (by_element, swapped)], 1),
        "qk_bias": np.stack([a[_L0 + n][rows] for n in ("bqr", "bkr") for rows in (by_element, swapped)], 1),
        "wkv": a[_L0 + "wkv"], "bkv": a[_L0 + "bkv"][:, None],
        "wv": np.concatenate([a[_L0 + "wv"], a[_L0 + "bv"][None]]),
        "wo": a[_L0 + "wo"], "bo": tile_rows(a[_L0 + "bo"], P),
        "router0": a["L0_ffn_router_w"],
        "indices": tile_rows(np.arange(EXPERTS, dtype=f32), P),
        "ffn0_gate": with_shared(by_chunk(a["L0_ffn_wg_r"], 4), by_chunk(a["L0_ffn_wg_s"], 2)[:, 0]),
        "ffn0_up": with_shared(by_chunk(a["L0_ffn_wu_r"], 4), by_chunk(a["L0_ffn_wu_s"], 2)[:, 0]),
        "ffn0_down": with_shared(down(a["L0_ffn_wd_r"], 4), down(a["L0_ffn_wd_s"], 2)[:, 0]),
        "ffn0_spread": spread(4, 4),
        "gate_rows": np.concatenate([gates, gates], 1).transpose(1, 0, 2),
        "qk_norm": tile_rows(np.stack([a[_L1 + "q_norm_w"], a[_L1 + "k_norm_w"]]), P),
        "qkv1": np.stack([a[_L1 + n].T for n in ("wq_w", "wk_w", "wv_w")], 1),
        "ones": np.ones((P, P), f32),
        "block_ones": np.kron(np.eye(2), np.ones((half, half))).astype(f32),
        "mean_ones": np.full((P, P), 1.0 / P, f32),
        "half": np.full((P, 1), 0.5, f32),
        "memory": np.concatenate([a[_L1 + "mem_w0"].T, a[_L1 + "mem_w1"],
                                  a[_L1 + "mem_w1"].T.reshape(2, P, P).transpose(1, 0, 2).reshape(P, 2 * P),
                                  tile_rows(a[_L1 + "mem_ln_w"], P)], 1),
        "router1": a["L1_ffn_gate_w"].T,
        "router1_bias": tile_rows(a["L1_ffn_gate_b"], P),
        "ffn1_gate": with_shared(by_chunk(gate1, 2), a["L1_ffn_w13_s"][:mid1].T),
        "ffn1_up": with_shared(by_chunk(up1, 2), a["L1_ffn_w13_s"][mid1:].T),
        "ffn1_down": with_shared(down(w2.transpose(0, 2, 1), 2), a["L1_ffn_w2_s"].T),
        "ffn1_spread": spread(8, 2),
    }


def kernel(**inputs):
    import numpy as np
    from concourse import bacc
    from concourse.bass_utils import run_bass_kernel_spmd

    nc = bacc.Bacc("TRN2", target_bir_lowering=False, num_devices=1)
    arrays, io = {}, {}
    for name, array in laid_out(inputs).items():
        array = np.ascontiguousarray(array)
        arrays["in_" + name] = array
        io[name] = nc.dram_tensor("in_" + name, list(array.shape), mybir.dt.from_np(array.dtype), kind="ExternalInput").ap()
    out = nc.dram_tensor("out", [BATCH, SEQ, P], FP32, kind="ExternalOutput").ap()
    build(nc, io, out)
    result = run_bass_kernel_spmd(nc, [arrays], core_ids=[0])
    return result.results[0]["out"]
```

```python
from contextlib import ExitStack

import concourse.bass as bass
from concourse import mybir

FP32 = mybir.dt.float32
BF16 = mybir.dt.bfloat16
ACT = mybir.ActivationFunctionType
ALU = mybir.AluOpType

P = 128
BATCH, SEQ = 4, 1024
HEADS, HEAD_DIM = 16, 8
HEAD_GROUP = 4
HEAD_GROUPS = HEADS // HEAD_GROUP
LATENT = 32
GROUP = 512
TILES = GROUP // P
GROUPS = BATCH * SEQ // GROUP
KEY_TILES = SEQ // P
HALVES = SEQ // GROUP
V_COLS = HEAD_GROUP * (HEAD_DIM + 1)
V_SLOT = V_COLS + 32
LN_EPS = 1e-5
NEG = -1.0e30


def wait(engine, semaphore, value):
    if isinstance(value, int) and value <= 0:
        return
    engine.wait_ge(semaphore, value)


def settle(engine, idle):
    engine.sem_inc(idle, 1)


class Chain:

    def __init__(self, engine, semaphore):
        self.engine, self.semaphore, self.base, self.n = engine, semaphore, 0, 0

    def at(self, base):
        self.base, self.n = base, 0

    def add(self, instruction):
        instruction.then_inc(self.semaphore, 1)
        self.n += 1
        return self.base + self.n

    def wait(self, value=None):
        self.engine.wait_ge(self.semaphore, self.base + self.n if value is None else value)


class Memory:

    def __init__(self, nc, stack, prefix=""):
        self.nc, self.stack, self.prefix = nc, stack, prefix
        self.semaphores = []

    def sb(self, name, shape, dtype=FP32):
        return self.stack.enter_context(self.nc.sbuf_tensor(self.prefix + name, shape, dtype))

    def ps(self, name, shape, dtype=FP32):
        return self.stack.enter_context(self.nc.psum_tensor(self.prefix + name, shape, dtype))

    def sem(self, name):
        if not self.semaphores:
            self.stack.callback(self.release)
        self.semaphores.append(self.nc.alloc_semaphore(self.prefix + name))
        return self.semaphores[-1]

    def release(self):
        self.nc.clear_and_free_semaphores(self.semaphores)
        self.nc.all_engine_barrier()


def project_stage(nc, keep, w, io):
    with ExitStack() as stack:
        m = Memory(nc, stack, "in_")
        norm = Norm(nc, keep, m, "n_in", w["ident"][:])
        xnT = m.sb("xnT", [P, 2, GROUP])
        straight = m.sb("rope_straight", [P, 2, 2, GROUP])
        crossed = m.sb("rope_crossed", [P, 2, 2, GROUP])
        roped = m.sb("roped", [P, 2, GROUP])
        qk = m.sb("qk_gelu", [P, 2, GROUP])
        rest = m.sb("qk_rest", [P, 2, GROUP])
        parts = m.sb("qk_parts_sb", [P, 2, 2, 3, GROUP], BF16)
        latent = m.sb("latent", [LATENT + 1, 2, GROUP])
        proj_ps = [m.ps(f"proj_ps{n}", [P, GROUP]) for n in range(4)]
        lat_ps = m.ps("lat_ps", [P, GROUP])
        v_ps = m.ps("v_ps", [P, GROUP])

        x_loaded = [m.sem(f"x_loaded{n}") for n in range(GROUPS)]
        projected, stats_done = m.sem("projected"), m.sem("stats_done_in")
        lat_done, lat_ready, v_done, v_kept = m.sem("lat_done"), m.sem("lat_ready"), m.sem("v_done"), m.sem("v_kept")
        rotated, summed, gelu_done = m.sem("rotated"), m.sem("summed"), m.sem("gelu_done")
        hi_done, rest_done, mid_done, lo_done = m.sem("hi_done"), m.sem("rest_done"), m.sem("mid_done"), m.sem("lo_done")
        latent_ones, v_ones = m.sem("latent_ones"), m.sem("v_ones")
        stored = keep.parts_stored

        x_v = io["x"].rearrange("b (h t p) e -> (b h) p t e", h=HALVES, p=P)
        parts_v = io["parts"].rearrange("k b a r s -> k b r a s")
        V_v = keep.V[:].rearrange("p b h j (g c) -> p b h j g c", c=HEAD_DIM + 1)

        block = stack.enter_context(nc.Block())

        def batches(engine, body):
            body(0, False)
            with engine.Fori(1, BATCH - 1) as b:
                body(b, False)
            body(BATCH - 1, True)

        @block.sync
        def _(sp):
            def store(g, b, half):
                sp.wait_ge(lo_done, g + 1)
                sp.wait_ge(mid_done, g + 1)
                sp.wait_ge(hi_done, g + 1)
                for k in range(2):
                    sp.dma_start(parts_v[k, b][:, :, half * GROUP:(half + 1) * GROUP],
                                 parts[:, half, k]).then_inc(stored[half], 16)

            for g in range(GROUPS):
                sp.dma_start(norm.x_v[:, g], x_v[g]).then_inc(x_loaded[g], 16)
            for dst, src in w["first_loads"]:
                sp.dma_start(dst, src).then_inc(keep.first_weights, 16)

            def body(b, last):
                for half in range(HALVES):
                    g = 2 * b + half
                    if half == 1:
                        store(g - 1, b, 0)
                    elif not (isinstance(b, int) and b == 0):
                        store(g - 1, b - 1, 1)

            batches(sp, body)
            store(HALVES * BATCH - 1, BATCH - 1, 1)
            for half in range(HALVES):
                sp.wait_ge(stored[half], 32 * BATCH)

        @block.vector
        def _(dve):
            def rotate(g, half):
                wait(dve, summed, g - 1)
                cols = slice(half * GROUP, (half + 1) * GROUP)
                for k in range(2):
                    dve.wait_ge(projected, 2 * g + k + 1)
                    nc.vector.scalar_tensor_tensor(straight[:, half, k], proj_ps[2 * k][:], w["qk_bias"][:, 2 * k:2 * k + 1],
                                                   w["cos"][:, cols], ALU.add, ALU.mult)
                    nc.vector.scalar_tensor_tensor(crossed[:, half, k], proj_ps[2 * k + 1][:],
                                                   w["qk_bias"][:, 2 * k + 1:2 * k + 2],
                                                   w["sin"][:, cols], ALU.add, ALU.mult).then_inc(rotated, 1)

            def low_part(g, b, half):
                dve.wait_ge(mid_done, g + 1)
                wait(dve, stored[half], 32 * b)
                nc.vector.tensor_tensor(parts[:, half, :, 2], rest[:], parts[:, half, :, 1],
                                        ALU.subtract).then_inc(lo_done, 1)

            nc.vector.memset(latent[LATENT:LATENT + 1], 1.0).then_inc(latent_ones, 1)
            for g in range(GROUPS):
                dve.wait_ge(x_loaded[g], 16)
                last = norm.take_stats(g)
            last.then_inc(stats_done, 1)
            dve.wait_ge(stats_done, 1)
            norm.finish(dve)
            dve.wait_ge(norm.rstd_ready, 1)
            norm.scale(dve, 0, 0)
            norm.scale(dve, 1, 1)
            dve.wait_ge(keep.first_weights, 16 * len(w["first_loads"]))

            def body(b, last):
                for half in range(HALVES):
                    g = 2 * b + half
                    if not last:
                        norm.scale(dve, g + 2, half)
                    rotate(g, half)
                    if half == 1:
                        low_part(g - 1, b, 0)
                    elif not (isinstance(b, int) and b == 0):
                        low_part(g - 1, b - 1, 1)

            batches(dve, body)
            low_part(HALVES * BATCH - 1, BATCH - 1, 1)

        @block.gpsimd
        def _(pool):
            nc.gpsimd.memset(keep.minus_half[:], -0.5).then_inc(keep.started, 1)
            pool.wait_ge(keep.started, 1)
            norm.root(pool)
            nc.gpsimd.memset(keep.V[:], 1.0).then_inc(v_ones, 1)

            def body(b, last):
                for half in range(HALVES):
                    g = 2 * b + half
                    pool.wait_ge(rotated, 2 * g + 2)
                    wait(pool, gelu_done, g)
                    nc.gpsimd.tensor_tensor(roped[:], straight[:, half], crossed[:, half],
                                            ALU.add).then_inc(summed, 1)
                    pool.wait_ge(hi_done, g + 1)
                    wait(pool, lo_done, g)
                    nc.gpsimd.tensor_tensor(rest[:], qk[:], parts[:, half, :, 0],
                                            ALU.subtract).then_inc(rest_done, 1)

            batches(pool, body)

        @block.scalar
        def _(act):
            act.wait_ge(latent_ones, 1)

            def keep_xT(g, half):
                act.wait_ge(norm.turned, g + 1)
                wait(act, projected, 2 * (g - 1))
                nc.scalar.copy(xnT[:, half], norm.turn_ps[half][:]).then_inc(norm.copied, 1)

            def middle(g, half):
                act.wait_ge(rest_done, g + 1)
                nc.scalar.copy(parts[:, half, :, 1], rest[:]).then_inc(mid_done, 1)

            keep_xT(0, 0)
            act.wait_ge(v_ones, 1)

            def body(b, last):
                for half in range(HALVES):
                    g = 2 * b + half
                    act.wait_ge(lat_done, g + 1)
                    wait(act, v_done, g - 1)
                    nc.scalar.activation(latent[0:LATENT, half], lat_ps[0:LATENT, :], ACT.Gelu,
                                         bias=w["bkv"][:, 0:1]).then_inc(lat_ready, 1)
                    if not (last and half == 1):
                        keep_xT(g + 1, 1 - half)
                    if not (isinstance(g, int) and g == 0):
                        middle(g - 1, 1 - half)
                    act.wait_ge(v_done, g + 1)
                    src = v_ps[:].rearrange("p (t h g d) -> p t h g d", t=TILES, h=HEAD_GROUPS, g=HEAD_GROUP)
                    for h in range(HEAD_GROUPS):
                        last_copy = nc.scalar.copy(V_v[:, b, h, half * TILES:(half + 1) * TILES, :, 0:HEAD_DIM], src[:, :, h])
                    last_copy.then_inc(v_kept, 1)
                    act.wait_ge(summed, g + 1)
                    wait(act, rest_done, g)
                    nc.scalar.activation(qk[:], roped[:], ACT.Gelu).then_inc(gelu_done, 1)
                    act.wait_ge(gelu_done, g + 1)
                    wait(act, stored[half], 32 * b)
                    nc.scalar.copy(parts[:, half, :, 0], qk[:]).then_inc(hi_done, 1)

            batches(act, body)
            middle(HALVES * BATCH - 1, 1)

        @block.tensor
        def _(pe):
            pe.wait_ge(keep.first_weights, 16 * len(w["first_loads"]))

            norm.turn(pe, 0, 0)

            def body(b, last):
                for half in range(HALVES):
                    g = 2 * b + half
                    pe.wait_ge(norm.copied, g + 1)
                    wait(pe, lat_ready, g)
                    nc.tensor.matmul(lat_ps[0:LATENT, :], w["wkv"][:], xnT[:, half], start=True,
                                     stop=True).then_inc(lat_done, 1)
                    if not (last and half == 1):
                        norm.turn(pe, g + 1, 1 - half)
                    for k in range(2):
                        wait(pe, rotated, 2 * (g - 1) + k + 1)
                        for n in range(2):
                            mm = nc.tensor.matmul(proj_ps[2 * k + n][:], w["wqk"][:, 2 * k + n], xnT[:, half], start=True, stop=True)
                        mm.then_inc(projected, 1)
                        if k == 0:
                            pe.wait_ge(lat_ready, g + 1)
                            wait(pe, v_kept, g)
                            for t in range(TILES):
                                mm = nc.tensor.matmul(v_ps[:, t * P:(t + 1) * P], latent[:, half, t * P:(t + 1) * P],
                                                      w["wv"][:], start=True, stop=True)
                            mm.then_inc(v_done, 1)

            batches(pe, body)


def attention_schedule():
    tasks = []
    halves = [[("max", g, i) for i in range(KEY_TILES // 2) for g in range(HEAD_GROUP)],
              [("max", g, i) for i in range(KEY_TILES // 2, KEY_TILES) for g in range(HEAD_GROUP)]]
    tasks += halves[0][:9] + [("out", 1)] + halves[0][9:] + halves[1][:2] + [("rows", 0)] + halves[1][2:8] + [("out", 0)] + halves[1][8:] + [("rows", 1)]
    cost = lambda t: {"out": 900, "rows": 250}.get(t[0]) or 190 + (t[2] + 1) * P
    width = lambda half, j: GROUP - max(0, j * P - half * GROUP)
    chunk_ends, passed = [], 0
    for half in range(HALVES):
        for j in range((half + 1) * TILES):
            for _ in range(HEAD_GROUP):
                passed += 60 + width(half, j)
                chunk_ends.append(passed)
    total, spent, places = sum(map(cost, tasks)), 0, []
    for t in tasks:
        at = spent / total * passed
        places.append(next(n for n, end in enumerate(chunk_ends) if end > at))
        spent += cost(t)
    out0, out1 = tasks.index(("out", 0)), tasks.index(("out", 1))
    places = [p if n < out1 else max(p, 5) if n < out0 else max(p, 20) for n, p in enumerate(places)]
    return tasks, places


ENTRIES = 36
CHUNKS = 48
ROUNDS = CHUNKS // HEAD_GROUP
ROUND_LIST = [(half, j) for half in range(HALVES) for j in range((half + 1) * TILES)]
MAX_ROWS = 72
STACK = MAX_ROWS + 2
LOADS = 13


def attention_stage(nc, keep, w, io):
    tasks, places = attention_schedule()
    assert len(tasks) == ENTRIES
    out0_at, out1_at = tasks.index(("out", 0)), tasks.index(("out", 1))
    LAST_UNIT = HEAD_GROUPS * BATCH - 1
    with ExitStack() as stack:
        m = Memory(nc, stack, "attn_")
        q_stack = m.sb("q_stack", [P, HEAD_GROUPS, HALVES, HEAD_GROUP, GROUP], BF16)
        k_stack = m.sb("k_stack", [P, HEAD_GROUPS, HEAD_GROUP, SEQ], BF16)
        V_slot = m.sb("V_slot", [P, 2, KEY_TILES, V_SLOT])
        probs = m.sb("probs", [P, 2, HEAD_GROUP, GROUP])
        ones = m.sb("ones", [2 * HEAD_GROUPS * HEAD_GROUP * SEQ // GROUP, GROUP], BF16)
        outT = m.sb("outT", [P, 2, GROUP])
        junk = m.sb("junk", [P, 2, SEQ], BF16)
        maxima = m.sb("maxima", [P, 2, HALVES, HEAD_GROUP, TILES])
        max_rows = m.sb("max_rows", [HEAD_GROUP * TILES, HALVES, 2, P], BF16)
        recip = m.sb("recip", [P, 2, TILES, HEAD_GROUP])
        ring = [m.ps(f"ring{n}", [P, 2 * GROUP]) for n in range(2)]
        score_ps = [m.ps(f"score_ps{n}", [P, GROUP]) for n in range(3)]
        out_ps = m.ps("out_ps", [P, GROUP])

        ones_set, ones_loaded = m.sem("ones_set"), m.sem("ones_loaded")
        stack_loaded = [m.sem(f"stack_loaded{n}") for n in range(HEAD_GROUPS)]
        ring_filled, ring_read = m.sem("ring_filled"), m.sem("ring_read")
        rows_loaded = [m.sem("rows_loaded0"), m.sem("rows_loaded1")]
        scored, exp_done, round_done = m.sem("scored"), m.sem("exp_done"), m.sem("round_done")
        out_copied = [m.sem("out_copied0"), m.sem("out_copied1")]
        V_ready, recip_ready, rows_hi = m.sem("V_ready"), m.sem("recip_ready"), m.sem("rows_hi")
        V_pad, idle = m.sem("V_pad"), m.sem("idle_attn")
        attn_v = keep.attn[:].rearrange("p b i (h g d) -> p b i h g d", h=HEAD_GROUPS, g=HEAD_GROUP)

        parts_v = io["parts"].rearrange("k b a (d h) s -> k b (a d) h s", h=HEADS)

        def entry(u, n):
            return ENTRIES * u + 33 + n + shift(u, n)

        def shift(u, n):
            return int(isinstance(u, int) and u == 0 and n < out1_at)

        first_maxima = [t for t in tasks if t[0] != "out"]

        def batches(engine, body):
            body(0)
            with engine.Fori(1, BATCH - 1) as b:
                body(b)
            body(BATCH - 1)

        block = stack.enter_context(nc.Block())

        @block.sync
        def _(sp):
            def load(b, h):
                wait(sp, scored, CHUNKS * (4 * b + h - 3))
                q_src, k_src = (parts_v[k, b][:, HEAD_GROUP * h:HEAD_GROUP * (h + 1), :] for k in range(2))
                for turn in range(3):
                    row = 24 * turn
                    sp.dma_start(k_stack[row:row + 24, h], k_src).then_inc(stack_loaded[h], 16)
                    cut = 8 * turn
                    for half in range(HALVES):
                        cols = slice(half * GROUP, (half + 1) * GROUP)
                        sp.dma_start(q_stack[row:row + 24 - cut, h, half], q_src[cut:24, :, cols]).then_inc(stack_loaded[h], 16)
                        if turn:
                            sp.dma_start(q_stack[row + 24 - cut:row + 24, h, half],
                                         q_src[0:cut, :, cols]).then_inc(stack_loaded[h], 16)

            load(0, 0)
            sp.wait_ge(ones_set, 1)
            sp.dma_start(k_stack[MAX_ROWS:STACK].rearrange("p h g s -> p (h g s)"), ones[:]).then_inc(ones_loaded, 16)
            load(0, 1)

            def put_rows(u, h, half):
                made = entry(u - 1, tasks.index(("rows", half))) + 1
                if isinstance(u, int) and u == 0:
                    made = first_maxima.index(("rows", half)) + 1
                sp.wait_ge(ring_read, made)
                for n in range(2):
                    sp.dma_start(q_stack[MAX_ROWS + n:MAX_ROWS + n + 1, h, half],
                                 max_rows[:, half, n]).then_inc(rows_loaded[half], 16)

            put_rows(0, 0, 0)
            put_rows(0, 0, 1)
            for dst, src in w["loads"]:
                sp.dma_start(dst, src).then_inc(keep.weights, 16)

            def body(b):
                for h in range(HEAD_GROUPS):
                    u = HEAD_GROUPS * b + h
                    final = isinstance(b, int) and b == BATCH - 1
                    if h < 2:
                        load(b, h + 2)
                    elif not final:
                        load(b + 1, h - 2)
                    if not (final and h == 3):
                        put_rows(u + 1, (h + 1) % 4, 0)
                        put_rows(u + 1, (h + 1) % 4, 1)

            batches(sp, body)
            sp.wait_ge(keep.weights, 16 * len(w["loads"]))

        @block.gpsimd
        def _(pool):
            nc.gpsimd.memset(ones[:], 1.0).then_inc(ones_set, 1)
            nc.gpsimd.memset(V_slot[:], 0.0).then_inc(V_pad, 1)
            pool.wait_ge(V_pad, 1)

            def body(b):
                for h in range(HEAD_GROUPS):
                    u = HEAD_GROUPS * b + h
                    wait(pool, round_done, ROUNDS * (u - 1))
                    nc.gpsimd.tensor_copy(V_slot[:, h % 2, :, 0:V_COLS], keep.V[:, b, h]).then_inc(V_ready, 1)

            batches(pool, body)

        @block.scalar
        def _(act):
            def keep_output(u, half):
                act.wait_ge(round_done, ROUNDS * u + (ROUNDS if half else TILES))
                if isinstance(u, int) and u == LAST_UNIT and half:
                    act.wait_ge(ring_filled, entry(u, 0) + 1)
                elif not (isinstance(u, int) and u == 0):
                    act.wait_ge(ring_filled, entry(u, out1_at) + 1 if half else entry(u - 1, out0_at) + 1)
                nc.scalar.copy(outT[:, half], out_ps[:]).then_inc(out_copied[half], 1)

            def body(b):
                for h in range(HEAD_GROUPS):
                    u = HEAD_GROUPS * b + h
                    for r, (half, j) in enumerate(ROUND_LIST):
                        lo = max(0, j * P - half * GROUP)
                        for g in range(HEAD_GROUP):
                            n = r * HEAD_GROUP + g
                            act.wait_ge(scored, CHUNKS * u + n + 1)
                            if g == 0:
                                wait(act, round_done, ROUNDS * u + r - 1)
                            nc.scalar.activation(probs[:, r % 2, g, lo:], score_ps[n % 3][:, lo:], ACT.Exp,
                                                 scale=HEAD_DIM ** -0.5).then_inc(exp_done, 1)
                            if n == 3 and not (isinstance(u, int) and u == 0):
                                keep_output(u - 1, 1)
                            if n == HEAD_GROUP * TILES + 2:
                                keep_output(u, 0)

            batches(act, body)
            keep_output(LAST_UNIT, 1)

        @block.vector
        def _(dve):
            def maximum(G, p, g, i):
                width = (i + 1) * P
                wait(dve, ring_read, G - 1)
                dve.wait_ge(ring_filled, G + 1)
                settle(dve, idle)
                nc.vector.tensor_tensor_reduce(out=junk[:, G0(G) % 2, 0:width], in0=ring[G0(G) % 2][:, 0:width],
                                               in1=w["causal"][:, SEQ - width:SEQ], scale=1.0, scalar=-3.0e38,
                                               op0=ALU.add, op1=ALU.max,
                                               accum_out=maxima[:, p, i // TILES, g, i % TILES:i % TILES + 1]
                                               ).then_inc(ring_read, 1)

            parity = [0]

            def G0(_):
                return parity[0]

            def rows(G, u, half):
                dve.wait_ge(ring_filled, G + 1)
                wait(dve, rows_loaded[half], 32 * u)
                src = ring[G0(G) % 2][0:HEAD_GROUP * TILES, 0:P]
                nc.vector.tensor_scalar_mul(max_rows[:, half, 0], src, -1.0).then_inc(rows_hi, 1)
                dve.wait_ge(rows_hi, 2 * u + half + 1)
                nc.vector.scalar_tensor_tensor(max_rows[:, half, 1], src, -1.0, max_rows[:, half, 0],
                                               ALU.mult, ALU.subtract).then_inc(ring_read, 1)

            def out(G, u, b, h, half):
                dve.wait_ge(ring_filled, G + 1)
                src = ring[G0(G) % 2][:, 0:GROUP].rearrange("p (i g c) -> p i g c", i=TILES, g=HEAD_GROUP)
                nc.vector.reciprocal(recip[:, half], src[:, :, :, HEAD_DIM]).then_inc(recip_ready, 1)
                dve.wait_ge(recip_ready, 2 * u + half + 1)
                nc.vector.tensor_tensor(attn_v[:, b, half * TILES:(half + 1) * TILES, h],
                                        src[:, :, :, 0:HEAD_DIM],
                                        recip[:, half].unsqueeze(3).to_broadcast([P, TILES, HEAD_GROUP, HEAD_DIM]),
                                        ALU.mult).then_inc(ring_read, 1)

            for G, t in enumerate(first_maxima):
                parity[0] = G % 2
                if t[0] == "max":
                    maximum(G, 0, t[1], t[2])
                else:
                    rows(G, 0, t[1])

            def body(b):
                for h in range(HEAD_GROUPS):
                    u = HEAD_GROUPS * b + h
                    final = isinstance(b, int) and b == BATCH - 1 and h == 3
                    for n, t in enumerate(tasks):
                        G = entry(u, n)
                        parity[0] = (33 + n + shift(u, n)) % 2
                        if t[0] == "out" and t[1] == 1:
                            if final:
                                G, parity[0] = entry(u, 0), 33 % 2
                            if not (isinstance(u, int) and u == 0):
                                out(G, u - 1, b if h else b - 1, (h - 1) % 4, 1)
                        elif final and t[0] != "out":
                            continue
                        elif t[0] == "max":
                            maximum(G, (h + 1) % 2, t[1], t[2])
                        elif t[0] == "rows":
                            rows(G, u + 1, t[1])
                        else:
                            G = entry(u, 1) if final else G
                            parity[0] = 34 % 2 if final else parity[0]
                            out(G, u, b, h, 0)
                    if final:
                        parity[0] = 35 % 2
                        out(entry(u, 2), u, b, h, 1)

            batches(dve, body)

        @block.tensor
        def _(pe):
            def maximum(G, p, slot, g, i):
                wait(pe, ring_read, G - 1)
                for c in range(0, (i + 1) * P, GROUP):
                    width = min(GROUP, (i + 1) * P - c)
                    mm = nc.tensor.matmul(ring[p][:, c:c + width], q_stack[0:72, slot, i // TILES, g, i % TILES * P:(i % TILES + 1) * P],
                                          k_stack[0:72, slot, g, c:c + width], start=True, stop=True)
                mm.then_inc(ring_filled, 1)

            def rows(G, p, half, par):
                pe.wait_ge(ring_read, G if half else G - 1)
                nc.tensor.matmul(ring[p][0:HEAD_GROUP * TILES, 0:P],
                                 maxima[:, par, half].rearrange("p g i -> p (g i)"), w["ident"][:],
                                 start=True, stop=True).then_inc(ring_filled, 1)

            def out(G, p, u, half):
                pe.wait_ge(out_copied[half], u + 1)
                wait(pe, ring_read, G - 1)
                for t in range(TILES):
                    mm = nc.tensor.transpose(ring[p][:, t * P:(t + 1) * P], outT[:, half, t * P:(t + 1) * P], w["ident"][:])
                mm.then_inc(ring_filled, 1)

            pe.wait_ge(stack_loaded[0], LOADS * 16)
            for G, t in enumerate(first_maxima):
                if t[0] == "max":
                    maximum(G, G % 2, 0, t[1], t[2])
                else:
                    rows(G, G % 2, t[1], 0)

            pe.wait_ge(ones_loaded, 16)

            def body(b):
                for h in range(HEAD_GROUPS):
                    u = HEAD_GROUPS * b + h
                    final = isinstance(b, int) and b == BATCH - 1 and h == 3

                    def values(r, u=u, slot=h % 2):
                        half, j = ROUND_LIST[r]
                        lo = max(0, j * P - half * GROUP)
                        if r == 0:
                            pe.wait_ge(V_ready, u + 1)
                        if j == 0 and half == 0:
                            wait(pe, out_copied[1], u)
                        elif j == 0:
                            pe.wait_ge(out_copied[0], u + 1)
                        pe.wait_ge(exp_done, CHUNKS * u + HEAD_GROUP * (r + 1))
                        for g in range(HEAD_GROUP):
                            mm = nc.tensor.matmul(out_ps[32 * g:32 * g + 32, lo:],
                                                  V_slot[:, slot, j, g * (HEAD_DIM + 1):g * (HEAD_DIM + 1) + 32],
                                                  probs[:, r % 2, g, lo:], start=(j == 0),
                                                  stop=(j == (half + 1) * TILES - 1))
                        mm.then_inc(round_done, 1)

                    for n in range(CHUNKS):
                        r, g = divmod(n, HEAD_GROUP)
                        half, j = ROUND_LIST[r]
                        lo = max(0, j * P - half * GROUP)
                        diagonal = j >= half * TILES
                        if n == 0:
                            pe.wait_ge(rows_loaded[0], 32 * (u + 1))
                            if not final:
                                if h < 3:
                                    pe.wait_ge(stack_loaded[h + 1], LOADS * 16 * (b + 1))
                                else:
                                    pe.wait_ge(stack_loaded[0], LOADS * 16 * (b + 2))
                        if n == HEAD_GROUP * TILES:
                            pe.wait_ge(rows_loaded[1], 32 * (u + 1))
                        wait(pe, exp_done, CHUNKS * u + n - 2)
                        mm = nc.tensor.matmul(score_ps[n % 3][:, lo:], k_stack[0:STACK, h, g, j * P:(j + 1) * P],
                                              q_stack[0:STACK, h, half, g, lo:],
                                              start=True, stop=not diagonal)
                        if diagonal:
                            mm = nc.tensor.matmul(score_ps[n % 3][:, lo:lo + P], w["ident_bf"][:], w["future_bf"][:],
                                                  start=False, stop=True)
                        mm.then_inc(scored, 1)
                        if g == 1 and r:
                            values(r - 1)
                        elif g == 1 and not (isinstance(u, int) and u == 0):
                            values(ROUNDS - 1, u - 1, (h + 1) % 2)
                        for k, t in enumerate(tasks):
                            if places[k] != n:
                                continue
                            G, p = entry(u, k), (33 + k + shift(u, k)) % 2
                            if t == ("out", 1):
                                if final:
                                    G, p = entry(u, 0), 33 % 2
                                if not (isinstance(u, int) and u == 0):
                                    out(G, p, u - 1, 1)
                            elif final and t[0] != "out":
                                continue
                            elif t[0] == "max":
                                maximum(G, p, (h + 1) % 4, t[1], t[2])
                            elif t[0] == "rows":
                                rows(G, p, t[1], (h + 1) % 2)
                            else:
                                out(entry(u, 1) if final else G, 34 % 2 if final else p, u, 0)
                    if final:
                        values(ROUNDS - 1)
                        out(entry(u, 2), 35 % 2, u, 1)

            batches(pe, body)



CHUNK_LEN = 64
ALL_TILES = BATCH * SEQ // P
EXPERTS = 16
COMB_ROWS = 96


def pairs(engine, body):
    body(0)
    with engine.Fori(1, GROUPS // 2) as g2:
        body(g2)


def pairs_ahead(engine, body):
    body(0)
    with engine.Fori(1, GROUPS // 2 - 1) as g2:
        body(g2)
    body(GROUPS // 2 - 1)


class Norm:

    def __init__(self, nc, keep, m, name, ident):
        self.nc, self.keep, self.ident = nc, keep, ident
        self.stats = m.sb(name + "_stats", [P, ALL_TILES, 6])
        self.work = m.sb(name + "_work", [P, 5, ALL_TILES])
        self.mean, self.rstd = m.sb(name + "_mean", [P, ALL_TILES]), m.sb(name + "_rstd", [P, ALL_TILES])
        self.xn = m.sb(name + "_xn", [P, 2, TILES, P])
        self.turn_ps = [m.ps(f"{name}_turn{n}", [P, GROUP]) for n in range(2)]
        self.var_ready, self.rstd_ready = m.sem(name + "_var"), m.sem(name + "_rstd")
        self.xn_ready, self.turned, self.copied = m.sem(name + "_xn"), m.sem(name + "_turned"), m.sem(name + "_copied")
        self.own_sem = m.sem(name + "_own")
        self.x_v = keep.x[:].rearrange("p (g t) e -> p g t e", t=TILES)
        self.stats_v = self.stats[:].rearrange("p (g t) s -> p g t s", t=TILES)
        self.xT_v = keep.xT and keep.xT[:].rearrange("p (g n) -> p g n", n=GROUP)

    def take_stats(self, g):
        for t in range(TILES):
            last = self.nc.vector.bn_stats(self.stats_v[:, g, t], self.x_v[:, g, t])
        return last

    def finish(self, dve):
        nc, s, work = self.nc, self.stats, self.work
        own = Chain(dve, self.own_sem)
        total, diff, m2, square, var = (work[:, n] for n in range(5))
        nc.vector.tensor_tensor(total, s[:, :, 1], s[:, :, 4], ALU.add)
        nc.vector.tensor_tensor(diff, s[:, :, 1], s[:, :, 4], ALU.subtract)
        own.add(nc.vector.tensor_tensor(m2, s[:, :, 2], s[:, :, 5], ALU.add))
        own.wait()
        nc.vector.tensor_scalar_mul(self.mean[:], total, 0.5)
        own.add(nc.vector.scalar_tensor_tensor(square, diff, 0.25, diff, ALU.mult, ALU.mult))
        own.wait()
        own.add(nc.vector.scalar_tensor_tensor(var, m2, 1.0 / P, square, ALU.mult, ALU.add))
        own.wait()
        nc.vector.tensor_scalar_add(total, var, LN_EPS).then_inc(self.var_ready, 1)

    def root(self, pool):
        pool.wait_ge(self.var_ready, 1)
        self.nc.gpsimd.tensor_tensor(self.rstd[:], self.work[:, 0], self.keep.minus_half[:], ALU.pow).then_inc(self.rstd_ready, 1)

    def scale(self, dve, g, q):
        wait(dve, self.turned, g - 1)
        for t in range(TILES):
            last = self.nc.vector.tensor_scalar(self.xn[:, q, t], self.x_v[:, g, t],
                                                self.mean[:].rearrange("p (g t) -> p g t", t=TILES)[:, g, t:t + 1],
                                                self.rstd[:].rearrange("p (g t) -> p g t", t=TILES)[:, g, t:t + 1],
                                                ALU.subtract, ALU.mult)
        last.then_inc(self.xn_ready, 1)

    def turn(self, pe, g, q):
        pe.wait_ge(self.xn_ready, g + 1)
        wait(pe, self.copied, g - 1)
        for t in range(TILES):
            mm = self.nc.tensor.transpose(self.turn_ps[q][:, t * P:(t + 1) * P], self.xn[:, q, t], self.ident)
        mm.then_inc(self.turned, 1)

    def copy(self, act, g, q):
        act.wait_ge(self.turned, g + 1)
        self.nc.scalar.copy(self.xT_v[:, g], self.turn_ps[q][:]).then_inc(self.copied, 1)


def output_projection_stage(nc, keep, w, io):
    with ExitStack() as stack:
        m = Memory(nc, stack, "out_")
        norm = Norm(nc, keep, m, "n0", w["ident"][:])
        a_in = m.sb("a_in", [P, 2, BATCH, P])
        aT = m.sb("aT", [P, 2, GROUP])
        x_in = m.sb("x_in2", [P, 2, TILES, P])
        a_ps = [m.ps(f"a_ps{n}", [P, GROUP]) for n in range(2)]
        y_ps = [m.ps(f"y_ps{n}", [P, GROUP]) for n in range(2)]
        x_loaded = [m.sem("x2_loaded0"), m.sem("x2_loaded1")]
        a_ready, biased, a_turned, aT_ready = m.sem("a_ready"), m.sem("biased"), m.sem("a_turned"), m.sem("aT_ready")
        y_done, x_ready, stats_done = m.sem("y_done"), m.sem("x_ready"), m.sem("stats_done")
        x_v = io["x"].rearrange("b (c s) e -> c b s e", s=CHUNK_LEN)
        block = stack.enter_context(nc.Block())

        @block.sync
        def _(sp):
            def body(g2):
                for q in range(2):
                    g = 2 * g2 + q
                    wait(sp, x_ready, g - 1)
                    for t in range(TILES):
                        for half in range(2):
                            sp.dma_start(x_in[64 * half:64 * half + 64, q, t],
                                         x_v[2 * g + t // 2, 2 * (t % 2) + half]).then_inc(x_loaded[q], 16)

            pairs(sp, body)

        @block.gpsimd
        def _(pool):
            def body(g2):
                for q in range(2):
                    g = 2 * g2 + q
                    wait(pool, a_turned, g - 1)
                    nc.gpsimd.tensor_copy(a_in[:, q], keep.attn[:, :, g]).then_inc(a_ready, 1)
                    pool.wait_ge(x_loaded[q], 128 * (g2 + 1))
                    nc.gpsimd.tensor_tensor(x_in[:, q], x_in[:, q], w["bo"][:].unsqueeze(1).to_broadcast([P, TILES, P]),
                                            ALU.add).then_inc(biased, 1)

            pairs(pool, body)
            norm.root(pool)

        @block.tensor
        def _(pe):
            def body(g2):
                for q in range(2):
                    g = 2 * g2 + q
                    pe.wait_ge(a_ready, g + 1)
                    wait(pe, aT_ready, g - 1)
                    for b in range(BATCH):
                        mm = nc.tensor.transpose(a_ps[q][:, b * P:(b + 1) * P], a_in[:, q, b], w["ident"][:])
                    mm.then_inc(a_turned, 1)
                    pe.wait_ge(aT_ready, g + 1)
                    wait(pe, x_ready, g - 1)
                    for t in range(TILES):
                        mm = nc.tensor.matmul(y_ps[q][:, t * P:(t + 1) * P], aT[:, q, t * P:(t + 1) * P], w["wo"][:],
                                              start=True, stop=True)
                    mm.then_inc(y_done, 1)

            pairs(pe, body)

            def turns(g2):
                for q in range(2):
                    norm.turn(pe, 2 * g2 + q, q)

            pairs(pe, turns)

        @block.scalar
        def _(act):
            def body(g2):
                for q in range(2):
                    g = 2 * g2 + q
                    act.wait_ge(a_turned, g + 1)
                    wait(act, y_done, g - 1)
                    nc.scalar.copy(aT[:, q].rearrange("p (c b s) -> p c b s", c=2, b=BATCH),
                                   a_ps[q][:].rearrange("p (b c s) -> p c b s", b=BATCH, c=2)).then_inc(aT_ready, 1)

            pairs(act, body)

            def copies(g2):
                for q in range(2):
                    norm.copy(act, 2 * g2 + q, q)

            pairs(act, copies)

        @block.vector
        def _(dve):
            def body(g2):
                for q in range(2):
                    g = 2 * g2 + q
                    dve.wait_ge(y_done, g + 1)
                    dve.wait_ge(biased, g + 1)
                    nc.vector.tensor_tensor(norm.x_v[:, g], y_ps[q][:].rearrange("p (t e) -> p t e", t=TILES), x_in[:, q],
                                            ALU.add).then_inc(x_ready, 1)
                    dve.wait_ge(x_ready, g + 1)
                    norm.take_stats(g).then_inc(stats_done, 1)

            pairs(dve, body)
            dve.wait_ge(stats_done, GROUPS)
            norm.finish(dve)
            dve.wait_ge(norm.rstd_ready, 1)

            def scales(g2):
                for q in range(2):
                    norm.scale(dve, 2 * g2 + q, q)

            pairs(dve, scales)


def route_stage(nc, keep, w, router, top_k, sigmoid_bias=None, route_scale=None):
    with ExitStack() as stack:
        m = Memory(nc, stack, "rt%d_" % top_k)
        scores = m.sb("scores", [P, ALL_TILES, EXPERTS])
        ranked = m.sb("ranked", [P, ALL_TILES, 8])
        ranks = m.sb("ranks", [P, ALL_TILES, 8], mybir.dt.uint32)
        best = m.sb("best", [P, ALL_TILES, top_k])
        raised = m.sb("raised", [P, ALL_TILES, EXPERTS])
        chosen = m.sb("chosen", [P, ALL_TILES, EXPERTS])
        hit = m.sb("hit", [P, ALL_TILES, EXPERTS])
        gates = m.sb("gates", [P, ALL_TILES, EXPERTS])
        comb = m.sb("comb", [P, ALL_TILES, EXPERTS])
        sums = m.sb("sums", [P, 3, ALL_TILES])
        rest = m.sb("comb_rest", [EXPERTS, 2, GROUP])
        mid = m.sb("comb_mid", [EXPERTS, 2, GROUP], BF16)
        high = m.sb("comb_high", [EXPERTS, 2, GROUP])
        logit_ps = m.ps("logit_ps", [P, ALL_TILES * EXPERTS])
        comb_ps = [m.ps(f"combT_ps{n}", [P, GROUP]) for n in range(2)]
        clear, logits_done, raised_ready = m.sem("comb_clear"), m.sem("logits_done"), m.sem("raised_ready")
        gates_ready, comb_ready, turned = m.sem("gates_ready"), m.sem("comb_ready"), m.sem("comb_turned")
        hi_done, rest_done, mid_done, parts_done = m.sem("chi"), m.sem("crest"), m.sem("cmid"), m.sem("cparts")
        own_sem, mid_kept = m.sem("route_own"), m.sem("cmid_kept")
        comb3_v = keep.comb3[:].rearrange("p (g n) -> p g n", n=GROUP)
        wide = [P, ALL_TILES, EXPERTS]
        block = stack.enter_context(nc.Block())

        @block.tensor
        def _(pe):
            for t in range(ALL_TILES):
                mm = nc.tensor.matmul(logit_ps[:, t * EXPERTS:(t + 1) * EXPERTS], keep.xT[:, t * P:(t + 1) * P], router[:],
                                      start=True, stop=True)
            mm.then_inc(logits_done, 1)
            pe.wait_ge(comb_ready, 1)
            for g in range(GROUPS):
                wait(pe, rest_done, g - 1)
                for t in range(TILES):
                    mm = nc.tensor.matmul(comb_ps[g % 2][0:EXPERTS, t * P:(t + 1) * P], comb[:, TILES * g + t], w["ident"][:],
                                          start=True, stop=True)
                mm.then_inc(turned, 1)

        @block.scalar
        def _(act):
            act.wait_ge(raised_ready, 1)
            nc.scalar.activation(gates[:], raised[:], ACT.Sigmoid if sigmoid_bias is not None else ACT.Exp).then_inc(gates_ready, 1)
            act.wait_ge(clear, 1)
            for g in range(GROUPS):
                q = g % 2
                act.wait_ge(turned, g + 1)
                nc.scalar.copy(comb3_v[0:EXPERTS, g], comb_ps[q][0:EXPERTS, :]).then_inc(hi_done, 1)
                act.wait_ge(rest_done, g + 1)
                wait(act, parts_done, g - 1)
                nc.scalar.copy(mid[:, q], rest[:, q]).then_inc(mid_done, 1)
                nc.scalar.copy(comb3_v[32:32 + EXPERTS, g], rest[:, q]).then_inc(mid_kept, 1)

        @block.gpsimd
        def _(pool):
            nc.gpsimd.memset(keep.comb3[:], 0.0).then_inc(clear, 1)
            pool.wait_ge(clear, 1)
            for g in range(GROUPS):
                q = g % 2
                pool.wait_ge(mid_done, g + 1)
                nc.gpsimd.tensor_tensor(comb3_v[64:64 + EXPERTS, g], rest[:, q], mid[:, q],
                                        ALU.subtract).then_inc(parts_done, 1)

        @block.vector
        def _(dve):
            own = Chain(dve, own_sem)
            flat = logit_ps[:].rearrange("p (t e) -> p t e", t=ALL_TILES)
            dve.wait_ge(logits_done, 1)
            if sigmoid_bias is not None:
                own.add(nc.vector.tensor_copy(raised[:], flat))
                own.wait()
                dve.sem_inc(raised_ready, 1)
                dve.wait_ge(gates_ready, 1)
                own.add(nc.vector.tensor_tensor(scores[:], gates[:], sigmoid_bias[:].unsqueeze(1).to_broadcast(wide), ALU.add))
            else:
                own.add(nc.vector.tensor_copy(scores[:], flat))
            own.wait()
            for t in range(ALL_TILES):
                last = nc.vector.max(ranked[:, t], scores[:, t])
            own.add(last)
            own.wait()
            if sigmoid_bias is None:
                nc.vector.tensor_tensor(raised[:], scores[:], ranked[:, :, 0:1].to_broadcast(wide),
                                        ALU.subtract).then_inc(raised_ready, 1)
            for t in range(ALL_TILES):
                last = nc.vector.max_index(ranks[:, t], ranked[:, t], scores[:, t])
            own.add(last)
            own.wait()
            own.add(nc.vector.tensor_copy(best[:], ranks[:, :, 0:top_k]))
            own.wait()
            for k in range(top_k):
                dst = chosen if k == 0 else hit
                own.add(nc.vector.tensor_tensor(dst[:], w["indices"][:].unsqueeze(1).to_broadcast(wide),
                                                best[:, :, k:k + 1].to_broadcast(wide), ALU.is_equal))
                own.wait()
                if k:
                    own.add(nc.vector.tensor_tensor(chosen[:], chosen[:], hit[:], ALU.add))
                    own.wait()
            dve.wait_ge(gates_ready, 1)
            nc.vector.reduce_sum(sums[:, 0], gates[:], mybir.AxisListType.X)
            own.add(nc.vector.tensor_tensor(chosen[:], chosen[:], gates[:], ALU.mult))
            own.wait()
            own.add(nc.vector.reduce_sum(sums[:, 1], chosen[:], mybir.AxisListType.X))
            own.wait()
            if sigmoid_bias is None:
                own.add(nc.vector.scalar_tensor_tensor(sums[:, 2], sums[:, 0], 1e-9, sums[:, 1], ALU.mult, ALU.add))
            else:
                own.add(nc.vector.tensor_scalar_mul(sums[:, 2], sums[:, 1], 1.0 / route_scale))
            own.wait()
            own.add(nc.vector.reciprocal(sums[:, 0], sums[:, 2]))
            own.wait()
            nc.vector.tensor_tensor(comb[:], chosen[:], sums[:, 0].unsqueeze(2).to_broadcast(wide),
                                    ALU.mult).then_inc(comb_ready, 1)
            for g in range(GROUPS):
                q = g % 2
                dve.wait_ge(hi_done, g + 1)
                wait(dve, parts_done, g - 1)
                wait(dve, mid_kept, g - 1)
                nc.vector.tensor_tensor(rest[:, q], comb_ps[q][0:EXPERTS, :], comb3_v[0:EXPERTS, g],
                                        ALU.subtract).then_inc(rest_done, 1)


def expert_stage(nc, keep, w, name, routed, shared_rows, store=None):
    chunks = routed + 1
    rows = lambda c: shared_rows if c == routed else P
    gate_w, up_w, down_w, spread = w[name + "_gate"], w[name + "_up"], w[name + "_down"], w[name + "_spread"]
    with ExitStack() as stack:
        m = Memory(nc, stack, name + "_")
        gated = m.sb("gated", [P, 2, GROUP])
        product = m.sb("product", [P, 2, GROUP])
        hid = m.sb("hid", [P, 2, chunks, GROUP])
        result = m.sb("result", [P, 2, TILES, P]) if store is not None else None
        gate_ps = [m.ps(f"gate_ps{n}", [P, GROUP]) for n in range(2)]
        up_ps = [m.ps(f"up_ps{n}", [P, GROUP]) for n in range(2)]
        comb_ps = m.ps("comb_ps", [P, GROUP])
        y_ps = [m.ps(f"yy_ps{n}", [P, GROUP]) for n in range(2)]
        gate_done, up_done, silu_done = m.sem("gate_done"), m.sem("up_done"), m.sem("silu_done")
        comb_shown, product_done, hid_done = m.sem("comb_shown"), m.sem("product_done"), m.sem("hid_done")
        y_done, x_ready = m.sem("yy_done"), m.sem("xx_ready")
        stored = [m.sem("stored0"), m.sem("stored1")]
        x_v = keep.x[:].rearrange("p (g t) e -> p g t e", t=TILES)
        xT_v = keep.xT[:].rearrange("p (g n) -> p g n", n=GROUP)
        comb3_v = keep.comb3[:].rearrange("p (g n) -> p g n", n=GROUP)
        block = stack.enter_context(nc.Block())

        @block.tensor
        def _(pe):
            def down(g, q):
                pe.wait_ge(hid_done, chunks * (g + 1))
                wait(pe, x_ready, g - 1)
                for t in range(TILES):
                    for c in range(chunks):
                        mm = nc.tensor.matmul(y_ps[q][:, t * P:(t + 1) * P], hid[0:rows(c), q, c, t * P:(t + 1) * P],
                                              down_w[0:rows(c), c], start=(c == 0), stop=(c == chunks - 1))
                mm.then_inc(y_done, 1)

            def body(g2):
                for q in range(2):
                    g = 2 * g2 + q
                    for c in range(chunks):
                        n = chunks * g + c
                        par = (chunks * q + c) % 2
                        wait(pe, silu_done, n - 1)
                        nc.tensor.matmul(gate_ps[par][0:rows(c), :], gate_w[:, c, 0:rows(c)], xT_v[:, g],
                                         start=True, stop=True).then_inc(gate_done, 1)
                        wait(pe, product_done, n - 1)
                        nc.tensor.matmul(up_ps[par][0:rows(c), :], up_w[:, c, 0:rows(c)], xT_v[:, g],
                                         start=True, stop=True).then_inc(up_done, 1)
                        if c < routed:
                            wait(pe, hid_done, n if c else n - 1)
                            nc.tensor.matmul(comb_ps[:], spread[:, c], comb3_v[:, g], start=True,
                                             stop=True).then_inc(comb_shown, 1)
                        if c == 1 and not (isinstance(g, int) and g == 0):
                            down(g - 1, 1 - q)

            pairs(pe, body)
            down(GROUPS - 1, 1)

        @block.scalar
        def _(act):
            def body(g2):
                for q in range(2):
                    g = 2 * g2 + q
                    for c in range(chunks):
                        n, par = chunks * g + c, (chunks * q + c) % 2
                        act.wait_ge(gate_done, n + 1)
                        wait(act, product_done, n - 1)
                        nc.scalar.activation(gated[0:rows(c), par], gate_ps[par][0:rows(c), :],
                                             ACT.Silu).then_inc(silu_done, 1)

            pairs(act, body)

        @block.vector
        def _(dve):
            def residual(g, q, g2):
                dve.wait_ge(y_done, g + 1)
                y = y_ps[q][:].rearrange("p (t e) -> p t e", t=TILES)
                if store is not None:
                    wait(dve, stored[q], 128 * g2)
                    nc.vector.tensor_tensor(result[:, q], y, x_v[:, g], ALU.add).then_inc(x_ready, 1)
                else:
                    nc.vector.tensor_tensor(x_v[:, g], y, x_v[:, g], ALU.add).then_inc(x_ready, 1)

            def body(g2):
                for q in range(2):
                    g = 2 * g2 + q
                    for c in range(chunks):
                        n, par = chunks * g + c, (chunks * q + c) % 2
                        dve.wait_ge(up_done, n + 1)
                        dve.wait_ge(silu_done, n + 1)
                        R = rows(c)
                        if c == 0:
                            wait(dve, y_done, g - 1)
                        if c < routed:
                            wait(dve, hid_done, n - 1)
                            nc.vector.tensor_tensor(product[:, par], up_ps[par][:], gated[:, par],
                                                    ALU.mult).then_inc(product_done, 1)
                            dve.wait_ge(comb_shown, routed * g + c + 1)
                            dve.wait_ge(product_done, n + 1)
                            nc.vector.tensor_tensor(hid[:, q, c], comb_ps[:], product[:, par], ALU.mult).then_inc(hid_done, 1)
                        else:
                            nc.vector.tensor_tensor(hid[0:R, q, c], up_ps[par][0:R, :], gated[0:R, par],
                                                    ALU.mult).then_inc(product_done, 1)
                            dve.wait_ge(product_done, n + 1)
                            dve.sem_inc(hid_done, 1)
                        if c == 2 and not (isinstance(g, int) and g == 0):
                            residual(g - 1, 1 - q, g2 if q else g2 - 1)

            pairs(dve, body)
            residual(GROUPS - 1, 1, GROUPS // 2 - 1)

        if store is not None:
            out_v = store.rearrange("b (c s) e -> c b s e", s=CHUNK_LEN)

            @block.sync
            def _(sp):
                def body(g2):
                    for q in range(2):
                        g = 2 * g2 + q
                        sp.wait_ge(x_ready, g + 1)
                        for t in range(TILES):
                            for half in range(2):
                                sp.dma_start(out_v[2 * g + t // 2, 2 * (t % 2) + half],
                                             result[64 * half:64 * half + 64, q, t]).then_inc(stored[q], 16)

                pairs(sp, body)
                for q in range(2):
                    sp.wait_ge(stored[q], 128 * GROUPS // 2)



INNER = 256
RMS_EPS = 1e-6
STEPS = SEQ // CHUNK_LEN
BASE_RATE = 0.01
CHUNK_TOKENS = BATCH * CHUNK_LEN
FILL_LONG, FILL_SHORT = 8, 5
HALVES_IN = INNER // P


def memory_inputs_stage(nc, keep, w):
    with ExitStack() as stack:
        m = Memory(nc, stack, "mi_")
        norm = Norm(nc, keep, m, "n1", w["ident"][:])
        xT_s = m.sb("xT_s", [P, 2, GROUP])
        dot_terms = m.sb("dot_terms", [P, 3, TILES, P])
        dot_sums = m.sb("dot_sums", [P, 2, 3, TILES])
        raw = m.sb("raw", [P, 2, TILES, P])
        squares = m.sb("squares", [P, 2, TILES, P])
        mean_sq = m.sb("mean_sq", [P, 2, 2, TILES])
        inv = m.sb("inv", [P, 2, TILES])
        scaled_qk = m.sb("scaled_qk", [P, 2, TILES, P])
        normed = m.sb("normed", [P, 2, TILES, P])
        proj_ps = [m.ps(f"proj{n}", [P, GROUP]) for n in range(3)]
        back_ps = [m.ps(f"back{n}", [P, GROUP]) for n in range(2)]
        stats_done, x_read, xT_ready = m.sem("st_done"), m.sem("xread"), m.sem("xT_s_ready")
        dots_ready, dots_taken = m.sem("dots_ready"), m.sem("dots_taken")
        projected, activated, v_active = m.sem("projected3"), m.sem("activated"), m.sem("v_active")
        squared, summed, inv_ready = m.sem("squared"), m.sem("summed_sq"), m.sem("inv_ready")
        normed_ready, kept, back_done, back_kept = m.sem("normed_r"), m.sem("nkept"), m.sem("back_d"), m.sem("back_k")
        scaled, own_sem = m.sem("scaled"), m.sem("mi_own")
        tok_v = [a[:].rearrange("p (g t) e -> p g t e", t=TILES) for a in (keep.q, keep.k, keep.v)]
        T_v = [a[:].rearrange("p (g n) -> p g n", n=GROUP) for a in (keep.qT, keep.kT)]
        dots_v = keep.dots[:].rearrange("p d (g t) -> p g d t", t=TILES)
        block = stack.enter_context(nc.Block())

        @block.vector
        def _(dve):
            own = Chain(dve, own_sem)

            def statistics(g2):
                for q in range(2):
                    norm.take_stats(2 * g2 + q).then_inc(stats_done, 1)

            pairs(dve, statistics)
            dve.wait_ge(stats_done, GROUPS)
            norm.finish(dve)
            dve.wait_ge(norm.rstd_ready, 1)

            norm.scale(dve, 0, 0)

            def body(g2):
                for q in range(2):
                    g = 2 * g2 + q
                    dve.wait_ge(norm.xn_ready, g + 1)
                    wait(dve, dots_taken, g)
                    for d in range(3):
                        for t in range(TILES):
                            last = nc.vector.tensor_tensor_reduce(out=dot_terms[:, d, t], in0=norm.xn[:, q, t], in1=w["gate_rows"][:, d],
                                                                  scale=1.0, scalar=0.0, op0=ALU.mult, op1=ALU.add,
                                                                  accum_out=dot_sums[:, q, d, t:t + 1])
                    last.then_inc(dots_ready, 1)
                    dve.wait_ge(dots_ready, g + 1)
                    nc.vector.tensor_copy(dots_v[:, g], dot_sums[:, q]).then_inc(dots_taken, 1)
                    if not (isinstance(g, int) and g == GROUPS - 1):
                        norm.scale(dve, g + 1, 1 - q)
                    own.at(g)
                    dve.wait_ge(squared, g + 1)
                    wait(dve, inv_ready, g)
                    own.add(nc.vector.reduce_sum(mean_sq[:, 0], squares[:], mybir.AxisListType.X))
                    own.wait()
                    nc.vector.tensor_scalar(mean_sq[:, 1], mean_sq[:, 0], 1.0 / P, RMS_EPS, ALU.mult, ALU.add).then_inc(summed, 1)

            pairs_ahead(dve, body)

        @block.gpsimd
        def _(pool):
            norm.root(pool)

            def body(g2):
                for q in range(2):
                    g = 2 * g2 + q
                    pool.wait_ge(summed, g + 1)
                    nc.gpsimd.tensor_tensor(inv[:], mean_sq[:, 1], keep.minus_half[:, 0:2 * TILES].rearrange("p (n t) -> p n t", n=2),
                                            ALU.pow).then_inc(inv_ready, 1)
                    pool.wait_ge(inv_ready, g + 1)
                    wait(pool, back_done, g)
                    nc.gpsimd.tensor_tensor(scaled_qk[:], raw[:], inv[:].unsqueeze(3).to_broadcast([P, 2, TILES, P]),
                                            ALU.mult).then_inc(scaled, 1)
                    pool.wait_ge(scaled, g + 1)
                    wait(pool, kept, g)
                    nc.gpsimd.tensor_tensor(normed[:], scaled_qk[:], w["qk_norm"][:].unsqueeze(2).to_broadcast([P, 2, TILES, P]),
                                            ALU.mult).then_inc(normed_ready, 1)

            pairs(pool, body)

        @block.scalar
        def _(act):
            def back(g):
                act.wait_ge(normed_ready, g + 1)
                for n in range(2):
                    last = nc.scalar.copy(tok_v[n][:, g], normed[:, n])
                last.then_inc(kept, 1)
                act.wait_ge(back_done, g + 1)
                for n in range(2):
                    last = nc.scalar.copy(T_v[n][:, g], back_ps[n][:])
                last.then_inc(back_kept, 1)

            def keep_xT(g, q):
                act.wait_ge(norm.turned, g + 1)
                wait(act, projected, g - 1)
                nc.scalar.copy(xT_s[:, q], norm.turn_ps[q][:]).then_inc(norm.copied, 1)

            keep_xT(0, 0)

            def body(g2):
                for q in range(2):
                    g = 2 * g2 + q
                    act.wait_ge(projected, g + 1)
                    wait(act, scaled, g)
                    for n in range(2):
                        last = nc.scalar.activation(raw[:, n], proj_ps[n][:].rearrange("p (t e) -> p t e", t=TILES), ACT.Silu)
                    last.then_inc(activated, 1)
                    act.wait_ge(activated, g + 1)
                    wait(act, summed, g)
                    nc.scalar.activation(squares[:], raw[:], ACT.Square).then_inc(squared, 1)
                    nc.scalar.activation(tok_v[2][:, g], proj_ps[2][:].rearrange("p (t e) -> p t e", t=TILES), ACT.Silu).then_inc(v_active, 1)
                    if not (isinstance(g, int) and g == GROUPS - 1):
                        keep_xT(g + 1, 1 - q)
                    if not (isinstance(g, int) and g == 0):
                        back(g - 1)

            pairs_ahead(act, body)
            back(GROUPS - 1)

        @block.tensor
        def _(pe):
            def back(g):
                pe.wait_ge(normed_ready, g + 1)
                wait(pe, back_kept, g)
                for n in range(2):
                    for t in range(TILES):
                        mm = nc.tensor.transpose(back_ps[n][:, t * P:(t + 1) * P], normed[:, n, t], w["ident"][:])
                mm.then_inc(back_done, 1)

            norm.turn(pe, 0, 0)

            def body(g2):
                for q in range(2):
                    g = 2 * g2 + q
                    pe.wait_ge(norm.copied, g + 1)
                    wait(pe, v_active, g)
                    for t in range(TILES):
                        for n in range(3):
                            mm = nc.tensor.matmul(proj_ps[n][:, t * P:(t + 1) * P], xT_s[:, q, t * P:(t + 1) * P], w["qkv1"][:, n],
                                                  start=True, stop=True)
                    mm.then_inc(projected, 1)
                    if not (isinstance(g, int) and g == GROUPS - 1):
                        norm.turn(pe, g + 1, 1 - q)
                    if not (isinstance(g, int) and g == 0):
                        back(g - 1)

            pairs_ahead(pe, body)
            back(GROUPS - 1)


def recurrence_stage(nc, keep, w):
    W0, W1, W1T, GAIN, END = 0, INNER, 2 * INNER, 3 * INNER, 3 * INNER + P
    with ExitStack() as stack:
        m = Memory(nc, stack, "rc_")
        mem, moment = keep.mem, m.sb("moment", [P, END])
        faded, moment_faded = m.sb("faded", [P, END]), m.sb("moment_faded", [P, END])
        k_s = m.sb("k_s", [P, 2, 2, P])
        kT_s = m.sb("kT_s", [P, 2, CHUNK_TOKENS])
        kv = m.sb("kv", [P, 2, 2, P])
        gates = m.sb("gates_s", [P, 3, ALL_TILES])
        term_sums = m.sb("term_sums", [P, 3, ALL_TILES])
        pair_sum = m.sb("pair_sum", [P, 2, STEPS])
        rate_s = m.sb("rate_s", [P, 2, 2])
        fade_s = m.sb("fade_s", [P, 2, 2])
        sigT, sig = m.sb("sigT", [P, 2, CHUNK_TOKENS]), m.sb("sig", [P, 2, INNER])
        hT, h = m.sb("hT", [P, 2, CHUNK_TOKENS]), m.sb("h", [P, 2, INNER])
        slope = m.sb("slope", [P, 2, 2, INNER])
        sq_junk = m.sb("sq_junk", [P, 3, 2 * INNER])
        ss = m.sb("ss", [P, 2, 2])
        r = m.sb("r", [P, 2])
        yr = m.sb("yr", [P, 2, P])
        yg = m.sb("yg", [P, 2, P])
        yg2 = m.sb("yg_second", [P, 2, P])
        gain2 = m.sb("gain_squared", [P, P])
        kvg = m.sb("kv_gain", [P, 2, P])
        G = m.sb("G", [P, 2, P])
        D = m.sb("D", [P, 2, P])
        Gy = m.sb("Gy", [P, 2, P])
        Dy_junk = m.sb("Dy_junk", [P, 2, P])
        Dy = m.sb("Dy", [P, 3, 2])
        inner = m.sb("inner", [P, 2, P])
        dy = m.sb("dy", [P, 2, P])
        dyT = m.sb("dyT", [P, 2 * P])
        da = m.sb("da", [P, 2, INNER])
        norms = m.sb("norms", [P, 3])
        size = m.sb("size", [P, 4])
        aT_ps = m.ps("aT_ps", [P, 2, CHUNK_TOKENS])
        a_ps = m.ps("aa_ps", [P, 2, INNER])
        y_ps = m.ps("y3_ps", [P, 4, P])
        dyT_ps = m.ps("dyT_ps", [P, 4 * P])
        dh_ps = m.ps("dh_ps", [P, 2, INNER])
        g01_ps = m.ps("g01_ps", [P, 2 * INNER])
        g1T_ps = m.ps("g1T_ps", [P, 2 * INNER])
        total_ps = m.ps("total_ps", [P, 2 * INNER])

        names = ("state_set dots_summed gates_ready k_ready kv_ready faded_ready sigT_done sig_done hT_ready h_ready "
                 "slope_ready aT_done a_done y_done y_squared ms_ready r_ready yr_ready yg_ready G_ready D_ready Gy_ready "
                 "Dy_ready dy_ready dyT_done dyT_ready dh_done da_ready g1_done g0_done gain_done w1_squared w0_squared "
                 "gain_squared totalled rooted clip_ready mem_ready moment_ready sums_copied pairs_summed gates_final inner_ready slope_parts c1_ready size_ready size_eps size_inv fed kv_raw fade_scaled kvg_ready yg2_ready").split()
        S = {n: m.sem("rc_" + n) for n in names}
        k_v = keep.k[:].rearrange("p (c t) e -> p c t e", t=2)
        v_v = keep.v[:].rearrange("p (c t) e -> p c t e", t=2)
        kT_v = keep.kT[:].rearrange("p (c n) -> p c n", n=CHUNK_TOKENS)
        gate_v = gates[:].rearrange("p d (c t) -> p d c t", t=2)
        step_v = gates[:]
        clip = m.sb("clip", [P, 1])
        gain_b = lambda: mem[:, GAIN:END].unsqueeze(1).to_broadcast([P, 2, P])
        block = stack.enter_context(nc.Block())

        def steps(engine, body):
            body(0)
            with engine.Fori(1, STEPS // 2 - 1) as c2:
                body(c2)
            body(STEPS // 2 - 1)

        @block.tensor
        def _(pe):
            def keep_clock(q, count):
                for _ in range(count):
                    nc.tensor.matmul(dyT_ps[:, 2 * P:], w["ones"][:], kT_s[:, q], start=True, stop=True)

            nc.tensor.matmul(total_ps[:, 0:ALL_TILES], w["block_ones"][:], keep.dots[:, 0], start=True, stop=True)
            nc.tensor.matmul(total_ps[:, ALL_TILES:3 * ALL_TILES], w["ones"][:], keep.dots[:, 1:3].rearrange("p d t -> p (d t)"),
                             start=True, stop=True).then_inc(S["dots_summed"], 1)

            def body(c2):
                for q in range(2):
                    c = 2 * c2 + q
                    pe.wait_ge(S["k_ready"], c + 1)
                    wait(pe, S["mem_ready"], c)
                    wait(pe, S["hT_ready"], c)
                    for i in range(2):
                        mm = nc.tensor.matmul(aT_ps[:, i], mem[:, W0 + i * P:W0 + (i + 1) * P], kT_s[:, q], start=True, stop=True)
                    mm.then_inc(S["aT_done"], 1)
                    wait(pe, S["h_ready"], c)
                    for t in range(2):
                        mm = nc.tensor.matmul(a_ps[:, t], kT_s[:, q, t * P:(t + 1) * P], mem[:, W0:W0 + INNER], start=True, stop=True)
                    mm.then_inc(S["a_done"], 1)
                    pe.wait_ge(S["hT_ready"], c + 1)
                    wait(pe, S["yr_ready"], c)
                    for t in range(2):
                        for i in range(2):
                            mm = nc.tensor.matmul(y_ps[:, t], hT[:, i, t * P:(t + 1) * P], mem[:, W1T + i * P:W1T + (i + 1) * P],
                                                  start=(i == 0), stop=(i == 1))
                    mm.then_inc(S["y_done"], 1)
                    wait(pe, S["dyT_ready"], c)
                    keep_clock(q, FILL_LONG)
                    pe.wait_ge(S["dy_ready"], c + 1)
                    wait(pe, S["dyT_ready"], c)
                    for t in range(2):
                        mm = nc.tensor.transpose(dyT_ps[:, t * P:(t + 1) * P], dy[:, t], w["ident"][:])
                    mm.then_inc(S["dyT_done"], 1)
                    pe.wait_ge(S["h_ready"], c + 1)
                    wait(pe, S["moment_ready"], c)
                    for t in range(2):
                        mm = nc.tensor.matmul(g01_ps[:, W1:W1 + INNER], dy[:, t], h[:, t], start=(t == 0), stop=(t == 1))
                    mm.then_inc(S["g1_done"], 1)
                    pe.wait_ge(S["dyT_ready"], c + 1)
                    wait(pe, S["da_ready"], c)
                    for t in range(2):
                        mm = nc.tensor.matmul(dh_ps[:, t], dyT[:, t * P:(t + 1) * P], mem[:, W1:W1 + INNER], start=True, stop=True)
                    mm.then_inc(S["dh_done"], 1)
                    for i in range(2):
                        for t in range(2):
                            nc.tensor.matmul(g1T_ps[:, i * P:(i + 1) * P], h[:, t, i * P:(i + 1) * P], dy[:, t],
                                             start=(t == 0), stop=(t == 1))
                    pe.wait_ge(S["Gy_ready"], c + 1)
                    for t in range(2):
                        mm = nc.tensor.matmul(g1T_ps[:, INNER:INNER + P], w["ones"][:], Gy[:, t], start=(t == 0), stop=(t == 1))
                    mm.then_inc(S["gain_done"], 1)
                    pe.wait_ge(S["da_ready"], c + 1)
                    pe.wait_ge(S["w1_squared"], c + 1)
                    for t in range(2):
                        mm = nc.tensor.matmul(g01_ps[:, W0:W0 + INNER], k_s[:, q, t], da[:, t], start=(t == 0), stop=(t == 1))
                    mm.then_inc(S["g0_done"], 1)
                    pe.wait_ge(S["w0_squared"], c + 1)
                    for n in range(3):
                        mm = nc.tensor.matmul(total_ps[:, 0:1], w["ones"][:] if n < 2 else w["mean_ones"][:], norms[:, n:n + 1],
                                              start=(n == 0), stop=(n == 2))
                    mm.then_inc(S["totalled"], 1)
                    keep_clock(q, FILL_SHORT)

            steps(pe, body)

        @block.scalar
        def _(act):
            act.wait_ge(S["pairs_summed"], 1)
            nc.scalar.activation(gates[:, 0], term_sums[:, 0], ACT.Sigmoid)
            nc.scalar.activation(gates[:, 1:3, 0:STEPS], pair_sum[:], ACT.Sigmoid, scale=1.0 / BATCH).then_inc(S["gates_ready"], 1)

            act.wait_ge(S["gates_final"], 1)

            def feed(c, q):
                wait(act, S["g0_done"], c - 1)
                wait(act, S["faded_ready"], c - 1)
                nc.scalar.copy(rate_s[:, q], gate_v[:, 0, c])
                nc.scalar.copy(fade_s[:, q], step_v[:, 1:3, c])
                nc.scalar.copy(k_s[:, q], k_v[:, c]).then_inc(S["fed"], 1)
                nc.scalar.copy(kT_s[:, q], kT_v[:, c]).then_inc(S["k_ready"], 1)

            feed(0, 0)

            def body(c2):
                for q in range(2):
                    c = 2 * c2 + q
                    last_step = isinstance(c, int) and c == STEPS - 1
                    act.wait_ge(S["aT_done"], c + 1)
                    nc.scalar.activation(sigT[:], aT_ps[:], ACT.Sigmoid).then_inc(S["sigT_done"], 1)
                    act.wait_ge(S["a_done"], c + 1)
                    wait(act, S["slope_ready"], c)
                    nc.scalar.activation(sig[:], a_ps[:], ACT.Sigmoid).then_inc(S["sig_done"], 1)
                    act.wait_ge(S["y_done"], c + 1)
                    wait(act, S["ms_ready"], c)
                    for t in range(2):
                        last = nc.scalar.activation(sq_junk[:, 0, t * P:(t + 1) * P], y_ps[:, t], ACT.Square, accum_out=ss[:, 0, t:t + 1])
                    last.then_inc(S["y_squared"], 1)
                    act.wait_ge(S["dyT_done"], c + 1)
                    wait(act, S["dh_done"], c)
                    nc.scalar.copy(dyT[:], dyT_ps[:, 0:2 * P]).then_inc(S["dyT_ready"], 1)
                    if not last_step:
                        feed(c + 1, 1 - q)
                    act.wait_ge(S["g1_done"], c + 1)
                    wait(act, S["totalled"], c)
                    nc.scalar.activation(sq_junk[:, 1, 0:INNER], g01_ps[:, W1:W1 + INNER], ACT.Square,
                                         accum_out=norms[:, 0:1]).then_inc(S["w1_squared"], 1)
                    act.wait_ge(S["gain_done"], c + 1)
                    nc.scalar.activation(sq_junk[:, 1, INNER:INNER + P], g1T_ps[:, INNER:INNER + P], ACT.Square,
                                         accum_out=norms[:, 2:3])
                    act.wait_ge(S["g0_done"], c + 1)
                    nc.scalar.activation(sq_junk[:, 2, 0:INNER], g01_ps[:, W0:W0 + INNER], ACT.Square,
                                         accum_out=norms[:, 1:2]).then_inc(S["w0_squared"], 1)
                    act.wait_ge(S["w0_squared"], c + 1)

            steps(act, body)

        @block.gpsimd
        def _(pool):
            nc.gpsimd.memset(moment[:], 0.0).then_inc(S["state_set"], 1)

            def body(c2):
                for q in range(2):
                    c = 2 * c2 + q
                    pool.wait_ge(S["ms_ready"], c + 1)
                    wait(pool, S["dy_ready"], c)
                    nc.gpsimd.tensor_tensor(r[:], ss[:, 1], keep.minus_half[:, 0:2], ALU.pow).then_inc(S["r_ready"], 1)
                    pool.wait_ge(S["h_ready"], c + 1)
                    wait(pool, S["da_ready"], c)
                    nc.gpsimd.tensor_tensor(slope[:, 1], h[:], sig[:], ALU.mult)
                    nc.gpsimd.tensor_tensor(slope[:, 0], h[:], sig[:], ALU.add).then_inc(S["slope_parts"], 1)
                    pool.wait_ge(S["slope_parts"], c + 1)
                    nc.gpsimd.tensor_tensor(slope[:, 0], slope[:, 0], slope[:, 1], ALU.subtract).then_inc(S["slope_ready"], 1)
                    pool.wait_ge(S["size_ready"], c + 1)
                    nc.gpsimd.tensor_tensor(size[:, 1:2], size[:, 0:1], w["half"][:, 0:1], ALU.pow).then_inc(S["rooted"], 1)

            steps(pool, body)

        @block.vector
        def _(dve):
            dve.wait_ge(S["dots_summed"], 1)
            nc.vector.tensor_copy(term_sums[:], total_ps[:, 0:3 * ALL_TILES].rearrange("p (d t) -> p d t", d=3)).then_inc(S["sums_copied"], 1)
            dve.wait_ge(S["sums_copied"], 1)
            both = term_sums[:, 1:3].rearrange("p d (c t) -> p d c t", t=2)
            nc.vector.tensor_tensor(pair_sum[:], both[:, :, :, 0], both[:, :, :, 1], ALU.add).then_inc(S["pairs_summed"], 1)
            dve.wait_ge(S["gates_ready"], 1)
            nc.vector.tensor_scalar_mul(gates[:, 0], gates[:, 0], 2.0 * BASE_RATE / (CHUNK_TOKENS * P))
            nc.vector.tensor_scalar(gates[:, 1, 0:STEPS], gates[:, 1, 0:STEPS], -1.0, 1.0, ALU.mult,
                                    ALU.add).then_inc(S["gates_final"], 1)

            def errors(c, q):
                nc.vector.tensor_tensor(kv[:, q], k_v[:, c], v_v[:, c], ALU.subtract).then_inc(S["kv_raw"], 1)
                dve.wait_ge(S["kv_raw"], c + 1)
                dve.wait_ge(S["fed"], c + 1)
                nc.vector.tensor_tensor(kv[:, q], kv[:, q], rate_s[:, q].unsqueeze(2).to_broadcast([P, 2, P]),
                                        ALU.mult).then_inc(S["kv_ready"], 1)

            dve.wait_ge(S["state_set"], 1)
            errors(0, 0)

            def body(c2):
                for q in range(2):
                    c = 2 * c2 + q
                    last_step = isinstance(c, int) and c == STEPS - 1
                    dve.wait_ge(S["kv_ready"], c + 1)
                    dve.wait_ge(S["sigT_done"], c + 1)
                    nc.vector.tensor_tensor(hT[:], aT_ps[:], sigT[:], ALU.mult).then_inc(S["hT_ready"], 1)
                    dve.wait_ge(S["sig_done"], c + 1)
                    nc.vector.tensor_tensor(h[:], a_ps[:], sig[:], ALU.mult).then_inc(S["h_ready"], 1)
                    nc.vector.tensor_tensor(gain2[:], mem[:, GAIN:END], mem[:, GAIN:END], ALU.mult)
                    nc.vector.tensor_tensor(kvg[:], kv[:, q], gain_b(), ALU.mult).then_inc(S["kvg_ready"], 1)
                    dve.wait_ge(S["kvg_ready"], c + 1)
                    dve.wait_ge(S["y_squared"], c + 1)
                    nc.vector.tensor_scalar(ss[:, 1], ss[:, 0], 1.0 / P, RMS_EPS, ALU.mult, ALU.add).then_inc(S["ms_ready"], 1)
                    dve.wait_ge(S["r_ready"], c + 1)
                    nc.vector.tensor_tensor(yr[:], y_ps[:, 0:2], r[:].unsqueeze(2).to_broadcast([P, 2, P]), ALU.mult).then_inc(S["yr_ready"], 1)
                    dve.wait_ge(S["yr_ready"], c + 1)
                    nc.vector.tensor_tensor(yg[:], yr[:], gain2[:].unsqueeze(1).to_broadcast([P, 2, P]), ALU.mult).then_inc(S["yg_ready"], 1)
                    dve.wait_ge(S["yg_ready"], c + 1)
                    for t in range(2):
                        last = nc.vector.scalar_tensor_tensor(D[:, t], yg[:, t], rate_s[:, q, t:t + 1], kvg[:, t], ALU.mult, ALU.add)
                    last.then_inc(S["D_ready"], 1)
                    dve.wait_ge(S["D_ready"], c + 1)
                    for t in range(2):
                        last = nc.vector.tensor_tensor_reduce(out=Dy_junk[:, t], in0=D[:, t], in1=yr[:, t], scale=1.0, scalar=0.0,
                                                              op0=ALU.mult, op1=ALU.add, accum_out=Dy[:, 0, t:t + 1])
                    last.then_inc(S["Dy_ready"], 1)
                    dve.wait_ge(S["Dy_ready"], c + 1)
                    nc.vector.tensor_scalar_mul(Dy[:, 1], Dy[:, 0], -1.0 / P).then_inc(S["c1_ready"], 1)
                    dve.wait_ge(S["c1_ready"], c + 1)
                    for t in range(2):
                        last = nc.vector.scalar_tensor_tensor(inner[:, t], yr[:, t], Dy[:, 1, t:t + 1], D[:, t], ALU.mult, ALU.add)
                    last.then_inc(S["inner_ready"], 1)
                    dve.wait_ge(S["inner_ready"], c + 1)
                    nc.vector.tensor_tensor(dy[:], inner[:], r[:].unsqueeze(2).to_broadcast([P, 2, P]), ALU.mult).then_inc(S["dy_ready"], 1)
                    nc.vector.tensor_tensor(yg2[:], yr[:], gain_b(), ALU.mult).then_inc(S["yg2_ready"], 1)
                    dve.wait_ge(S["yg2_ready"], c + 1)
                    for t in range(2):
                        last = nc.vector.scalar_tensor_tensor(G[:, t], yg2[:, t], rate_s[:, q, t:t + 1], kv[:, q, t], ALU.mult, ALU.add)
                    last.then_inc(S["G_ready"], 1)
                    dve.wait_ge(S["G_ready"], c + 1)
                    nc.vector.tensor_tensor(Gy[:], G[:], yr[:], ALU.mult).then_inc(S["Gy_ready"], 1)
                    dve.wait_ge(S["dh_done"], c + 1)
                    dve.wait_ge(S["slope_ready"], c + 1)
                    nc.vector.tensor_tensor(da[:], dh_ps[:], slope[:, 0], ALU.mult).then_inc(S["da_ready"], 1)
                    wait(dve, S["mem_ready"], c)
                    wait(dve, S["moment_ready"], c)
                    nc.vector.tensor_scalar_mul(moment_faded[:], moment[:], fade_s[:, q, 1:2]).then_inc(S["fade_scaled"], 1)
                    dve.wait_ge(S["fade_scaled"], c + 1)
                    nc.vector.scalar_tensor_tensor(faded[:], mem[:], fade_s[:, q, 0:1], moment_faded[:],
                                                   ALU.mult, ALU.add).then_inc(S["faded_ready"], 1)
                    if not last_step:
                        errors(c + 1, 1 - q)
                    dve.wait_ge(S["totalled"], c + 1)
                    nc.vector.tensor_copy(size[:, 0:1], total_ps[:, 0:1]).then_inc(S["size_ready"], 1)
                    dve.wait_ge(S["rooted"], c + 1)
                    nc.vector.tensor_scalar_add(size[:, 2:3], size[:, 1:2], 1e-6).then_inc(S["size_eps"], 1)
                    dve.wait_ge(S["size_eps"], c + 1)
                    nc.vector.reciprocal(size[:, 3:4], size[:, 2:3]).then_inc(S["size_inv"], 1)
                    dve.wait_ge(S["size_inv"], c + 1)
                    nc.vector.tensor_scalar(clip[:], size[:, 3:4], 1.0, -1.0, ALU.min, ALU.mult).then_inc(S["clip_ready"], 1)
                    dve.wait_ge(S["clip_ready"], c + 1)
                    dve.wait_ge(S["faded_ready"], c + 1)
                    for dst, base, sig_ in ((mem, faded, "mem_ready"), (moment, moment_faded, "moment_ready")):
                        nc.vector.scalar_tensor_tensor(dst[:, 0:W1T], g01_ps[:], clip[:], base[:, 0:W1T], ALU.mult, ALU.add)
                        nc.vector.scalar_tensor_tensor(dst[:, W1T:END], g1T_ps[:, 0:INNER + P], clip[:], base[:, W1T:END],
                                                       ALU.mult, ALU.add).then_inc(S[sig_], 1)

            steps(dve, body)


def memory_read_stage(nc, keep, w):
    W0, W1T, GAIN, END = 0, 2 * INNER, 3 * INNER, 3 * INNER + P
    mem = keep.mem
    with ExitStack() as stack:
        m = Memory(nc, stack, "mr_")
        norm = Norm(nc, keep, m, "n2", w["ident"][:])
        hT = m.sb("hT2", [P, 2, HALVES_IN, GROUP])
        xq = m.sb("xq", [P, 2, TILES, P])
        yr = m.sb("yr2", [P, 2, TILES, P])
        yg = m.sb("yg2", [P, TILES, P])
        junk = m.sb("sq_junk2", [P, GROUP])
        ss = m.sb("ss2", [P, 2, TILES])
        r = m.sb("r2", [P, TILES])
        a_ps = [m.ps(f"a2_ps{n}", [P, GROUP]) for n in range(4)]
        y_ps = [m.ps(f"y2_ps{n}", [P, GROUP]) for n in range(2)]
        a_done, h_ready, y_done, squared = m.sem("a2_done"), m.sem("h2_ready"), m.sem("y2_done"), m.sem("y2_sq")
        ms_ready, r_ready, yr_ready, xq_ready = m.sem("ms2"), m.sem("r2_ready"), m.sem("yr2_ready"), m.sem("xq_ready")
        yg_ready, x_ready, stats_done = m.sem("yg2_ready"), m.sem("x3_ready"), m.sem("st3_done")
        idle = m.sem("idle_read")
        qT_v = keep.qT[:].rearrange("p (g n) -> p g n", n=GROUP)
        q_v = keep.q[:].rearrange("p (g t) e -> p g t e", t=TILES)
        block = stack.enter_context(nc.Block())

        @block.tensor
        def _(pe):
            def read_out(g, q):
                pe.wait_ge(h_ready, g + 1)
                wait(pe, yr_ready, g - 1)
                for t in range(TILES):
                    for i in range(2):
                        mm = nc.tensor.matmul(y_ps[q][:, t * P:(t + 1) * P], hT[:, q, i, t * P:(t + 1) * P],
                                              mem[:, W1T + i * P:W1T + (i + 1) * P], start=(i == 0), stop=(i == 1))
                mm.then_inc(y_done, 1)

            def body(g2):
                for q in range(2):
                    g = 2 * g2 + q
                    wait(pe, h_ready, g - 1)
                    for i in range(2):
                        mm = nc.tensor.matmul(a_ps[2 * q + i][:], mem[:, W0 + i * P:W0 + (i + 1) * P], qT_v[:, g], start=True, stop=True)
                    mm.then_inc(a_done, 1)
                    if not (isinstance(g, int) and g == 0):
                        read_out(g - 1, 1 - q)

            pairs(pe, body)
            read_out(GROUPS - 1, 1)

            def turns(g2):
                for q in range(2):
                    norm.turn(pe, 2 * g2 + q, q)

            pairs(pe, turns)

        @block.scalar
        def _(act):
            def square(g, q):
                act.wait_ge(y_done, g + 1)
                wait(act, ms_ready, g)
                for t in range(TILES):
                    last = nc.scalar.activation(junk[:, t * P:(t + 1) * P], y_ps[q][:, t * P:(t + 1) * P], ACT.Square,
                                                accum_out=ss[:, 0, t:t + 1])
                last.then_inc(squared, 1)

            def body(g2):
                for q in range(2):
                    g = 2 * g2 + q
                    act.wait_ge(a_done, g + 1)
                    wait(act, y_done, g - 1)
                    for i in range(2):
                        last = nc.scalar.activation(hT[:, q, i], a_ps[2 * q + i][:], ACT.Silu)
                    last.then_inc(h_ready, 1)
                    if not (isinstance(g, int) and g == 0):
                        square(g - 1, 1 - q)

            pairs(act, body)
            square(GROUPS - 1, 1)

            def copies(g2):
                for q in range(2):
                    norm.copy(act, 2 * g2 + q, q)

            pairs(act, copies)

        @block.gpsimd
        def _(pool):
            def body(g2):
                for q in range(2):
                    g = 2 * g2 + q
                    nc.gpsimd.tensor_tensor(xq[:, q], norm.x_v[:, g], q_v[:, g], ALU.add).then_inc(xq_ready, 1)
                    pool.wait_ge(ms_ready, g + 1)
                    nc.gpsimd.tensor_tensor(r[:], ss[:, 1], keep.minus_half[:, 0:TILES], ALU.pow).then_inc(r_ready, 1)
                    pool.wait_ge(yr_ready, g + 1)
                    nc.gpsimd.tensor_tensor(yg[:], yr[:, q], mem[:, GAIN:END].unsqueeze(1).to_broadcast([P, TILES, P]),
                                            ALU.mult).then_inc(yg_ready, 1)
                    pool.wait_ge(yg_ready, g + 1)
                    settle(pool, idle)
                    nc.gpsimd.tensor_tensor(norm.x_v[:, g], yg[:], xq[:, q], ALU.add).then_inc(x_ready, 1)
                    pool.wait_ge(x_ready, g + 1)
                    settle(pool, idle)

            pairs(pool, body)
            norm.root(pool)

        @block.vector
        def _(dve):
            def statistics(g):
                dve.wait_ge(x_ready, g + 1)
                norm.take_stats(g).then_inc(stats_done, 1)

            def body(g2):
                for q in range(2):
                    g = 2 * g2 + q
                    dve.wait_ge(squared, g + 1)
                    nc.vector.tensor_scalar(ss[:, 1], ss[:, 0], 1.0 / P, RMS_EPS, ALU.mult, ALU.add).then_inc(ms_ready, 1)
                    dve.wait_ge(r_ready, g + 1)
                    nc.vector.tensor_tensor(yr[:, q], y_ps[q][:].rearrange("p (t e) -> p t e", t=TILES),
                                            r[:].unsqueeze(2).to_broadcast([P, TILES, P]), ALU.mult).then_inc(yr_ready, 1)
                    if not (isinstance(g, int) and g == 0):
                        statistics(g - 1)

            pairs(dve, body)
            statistics(GROUPS - 1)
            dve.wait_ge(stats_done, GROUPS)
            norm.finish(dve)
            dve.wait_ge(norm.rstd_ready, 1)

            def scales(g2):
                for q in range(2):
                    norm.scale(dve, 2 * g2 + q, q)

            pairs(dve, scales)


class Keep:
    pass


def build(nc, io, out, debug=None):
    with ExitStack() as stack:
        m = Memory(nc, stack)
        keep = Keep()
        keep.started, keep.weights, keep.first_weights = m.sem("started"), m.sem("weights"), m.sem("first_weights")
        keep.parts_stored = [m.sem("parts_stored0"), m.sem("parts_stored1")]
        keep.minus_half = m.sb("minus_half", [P, ALL_TILES])
        io["parts"] = nc.dram_tensor("qk_parts", [2, BATCH, 3, P, SEQ], BF16, kind="Internal").ap()
        w = {"loads": [], "first_loads": []}

        def load(memory, *names, when="loads"):
            for name in names:
                src = io[name]
                tile = memory.sb("w_" + name, list(src.shape), src.dtype)
                w[when].append((tile[:], src))
                w[name] = tile

        load(m, "ident", when="first_loads")
        load(m, "wo", "bo", "router0", "indices", "ffn0_gate", "ffn0_up", "ffn0_down", "ffn0_spread",
             "gate_rows", "qk_norm", "qkv1", "ones", "block_ones", "mean_ones", "half", "memory",
             "router1", "router1_bias", "ffn1_gate", "ffn1_up", "ffn1_down", "ffn1_spread")
        keep.mem = w["memory"]

        keep.x = m.sb("x", [P, ALL_TILES, P])
        keep.xT = keep.comb3 = None

        def routed_input(memory, n):
            keep.xT = memory.sb(f"xT_{n}", [P, ALL_TILES * P])
            keep.comb3 = memory.sb(f"comb3_{n}", [COMB_ROWS, ALL_TILES * P], BF16)

        with ExitStack() as attention:
            keep.attn = Memory(nc, attention).sb("attn", [P, BATCH, KEY_TILES, P])
            with ExitStack() as first:
                f = Memory(nc, first)
                load(f, "wkv", "bkv", "wqk", "qk_bias", "wv", "cos", "sin", "ident_bf", "future_bf", "causal", when="first_loads")
                keep.V = f.sb("V", [P, BATCH, HEAD_GROUPS, KEY_TILES, V_COLS])
                project_stage(nc, keep, w, io)
                attention_stage(nc, keep, w, io)
            routed_input(Memory(nc, attention), 0)
            output_projection_stage(nc, keep, w, io)
            route_stage(nc, keep, w, w["router0"], 2)
            expert_stage(nc, keep, w, "ffn0", 4, P)
        keep.xT = None
        with ExitStack() as memory:
            f = Memory(nc, memory)
            keep.q = f.sb("q1", [P, ALL_TILES, P])
            keep.qT = f.sb("qT1", [P, ALL_TILES * P])
            with ExitStack() as scan:
                f = Memory(nc, scan)
                keep.k = f.sb("k1", [P, ALL_TILES, P])
                keep.kT = f.sb("kT1", [P, ALL_TILES * P])
                keep.v = f.sb("v1", [P, ALL_TILES, P])
                keep.dots = f.sb("dots", [P, 3, ALL_TILES])
                memory_inputs_stage(nc, keep, w)
                recurrence_stage(nc, keep, w)
            routed_input(Memory(nc, memory), 1)
            memory_read_stage(nc, keep, w)
            route_stage(nc, keep, w, w["router1"], 4, w["router1_bias"], 2.5)
            expert_stage(nc, keep, w, "ffn1", 8, P, store=out)



_L0 = "L0_attn_"
_L1 = "L1_attn_"


def laid_out(inputs):
    import numpy as np

    a = {n: np.asarray(v) for n, v in inputs.items()}
    f32, bf = np.float32, mybir.dt.np(BF16)
    half = P // 2
    by_element = np.arange(P).reshape(HEADS, HEAD_DIM).T.ravel()
    swapped = np.roll(np.arange(P), -half)[by_element]
    inverse = 1.0 / 10000.0 ** (np.arange(0, P, 2, dtype=f32) / P)
    angle = (np.arange(SEQ, dtype=f32)[:, None] * inverse.astype(f32)[None, :]).T
    cos, sin = np.cos(angle).astype(f32), np.sin(angle).astype(f32)
    tile_rows = lambda v, n: np.broadcast_to(v, (n, *v.shape))
    q, k = np.arange(P)[:, None], np.arange(P)[None, :]
    pair = lambda e, rows, cols: e.reshape(-1, rows, *e.shape[1:])

    def spread(chunks, per):
        s = np.zeros((COMB_ROWS, chunks, P), bf)
        for c in range(chunks):
            for row in range(P):
                for part in range(3):
                    s[32 * part + c * per + row // (P // per), c, row] = 1
        return s

    def by_chunk(e, per):
        n, d, mid = e.shape
        return e.reshape(n // per, per, d, mid).transpose(2, 0, 1, 3).reshape(d, n // per, per * mid)

    def down(e, per):
        n, mid, d = e.shape
        return e.reshape(n // per, per * mid, d).transpose(1, 0, 2)

    def with_shared(routed, shared):
        out = np.zeros((P, routed.shape[1] + 1, P), f32)
        out[:, :-1] = routed
        out[:shared.shape[0], -1, :shared.shape[1]] = shared
        return out

    w13, w2 = a["L1_ffn_w13"], a["L1_ffn_w2"]
    mid1 = w13.shape[1] // 2
    gate1, up1 = w13[:, :mid1].transpose(0, 2, 1), w13[:, mid1:].transpose(0, 2, 1)
    gates = np.concatenate([a[_L1 + n + "_w"].reshape(1, CHUNK_LEN, P) for n in ("theta", "alpha", "eta")])
    return {
        "x": a[_L0 + "x"],
        "ident": np.eye(P, dtype=f32), "ident_bf": np.eye(P).astype(bf),
        "future_bf": np.where(k < q, NEG, 0).astype(bf),
        "causal": np.concatenate([np.zeros((P, SEQ - P)), np.where(k > q, NEG, 0)], 1).astype(f32),
        "cos": np.concatenate([cos, cos])[by_element],
        "sin": np.concatenate([-sin, sin])[by_element],
        "wqk": np.stack([a[_L0 + n][:, cols] for n in ("wqr", "wkr") for cols in (by_element, swapped)], 1),
        "qk_bias": np.stack([a[_L0 + n][rows] for n in ("bqr", "bkr") for rows in (by_element, swapped)], 1),
        "wkv": a[_L0 + "wkv"], "bkv": a[_L0 + "bkv"][:, None],
        "wv": np.concatenate([a[_L0 + "wv"], a[_L0 + "bv"][None]]),
        "wo": a[_L0 + "wo"], "bo": tile_rows(a[_L0 + "bo"], P),
        "router0": a["L0_ffn_router_w"],
        "indices": tile_rows(np.arange(EXPERTS, dtype=f32), P),
        "ffn0_gate": with_shared(by_chunk(a["L0_ffn_wg_r"], 4), by_chunk(a["L0_ffn_wg_s"], 2)[:, 0]),
        "ffn0_up": with_shared(by_chunk(a["L0_ffn_wu_r"], 4), by_chunk(a["L0_ffn_wu_s"], 2)[:, 0]),
        "ffn0_down": with_shared(down(a["L0_ffn_wd_r"], 4), down(a["L0_ffn_wd_s"], 2)[:, 0]),
        "ffn0_spread": spread(4, 4),
        "gate_rows": np.concatenate([gates, gates], 1).transpose(1, 0, 2),
        "qk_norm": tile_rows(np.stack([a[_L1 + "q_norm_w"], a[_L1 + "k_norm_w"]]), P),
        "qkv1": np.stack([a[_L1 + n].T for n in ("wq_w", "wk_w", "wv_w")], 1),
        "ones": np.ones((P, P), f32),
        "block_ones": np.kron(np.eye(2), np.ones((half, half))).astype(f32),
        "mean_ones": np.full((P, P), 1.0 / P, f32),
        "half": np.full((P, 1), 0.5, f32),
        "memory": np.concatenate([a[_L1 + "mem_w0"].T, a[_L1 + "mem_w1"],
                                  a[_L1 + "mem_w1"].T.reshape(2, P, P).transpose(1, 0, 2).reshape(P, 2 * P),
                                  tile_rows(a[_L1 + "mem_ln_w"], P)], 1),
        "router1": a["L1_ffn_gate_w"].T,
        "router1_bias": tile_rows(a["L1_ffn_gate_b"], P),
        "ffn1_gate": with_shared(by_chunk(gate1, 2), a["L1_ffn_w13_s"][:mid1].T),
        "ffn1_up": with_shared(by_chunk(up1, 2), a["L1_ffn_w13_s"][mid1:].T),
        "ffn1_down": with_shared(down(w2.transpose(0, 2, 1), 2), a["L1_ffn_w2_s"].T),
        "ffn1_spread": spread(8, 2),
    }


def kernel(**inputs):
    import numpy as np
    from concourse import bacc
    from concourse.bass_utils import run_bass_kernel_spmd

    nc = bacc.Bacc("TRN2", target_bir_lowering=False, num_devices=1)
    arrays, io = {}, {}
    for name, array in laid_out(inputs).items():
        array = np.ascontiguousarray(array)
        arrays["in_" + name] = array
        io[name] = nc.dram_tensor("in_" + name, list(array.shape), mybir.dt.from_np(array.dtype), kind="ExternalInput").ap()
    out = nc.dram_tensor("out", [BATCH, SEQ, P], FP32, kind="ExternalOutput").ap()
    build(nc, io, out)
    result = run_bass_kernel_spmd(nc, [arrays], core_ids=[0])
    return result.results[0]["out"]
```
